# Optimizing a Trainium2 kernel written in Bass

```python
import numpy as np
import jax
import jax.numpy as jnp

def _softmax(x, axis=-1):
    return jax.nn.softmax(x, axis=axis)

def _gelu(x):
    return jax.nn.gelu(x, approximate=True)

def _silu(x):
    return jax.nn.silu(x)

def _sigmoid(x):
    return jax.nn.sigmoid(x)

def _layernorm(x, axis=-1, eps=1e-05):
    m = jnp.mean(x, axis=axis, keepdims=True)
    v = jnp.var(x, axis=axis, keepdims=True)
    return (x - m) / jnp.sqrt(v + eps)

def _scatter_add(tgt, idx, src, axis=0):
    return tgt.at[idx].add(src)

def _segment_sum(src, seg, n):
    return jax.ops.segment_sum(src, seg, n)
kernel_name = 'mk_decoder_postln_d1_seqx_r8_6c7853'

def setup_inputs(seed: int=0):
    np.random.seed(seed)
    _w = jnp.asarray

    def _rec_inputs():
        import jax
        import jax.numpy as jnp
        _rk = jax.random.key(seed)
        x = 7.22e-05 + 1 * jax.random.normal(jax.random.fold_in(_rk, 1), (32, 64, 256), jnp.float32)
        _lenS = 64 - jax.random.randint(jax.random.fold_in(_rk, 7), (32,), 0, max(1, 64 // 4) + 1, jnp.int32)
        _lenS2 = 64 - jax.random.randint(jax.random.fold_in(_rk, 8), (32,), 0, max(1, 64 // 4) + 1, jnp.int32)
        _ctx_512P = jax.random.normal(jax.random.fold_in(_rk, 11), (32, 16, 64), jnp.float32)
        _ctx_512c = jax.random.dirichlet(jax.random.fold_in(_rk, 511), 0.3 * jnp.ones((16,), jnp.float32), (32, 64))
        _ctx_512t = jnp.einsum('bsk,bkd->bsd', _ctx_512c, _ctx_512P)
        _ctx_512t = _ctx_512t * jax.lax.rsqrt(jnp.mean(jnp.square(_ctx_512t)) + 1e-12) * 0.953939
        ctx_512 = -0.000514642 + 1.00011 * (_ctx_512t + 0.3 * jax.random.normal(jax.random.fold_in(_rk, 611), (32, 64, 64), jnp.float32))
        return (x, ctx_512)
    x, ctx_512 = _rec_inputs()

    def _L0_attn_setup():
        import jax, jax.numpy as jnp
        import numpy as np
        import math
        B, S, D, H = (4, 256, 256, 16)
        HD = D // H

        def _alibi_slopes(n_heads):
            return jnp.asarray([2.0 ** (-8.0 / n_heads * (h + 1)) for h in range(n_heads)], dtype=jnp.float32)
        key = jax.random.key(seed)
        ks = jax.random.split(key, 10)
        w = lambda k: jax.random.normal(k, (D, D), dtype=jnp.float32) * 0.02
        b = lambda k: jax.random.normal(k, (D,), dtype=jnp.float32) * 0.01
        return {'hidden_states': jax.random.normal(ks[0], (B, S, D), dtype=jnp.float32), 'Wq': w(ks[1]), 'bq': b(ks[2]), 'Wk': w(ks[3]), 'bk': b(ks[4]), 'Wv': w(ks[5]), 'bv': b(ks[6]), 'Wo': w(ks[7]), 'bo': b(ks[8]), 'alibi_slopes': _alibi_slopes(H)}
    _L0_attn_all = _L0_attn_setup()
    _L0_attn_in = {k: v for k, v in _L0_attn_all.items() if k in ('Wq', 'bq', 'Wk', 'bk', 'Wv', 'bv', 'Wo', 'bo', 'alibi_slopes')}
    del _L0_attn_all

    def _L0_xattn_setup():
        import jax, jax.numpy as jnp
        import numpy as np
        import math
        NUM_Q_HEADS = 32
        NUM_KV_HEADS = 8
        key = jax.random.key(seed)
        k1, k2, k3 = jax.random.split(key, 3)
        B, S, E = (2, 256, 256)
        kv_E = NUM_KV_HEADS * (E // NUM_Q_HEADS)
        q = jax.random.normal(k1, (B, S, E), dtype=jnp.float32)
        k = jax.random.normal(k2, (B, S, kv_E), dtype=jnp.float32)
        v = jax.random.normal(k3, (B, S, kv_E), dtype=jnp.float32)
        return {'q': q, 'k': k, 'v': v}
    _L0_xattn_all = _L0_xattn_setup()
    _L0_xattn_in = {k: v for k, v in _L0_xattn_all.items() if k in ()}
    del _L0_xattn_all

    def _L0_ffn_setup():
        import jax, jax.numpy as jnp
        import numpy as np
        HIDDEN = 256
        FFN = 176
        N_EXPERTS = 64
        TOP_K = 6
        N_SHARED = 2
        SHARED_FFN = FFN * N_SHARED
        ROUTED_SCALING = 1.0
        EPS = 1e-20

        def _moe_forward(x, gate_w, w_gate_up, w_down, ws_gate_up, ws_down):
            T = x.shape[0]
            logits = jnp.einsum('th,eh->te', x.astype(jnp.float32), gate_w.astype(jnp.float32))
            scores = jax.nn.softmax(logits, axis=-1)
            topk_w, topk_ids = jax.lax.top_k(scores, TOP_K)
            topk_w = topk_w / (jnp.sum(topk_w, axis=-1, keepdims=True) + EPS)
            topk_w = topk_w * ROUTED_SCALING
            comb = jnp.zeros((T, N_EXPERTS), dtype=x.dtype)
            comb = comb.at[jnp.arange(T)[:, None], topk_ids].add(topk_w.astype(x.dtype))
            gu = jnp.einsum('th,efh->tef', x, w_gate_up)
            g, u = (gu[..., :FFN], gu[..., FFN:])
            act = jax.nn.silu(g) * u
            act = act * comb[:, :, None]
            routed = jnp.einsum('tef,ehf->th', act, w_down)
            sgu = jnp.einsum('th,fh->tf', x, ws_gate_up)
            sg, su = (sgu[..., :SHARED_FFN], sgu[..., SHARED_FFN:])
            shared = jnp.einsum('tf,hf->th', jax.nn.silu(sg) * su, ws_down)
            return routed + shared
        key = jax.random.key(seed)
        k0, k1, k2, k3, k4, k5 = jax.random.split(key, 6)
        hidden_states = jax.random.normal(k0, (1, 32, HIDDEN), dtype=jnp.float32)
        gate_w = jax.random.normal(k1, (N_EXPERTS, HIDDEN), dtype=jnp.float32) * 0.05
        w_gate_up = jax.random.normal(k2, (N_EXPERTS, 2 * FFN, HIDDEN), dtype=jnp.float32) * 0.02
        w_down = jax.random.normal(k3, (N_EXPERTS, HIDDEN, FFN), dtype=jnp.float32) * 0.02
        ws_gate_up = jax.random.normal(k4, (2 * SHARED_FFN, HIDDEN), dtype=jnp.float32) * 0.02
        ws_down = jax.random.normal(k5, (HIDDEN, SHARED_FFN), dtype=jnp.float32) * 0.02
        return {'hidden_states': hidden_states, 'gate_w': gate_w, 'w_gate_up': w_gate_up, 'w_down': w_down, 'ws_gate_up': ws_gate_up, 'ws_down': ws_down}
    _L0_ffn_all = _L0_ffn_setup()
    _L0_ffn_in = {k: v for k, v in _L0_ffn_all.items() if k in ('gate_w', 'w_gate_up', 'w_down', 'ws_gate_up', 'ws_down')}
    del _L0_ffn_all
    return {'x': x, 'ctx_512': ctx_512, 'L0_attn_Wq': _L0_attn_in['Wq'], 'L0_attn_bq': _L0_attn_in['bq'], 'L0_attn_Wk': _L0_attn_in['Wk'], 'L0_attn_bk': _L0_attn_in['bk'], 'L0_attn_Wv': _L0_attn_in['Wv'], 'L0_attn_bv': _L0_attn_in['bv'], 'L0_attn_Wo': _L0_attn_in['Wo'], 'L0_attn_bo': _L0_attn_in['bo'], 'L0_attn_alibi_slopes': _L0_attn_in['alibi_slopes'], 'L0_ffn_gate_w': _L0_ffn_in['gate_w'], 'L0_ffn_w_gate_up': _L0_ffn_in['w_gate_up'], 'L0_ffn_w_down': _L0_ffn_in['w_down'], 'L0_ffn_ws_gate_up': _L0_ffn_in['ws_gate_up'], 'L0_ffn_ws_down': _L0_ffn_in['ws_down']}

def reference(x, ctx_512, L0_attn_Wq, L0_attn_bq, L0_attn_Wk, L0_attn_bk, L0_attn_Wv, L0_attn_bv, L0_attn_Wo, L0_attn_bo, L0_attn_alibi_slopes, L0_ffn_gate_w, L0_ffn_w_gate_up, L0_ffn_w_down, L0_ffn_ws_gate_up, L0_ffn_ws_down):
    import jax
    import jax.numpy as jnp

    def _L0_attn_ref(hidden_states, Wq, bq, Wk, bk, Wv, bv, Wo, bo, alibi_slopes):
        import jax, jax.numpy as jnp
        import numpy as np
        import math
        B, S, D, H = (4, 256, 256, 16)
        HD = D // H

        def _alibi_slopes(n_heads):
            return jnp.asarray([2.0 ** (-8.0 / n_heads * (h + 1)) for h in range(n_heads)], dtype=jnp.float32)
        Bn, t, _ = hidden_states.shape
        split = lambda x: x.reshape(Bn, t, H, HD).transpose(0, 2, 1, 3)
        q = split(hidden_states @ Wq.T + bq)
        k = split(hidden_states @ Wk.T + bk)
        v = split(hidden_states @ Wv.T + bv)
        scores = jnp.einsum('bhsd,bhtd->bhst', q, k)
        pos = jnp.arange(t)
        rel = (pos[None, :] - pos[:, None]).astype(scores.dtype)
        bias = alibi_slopes[:, None, None] * rel
        scores = (scores + bias[None]) / math.sqrt(HD)
        scores = 30.0 * jnp.tanh(scores / 30.0)
        causal = pos[:, None] >= pos[None, :]
        scores = jnp.where(causal[None, None], scores, -jnp.inf)
        probs = jax.nn.softmax(scores, axis=-1)
        ctx = jnp.einsum('bhst,bhtd->bhsd', probs, v)
        ctx = ctx.transpose(0, 2, 1, 3).reshape(Bn, t, D)
        return ctx @ Wo.T + bo

    def _L0_xattn_ref(q, k, v):
        import jax, jax.numpy as jnp
        import numpy as np
        import math
        NUM_Q_HEADS = 32
        NUM_KV_HEADS = 8
        B, S, E = q.shape
        H, KV = (NUM_Q_HEADS, NUM_KV_HEADS)
        D = E // H
        G = H // KV
        scale = math.sqrt(D)
        qh = q.reshape(B, S, KV, G, D).transpose(0, 2, 3, 1, 4)
        kh = k.reshape(B, S, KV, D).transpose(0, 2, 1, 3)
        vh = v.reshape(B, S, KV, D).transpose(0, 2, 1, 3)
        scores = jnp.einsum('bkgsd,bktd->bkgst', qh, kh) / scale
        weights = jax.nn.softmax(scores, axis=-1)
        out = jnp.einsum('bkgst,bktd->bkgsd', weights, vh)
        return out.transpose(0, 3, 1, 2, 4).reshape(B, S, E)

    def _L0_ffn_ref(hidden_states, gate_w, w_gate_up, w_down, ws_gate_up, ws_down):
        import jax, jax.numpy as jnp
        import numpy as np
        HIDDEN = 256
        FFN = 176
        N_EXPERTS = 64
        TOP_K = 6
        N_SHARED = 2
        SHARED_FFN = FFN * N_SHARED
        ROUTED_SCALING = 1.0
        EPS = 1e-20

        def _moe_forward(x, gate_w, w_gate_up, w_down, ws_gate_up, ws_down):
            T = x.shape[0]
            logits = jnp.einsum('th,eh->te', x.astype(jnp.float32), gate_w.astype(jnp.float32))
            scores = jax.nn.softmax(logits, axis=-1)
            topk_w, topk_ids = jax.lax.top_k(scores, TOP_K)
            topk_w = topk_w / (jnp.sum(topk_w, axis=-1, keepdims=True) + EPS)
            topk_w = topk_w * ROUTED_SCALING
            comb = jnp.zeros((T, N_EXPERTS), dtype=x.dtype)
            comb = comb.at[jnp.arange(T)[:, None], topk_ids].add(topk_w.astype(x.dtype))
            gu = jnp.einsum('th,efh->tef', x, w_gate_up)
            g, u = (gu[..., :FFN], gu[..., FFN:])
            act = jax.nn.silu(g) * u
            act = act * comb[:, :, None]
            routed = jnp.einsum('tef,ehf->th', act, w_down)
            sgu = jnp.einsum('th,fh->tf', x, ws_gate_up)
            sg, su = (sgu[..., :SHARED_FFN], sgu[..., SHARED_FFN:])
            shared = jnp.einsum('tf,hf->th', jax.nn.silu(sg) * su, ws_down)
            return routed + shared
        B, S, H = hidden_states.shape
        x = hidden_states.reshape(-1, H)
        out = _moe_forward(x, gate_w, w_gate_up, w_down, ws_gate_up, ws_down)
        return out.reshape(B, S, H)
    x = _layernorm(x + _L0_attn_ref(x, L0_attn_Wq, L0_attn_bq, L0_attn_Wk, L0_attn_bk, L0_attn_Wv, L0_attn_bv, L0_attn_Wo, L0_attn_bo, L0_attn_alibi_slopes), axis=-1)
    x = _layernorm(x + _L0_xattn_ref(x, ctx_512, ctx_512), axis=-1)
    x = _layernorm(x + _L0_ffn_ref(x, L0_ffn_gate_w, L0_ffn_w_gate_up, L0_ffn_w_down, L0_ffn_ws_gate_up, L0_ffn_ws_down), axis=-1)
    return x

_drawn_inputs = setup_inputs


def setup_inputs(seed=0):
    import zlib

    import numpy as np

    out = dict(_drawn_inputs(seed))
    spreads = {}
    factors = {'L0_attn_Wq': 8.0,
     'L0_attn_bq': 25.872,
     'L0_attn_Wk': 8.0,
     'L0_attn_bk': 64.0,
     'L0_attn_bv': 8.0,
     'L0_attn_bo': 6.3,
     'L0_attn_alibi_slopes': 7.555,
     'L0_ffn_gate_w': 8.0,
     'L0_ffn_w_gate_up': 8.0,
     'L0_ffn_w_down': 8.0,
     'L0_ffn_ws_gate_up': 2.846,
     'L0_ffn_ws_down': 2.844}
    for name, (base, spread) in spreads.items():
        noise = np.random.default_rng([zlib.crc32(name.encode()), seed]).standard_normal(out[name].shape)
        drawn = base * np.exp(spread * noise) if base else spread * noise
        out[name] = jnp.asarray(drawn.astype(out[name].dtype))
    for name, factor in factors.items():
        out[name] = (out[name] * factor).astype(out[name].dtype)
    return out
```

```python
from contextlib import ExitStack

import concourse.bass as bass
from concourse import mybir

ALU = mybir.AluOpType
ACT = mybir.ActivationFunctionType
AX = mybir.AxisListType.X
F32 = mybir.dt.float32
I32 = mybir.dt.int32
U32 = mybir.dt.uint32

P = 128
D = 256
KC = D // P
B, S = 32, 64
T = B * S
NT = T // P
H, HD = 16, 16
XH, XD, KV = 32, 8, 8
XG = XH // KV
HC = XH // KC
NE, F, TOPK = 64, 176, 6
FH = F // 2
SF = 352
SFC = ((0, 128), (128, 128), (256, 96))
LN_EPS, TOP_EPS = 1e-5, 1e-20
CAP = 30.0

ROW = 272
C_TOK, C_W, C_E = D, D + 1, D + 1 + TOPK
REGION = T + P
PAD_ROW = NE * REGION
NB = 160
WS = 4
WGU, WDN = KC * 2 * F, 2 * D
W_SLOT = WGU + WDN
XS = 4
GROUP = 4
N512 = 512


def wait(eng, sem, value):
    if isinstance(value, int) and value <= 0:
        return
    eng.wait_ge(sem, value)


class Steps:

    def __init__(self, eng, sem, run, total, spare=None):
        self.eng, self.sem, self.base, self.total, self.n = eng, sem, run * total, total, 0
        self.spare = spare

    def then(self, instruction, alone=False):
        self.n += 1
        assert self.n <= self.total
        instruction.then_inc(self.sem, 1)
        self.eng.wait_ge(self.sem, self.base + self.n)
        if alone:
            self.eng.sem_inc(self.spare, 1)


NEWTON = 3
LN_STEPS = 5 + 3 * NEWTON


def norm_steps(nc, steps, row, stats, mv, rstd, tmp, tmpi):
    v = nc.vector
    var = tmp[:, 0:1]
    steps.then(v.bn_stats(stats, row), alone=True)
    steps.then(v.bn_aggr(mv, stats))
    steps.then(v.tensor_scalar(var, mv[:, 1:2], LN_EPS, None, ALU.add))
    steps.then(v.tensor_scalar(tmpi, var.bitcast(I32), 1, None, ALU.arith_shift_right))
    steps.then(v.tensor_scalar(rstd.bitcast(I32), tmpi, -1.0, float(0x5F3759DF), ALU.mult, ALU.add))
    for _ in range(NEWTON):
        steps.then(v.scalar_tensor_tensor(tmp[:, 1:2], rstd, rstd, var, ALU.mult, ALU.mult))
        steps.then(v.tensor_scalar(tmp[:, 1:2], tmp[:, 1:2], -0.5, 1.5, ALU.mult, ALU.add))
        steps.then(v.tensor_tensor(rstd, rstd, tmp[:, 1:2], ALU.mult))


def decoder(nc, x, xT, ctxT, ctx, wqT, wkT, wvT, woT, bq, bk, bv, bo, slopes, gwT, wgu, wdn, wsgu, wsda, wsdb, out):
    with ExitStack() as stack:
        def sb(name, shape, dt=F32):
            return stack.enter_context(nc.sbuf_tensor(name, shape, dt))

        def sem(name):
            return stack.enter_context(nc.semaphore(name))

        rows_d = nc.dram_tensor("rows_d", [PAD_ROW + P, ROW], F32, kind="Internal").ap()
        acc_d = [nc.dram_tensor(f"acc{q}_d", [T + P, D], F32, kind="Internal").ap() for q in range(2)]
        tab_d = nc.dram_tensor("tab_d", [8, P], F32, kind="Internal").ap()
        tabi_d = nc.dram_tensor("tabi_d", [8, P], I32, kind="Internal").ap()

        ps = stack.enter_context(nc.psum_tensor("ps", [P, 8, N512], F32))

        x_sb = sb("x_sb", [P, NT, ROW])
        xT_sb = sb("xT_sb", [P, KC, T])
        share = xT_sb[:, :, :].rearrange("p c t -> p (c t)").rearrange("p (i d) -> p i d", i=NT)
        reg_qk = sb("reg_qk", [P, 2 * KC * T])
        qT = reg_qk[:, 0:KC * T].rearrange("p (c t) -> p c t", c=KC)
        kT = reg_qk[:, KC * T:].rearrange("p (c t) -> p c t", c=KC)
        xkey = reg_qk[:, :].rearrange("p (r c h t) -> p r c h t", r=2, c=KC, h=HC)
        NV = NT * H * 2 * (HD + 1)
        reg_v = sb("reg_v", [P, NV])
        v_sb = reg_v[:, :].rearrange("p (i h b e) -> p i h b e", i=NT, h=H, b=2)
        XP = HC * S
        xprob = reg_v[:, 0:4 * XP].rearrange("p (r c n) -> p r c n", r=2, c=KC)
        x2T = reg_v[:, 4 * XP:4 * XP + KC * T].rearrange("p (c t) -> p c t", c=KC)
        NQ = 2 * KC * 8 * P
        reg_q = sb("reg_q", [P, NQ + 2 * KC * P])
        qdiag = reg_q[:, 0:NQ].rearrange("p (r c h t) -> p r c h t", r=2, c=KC, h=8)
        kTr = reg_q[:, NQ:].rearrange("p (r c t) -> p r c t", r=2, c=KC)
        at = [0]

        def carve(n):
            at[0] += n
            return reg_q[:, at[0] - n:at[0]]

        xg = carve(XS * ROW).rearrange("p (r n) -> p r n", r=XS)
        xgT = carve(2 * D).rearrange("p (r n) -> p r n", r=2)
        gate = carve(2 * F).rearrange("p (r n) -> p r n", r=2)
        act = carve(2 * F).rearrange("p (r n) -> p r n", r=2)
        actT = carve(2 * 2 * P).rearrange("p (r n) -> p r n", r=2)
        y_sb = carve(XS * D).rearrange("p (r n) -> p r n", r=XS)
        wring = sb("wring", [P, WS * W_SLOT])
        ctx_st = wring[:, 0:B * S]
        prob = sb("prob", [P, 2, H * S])
        bias = sb("bias", [P, H, S])
        cbuf = sb("cbuf", [P, 4 * D])
        ctxn, ctxnT = (cbuf[:, q * 2 * D:(q + 1) * 2 * D].rearrange("p (r n) -> p r n", r=2) for q in range(2))
        NXV = 2 * KV * 2 * (XD + 1)
        xvr = cbuf[:, 0:2 * NXV].rearrange("p (r b k n) -> p r b k n", r=2, b=2, k=KV)
        x1r = sb("x1r", [P, 2, D])
        x1T = sb("x1T", [P, 2, KC, P])
        xpT = prob
        xval = sb("xval", [P, B, KV, 2, XD + 1])
        NVR = 2 * H * (HD + 1)
        vbuf = sb("vbuf", [P, 2 * NVR])
        vr = vbuf[:, :].rearrange("p (r h n) -> p r h n", r=2, h=H)
        x2r = vbuf[:, 0:2 * D].rearrange("p (r n) -> p r n", r=2)
        x2Tr = vbuf[:, 2 * D:4 * D].rearrange("p (r c t) -> p r c t", r=2, c=KC)
        res = sb("res", [P, 2, D])
        wq_sb, wk_sb, wv_sb, wo_sb = (sb(n, [P, KC, D]) for n in ("wq_sb", "wk_sb", "wv_sb", "wo_sb"))
        bq_sb, bk_sb = sb("bq_sb", [P, KC]), sb("bk_sb", [P, KC])
        bv_sb, bo_sb = sb("bv_sb", [P, D]), sb("bo_sb", [P, D])
        sl_sb = sb("sl_sb", [P, H])
        gw_sb = sb("gw_sb", [P, KC, NE])
        wsgu_sb = sb("wsgu_sb", [P, KC, 2 * SF])
        wsd_sb = sb("wsd_sb", [P, 3, D])
        sgate = prob[:, 0, 0:2 * N512].rearrange("p (r n) -> p r n", r=2)
        shid = reg_v[:, 0:3 * N512].rearrange("p (f n) -> p f n", f=3)
        ident, ones, tri = sb("ident", [P, P]), sb("ones", [P, P]), sb("tri", [P, P])
        rel_i, rel, mask = sb("rel_i", [P, S], I32), sb("rel", [P, S]), sb("mask", [P, S])
        ei_i, ei, eo = sb("ei_i", [P, NE], I32), sb("ei", [P, NE]), sb("eo", [P, NE])
        bi_i, bi = sb("bi_i", [P, 2], I32), sb("bi", [P, 2])
        pad = sb("pad", [P, ROW])
        crec = sb("crec", [P, 2, 8, 2])
        xmax = sb("xmax", [P, KC, HC])
        xrec = sb("xrec", [P, XH])
        lstats, lmv, lrs = sb("lstats", [P, 6]), sb("lmv", [P, 2]), sb("lrs", [P, 1])
        ltmp, ltmpi, nblki, wsi = sb("ltmp", [P, 2]), sb("ltmpi", [P, 1], I32), sb("nblki", [P, NE], I32), sb("wsi", [P, 2], I32)
        logit, lmax, lnmax = sb("logit", [P, NE]), sb("lmax", [P, 1]), sb("lnmax", [P, 1])
        pexp, psum, prs, pr = sb("pexp", [P, NE]), sb("psum", [P, 1]), sb("prs", [P, 1]), sb("pr", [P, NE])
        top, topi, topf = sb("top", [P, 8]), sb("topi", [P, 8], U32), sb("topf", [P, 8])
        tsum, trec = sb("tsum", [P, 1]), sb("trec", [P, 1])
        hot = reg_q[:, 0:2 * TOPK * NE].rearrange("p (r k e) -> p r k e", r=2, k=TOPK)
        hpos = reg_q[:, 2 * TOPK * NE:3 * TOPK * NE].rearrange("p (k e) -> p k e", k=TOPK)
        xtmp = reg_q[:, 3 * TOPK * NE:3 * TOPK * NE + D]
        sel, pos, slotf = sb("sel", [P, 2, NE]), sb("pos", [P, NE]), sb("slotf", [P, TOPK])
        slot = sb("slot", [P, NT * 8], I32)
        off = sb("off", [P, NE])
        at_tables = 3 * TOPK * NE + D
        nblk, pre0, pre1, start, rowof, ge_end, ge_start, inb = (
            reg_q[:, at_tables + n * NE:at_tables + (n + 1) * NE] for n in range(8))
        pre = [pre0, pre1]
        cols, ns = sb("cols", [P, 8]), sb("ns", [P, 2])
        tcol, tcoli = x1r[0:8, 0, 0:P], x1r[0:8, 0, P:2 * P].bitcast(I32)
        tab = bias[0:1, :, :].rearrange("p h s -> p (h s)").bitcast(I32)
        offi, endi = (x1r[0:1, 1, n * NE:(n + 1) * NE].bitcast(I32) for n in range(2))
        ebc = carve(2 * P)
        wcol, w6 = sb("wcol", [P, 2]), sb("w6", [P, TOPK])
        toks = sb("toks", [P, XS], I32)
        accl = prob[:, :, 0:2 * D]
        outr = ctxn

        l_x, l_xT, l_wqk, l_wv, l_wo, l_ctx, l_late = (sem(n) for n in ("l_x", "l_xT", "l_wqk", "l_wv", "l_wo", "l_ctx", "l_late"))
        const, vinit, xinit, relc, dinit = sem("const"), sem("vinit"), sem("xinit"), sem("relc"), sem("dinit")
        c_pool, row_in, waited, pool_waited = sem("c_pool"), sem("row_in"), sem("waited"), sem("pool_waited")
        iotas = sem("iotas")
        c_dve = sem("c_dve")
        qk_mm, qk_ev, v_mm, v_ev = sem("qk_mm"), sem("qk_ev"), sem("v_mm"), sem("v_ev")
        qd_in = [sem("qd_in0"), sem("qd_in1")]
        sc_mm, biased, tanhed, exped, masked = sem("sc_mm"), sem("biased"), sem("tanhed"), sem("exped"), sem("masked")
        pv_mm, ctx_rec, ctx_n, ctx_t, ctx_ev, o_mm, o_res, o_ln, x1_done = (
            sem(n) for n in ("pv_mm", "ctx_rec", "ctx_n", "ctx_t", "ctx_ev", "o_mm", "o_res", "o_ln", "x1_done"))
        xz, xk_in = sem("xz"), [sem("xk_in0"), sem("xk_in1")]
        x1r_in, x1_t, x1_ev = sem("x1r_in"), sem("x1_t"), sem("x1_ev")
        xs_mm, xs_max, xs_sub, xs_exp, xp_t, xp_evd, xp_eva = (
            sem(n) for n in ("xs_mm", "xs_max", "xs_sub", "xs_exp", "xp_t", "xp_evd", "xp_eva"))
        xv_mm, xn_steps, xc_free, x2_done, x2r_in, x2_t, x2_ev, x2T_in = (
            sem(n) for n in ("xv_mm", "xn_steps", "xc_free", "x2_done", "x2r_in", "x2_t", "x2_ev", "x2T_in"))
        lg_mm, lg_in, lg_steps, lg_max, lg_exp, ra_steps, sel_in = (
            sem(n) for n in ("lg_mm", "lg_in", "lg_steps", "lg_max", "lg_exp", "ra_steps", "sel_in"))
        rk_mm, rb_steps, rk_free, slot_in, scat = sem("rk_mm"), sem("rb_steps"), sem("rk_free"), sem("slot_in"), sem("scat")
        tb_cols, tb_t, tb_row, tb_d, tb_in, tb_off, pads = (
            sem(n) for n in ("tb_cols", "tb_t", "tb_row", "tb_d", "tb_in", "tb_off", "pads"))
        sg_mm, sg_act, sh_in, sd_mm, sd_ev = sem("sg_mm"), sem("sg_act"), sem("sh_in"), sem("sd_mm"), sem("sd_ev")
        w_in, w_ready = [sem(f"w_in{q}") for q in range(WS)], sem("w_ready")
        xg_in = [sem(f"xg_in{q}") for q in range(XS)]
        b_t1, b_xgT, b_gu, b_silu, b_act, b_t2, b_actT, b_dn, b_y, b_meta, b_w = (
            sem(n) for n in ("b_t1", "b_xgT", "b_gu", "b_silu", "b_act", "b_t2", "b_actT", "b_dn", "b_y", "b_meta", "b_w"))
        added = [sem("added0"), sem("added1")]
        ac_in, f_steps, f_out, stored = [sem("ac_in0"), sem("ac_in1")], sem("f_steps"), sem("f_out"), [sem("stored0"), sem("stored1")]

        N_CONST_DVE = 14
        LN_N, RA_N, RB_N, XN_N, FIN_N = LN_STEPS, 8, 3, 3 + LN_STEPS, 2 + LN_STEPS

        block = stack.enter_context(nc.Block())

        def tiles(eng, step, ahead, behind):
            lo = 4
            hi = NT - 2 * ((ahead + 1) // 2)
            for i in range(-ahead, lo):
                step(i, i % 2)
            with eng.Fori(lo // 2, hi // 2) as g:
                for r in range(2):
                    step(g * 2 + r, r)
            for i in range(hi, NT + behind):
                step(i, i % 2)

        def there(i, shift=0):
            return not isinstance(i, int) or 0 <= i + shift < NT

        def half(i, r):
            return (i - r) // 2 if isinstance(i, int) else None

        @block.sync
        def _(sp):
            sp.dma_start(wq_sb[:], wqT).then_inc(l_wqk, 16)
            sp.dma_start(wk_sb[:], wkT).then_inc(l_wqk, 16)
            sp.dma_start(bq_sb[:], bq).then_inc(l_wqk, 16)
            sp.dma_start(bk_sb[:], bk).then_inc(l_wqk, 16)
            sp.dma_start(xT_sb[:], xT).then_inc(l_xT, 16)
            sp.dma_start(wv_sb[:], wvT).then_inc(l_wv, 16)
            sp.dma_start(bv_sb[:], bv.to_broadcast([P, D])).then_inc(l_wv, 16)
            sp.dma_start(sl_sb[:], slopes.to_broadcast([P, H])).then_inc(l_x, 16)
            sp.dma_start(x_sb[:, :, 0:D], x).then_inc(l_x, 16)
            sp.dma_start(bo_sb[:], bo.to_broadcast([P, D])).then_inc(l_x, 16)
            sp.dma_start(wo_sb[:], woT).then_inc(l_wo, 16)
            for q in range(2):
                sp.dma_start(ctx_st[q * S:(q + 1) * S, :], ctx).then_inc(l_ctx, 16)
            sp.dma_start(gw_sb[:], gwT).then_inc(l_late, 16)
            sp.dma_start(wsgu_sb[:], wsgu).then_inc(l_late, 16)
            sp.dma_start(wsd_sb[:, 0:2, :], wsda).then_inc(l_late, 16)
            sp.dma_start(wsd_sb[0:SFC[2][1], 2, :], wsdb).then_inc(l_late, 16)
            sp.wait_ge(dinit, 3)
            for q in range(2):
                for j in range((T + P) // P):
                    sp.dma_start(acc_d[q][j * P:(j + 1) * P, :], pad[:, 0:D]).then_inc(pads, 16)
            sp.dma_start(rows_d[PAD_ROW:PAD_ROW + P, :], pad[:]).then_inc(pads, 16)

            sp.wait_ge(v_ev, 2 * NT)
            sp.wait_ge(qk_ev, 4 * KC * 2)
            sp.wait_ge(vinit, 4)

            def q_tile(i, r, n):
                wait(sp, sc_mm, i - 1)
                for h in range(8):
                    p = slice(HD * h, HD * (h + 1))
                    sp.dma_start(qdiag[p, r, :, h, :], qT[p, :, bass.ds(i * P, P)]).then_inc(qd_in[r], 16)
                sp.dma_start(kTr[:, r, :, :], kT[:, :, bass.ds(i * P, P)]).then_inc(qd_in[r], 16)
                wait(sp, pv_mm, i - 1)
                sp.dma_start(vr[:, r, :, :], v_sb[:, bass.ds(i, 1), :, :, :].rearrange("p i h b e -> p (i h) (b e)")).then_inc(qd_in[r], 16)

            for i in range(2):
                q_tile(i, i, 0)
            with sp.Fori(1, NT // 2) as g:
                for r in range(2):
                    q_tile(g * 2 + r, r, g)

            key_rows = ctxT.rearrange("(c k d) t -> k d c t", c=KC, d=XD)
            sp.wait_ge(xz, 1)
            sp.wait_ge(xinit, 4)

            def key_tile(i, r):
                if not (isinstance(i, int) and i < 2):
                    sp.wait_ge(xs_mm, (i - 1) * KC)
                for h in range(HC):
                    sp.dma_start(xkey[XD * h:XD * (h + 1), r, :, h, :],
                                 key_rows[h // XG, :, :, bass.ds(i * P, P)]).then_inc(xk_in[r], 16)
                if not (isinstance(i, int) and i < 2):
                    sp.wait_ge(xv_mm, (i - 1) * KC)
                sp.dma_start(xvr[:, r, :, :, :].rearrange("p b k n -> p b (k n)"),
                             xval[:, bass.ds(i * 2, 2), :, :, :].rearrange("p b k q e -> p b (k q e)")).then_inc(xk_in[r], 16)

            for i in range(2):
                key_tile(i, i)
            with sp.Fori(1, NT // 2) as g:
                for r in range(2):
                    key_tile(g * 2 + r, r)

            def weights(e, q):
                w = wring[:, q * W_SLOT:(q + 1) * W_SLOT]
                sp.dma_start(w[:, 0:WGU], wgu[bass.ds(e, 1), :, :].rearrange("e p n -> (e p) n")).then_inc(w_in[q], 16)
                sp.dma_start(w[0:FH, WGU:], wdn[bass.ds(e, 1), :, :].rearrange("e p n -> (e p) n")).then_inc(w_in[q], 16)

            sp.wait_ge(xinit, 4)
            for e in range(WS):
                weights(e, e)
            sp.wait_ge(tb_off, 1)
            with sp.Fori(0, NE) as e:
                at_row = sp.value_load(offi[0:1, bass.ds(e, 1)], min_val=0, max_val=PAD_ROW)
                sp.dma_start(rows_d[bass.ds(at_row, P), :], pad[:]).then_inc(pads, 16)
            sp.wait_ge(tb_row, 2)
            sp.dma_start(tabi_d, tcoli).then_inc(tb_d, 16)
            sp.dma_start(tab_d, tcol).then_inc(tb_d, 16)
            sp.wait_ge(tb_d, 32)
            sp.dma_start(tab, tabi_d.rearrange("(o a) n -> o (a n)", o=1)).then_inc(tb_in, 16)
            sp.dma_start(ebc, tab_d[0:2, :].rearrange("(o a) n -> o (a n)", o=1).to_broadcast([P, 2 * P])).then_inc(tb_in, 16)
            for e in range(2):
                sp.wait_ge(w_in[e], 32)
                sp.sem_inc(w_ready, 1)
            with sp.Fori(1, NE // WS) as g:
                for q in range(WS):
                    done = sp.value_load(endi[0:1, bass.ds((g - 1) * WS + q, 1)], min_val=0, max_val=NB)
                    sp.wait_ge(b_dn, done + 1)
                    weights(g * WS + q, q)
                    u = (q + 2) % WS
                    sp.wait_ge(w_in[u], g * 32 if q < 2 else (g + 1) * 32)
                    sp.sem_inc(w_ready, 1)
            for q in range(2, WS):
                sp.wait_ge(w_in[q], 32 * (NE // WS))
                sp.sem_inc(w_ready, 1)

            for q in range(2):
                sp.wait_ge(added[q], 16 * (NB // 2))

            def acc_tile(i, r):
                wait(sp, f_out, i - 1)
                for q in range(2):
                    sp.dma_start(accl[:, r, bass.ds(q * D, D)], acc_d[q][bass.ds(i * P, P), :]).then_inc(ac_in[r], 16)

            for i in range(2):
                acc_tile(i, i)
            with sp.Fori(1, NT // 2) as g:
                for r in range(2):
                    acc_tile(g * 2 + r, r)

        @block.gpsimd
        def _(pool):
            g = nc.gpsimd
            g.memset(ident[:], 0.0).then_inc(c_pool, 1)
            g.memset(tri[:], 1.0).then_inc(c_pool, 1)
            g.memset(ones[:], 1.0).then_inc(const, 1)
            pool.wait_ge(c_pool, 2)
            g.affine_select(out=ident[:], in_=ident[:], compare_op=ALU.not_equal, fill=1.0, base=0,
                            pattern=[[-1, P]], channel_multiplier=1).then_inc(const, 1)
            g.affine_select(out=tri[:], in_=tri[:], compare_op=ALU.is_gt, fill=0.0, base=0,
                            pattern=[[1, P]], channel_multiplier=-1).then_inc(const, 1)
            g.iota(rel_i[:], pattern=[[-1, S]], base=0, channel_multiplier=1).then_inc(iotas, 1)
            g.iota(ei_i[:], pattern=[[1, NE]], base=0, channel_multiplier=0).then_inc(iotas, 1)
            g.iota(bi_i[:], pattern=[[P, 2]], base=0, channel_multiplier=1).then_inc(iotas, 1)
            g.iota(pad[:, C_TOK:C_TOK + 1].bitcast(I32), pattern=[[0, 1]], base=T, channel_multiplier=1).then_inc(c_pool, 1)
            g.memset(pad[:, 0:D], 0.0).then_inc(dinit, 1)
            g.memset(pad[:, C_W:ROW], -1.0).then_inc(dinit, 1)
            pool.wait_ge(c_pool, 3)
            pool.sem_inc(dinit, 1)
            g.iota(x_sb[:, :, C_TOK:C_TOK + 1].bitcast(I32), pattern=[[P, NT], [0, 1]], base=0,
                   channel_multiplier=1).then_inc(xinit, 1)
            g.memset(x_sb[:, :, C_E + TOPK:ROW], 0.0).then_inc(xinit, 1)
            g.memset(xval[:], 0.0).then_inc(c_pool, 1)
            pool.wait_ge(c_pool, 4)
            pool.wait_ge(l_ctx, 32)
            for q in range(2):
                p = slice(q * S, (q + 1) * S)
                g.memset(xval[p, :, :, q, XD:XD + 1], 1.0).then_inc(c_pool, 1)
                g.tensor_copy(xval[p, :, :, q, 0:XD],
                              ctx_st[p, :].rearrange("p (b k d) -> p b k d", b=B, k=KV)).then_inc(xinit, 1)
                pool.wait_ge(c_pool, 5 + q)
                pool.wait_ge(xinit, 3 + q)

            def step(i):
                if there(i, 2):
                    j = i + 2
                    pool.wait_ge(x1_done, j + 1)
                    wait(pool, x1_t, j - 1)
                    g.tensor_copy(x1r[:, j % 2, :], x_sb[:, j, 0:D]).then_inc(x1r_in, 1)
                if there(i):
                    pool.wait_ge(x2_done, i + 1)
                    wait(pool, x2_t, i - 1)
                    g.tensor_copy(x2r[:, i % 2, :], x_sb[:, i, 0:D]).then_inc(x2r_in, 1)
                if there(i, -1):
                    j = i - 1
                    pool.wait_ge(x2_ev, j + 1)
                    g.tensor_copy(x2T[:, :, j * P:(j + 1) * P], x2Tr[:, j % 2, :, :]).then_inc(x2T_in, 1)
                if there(i, -2):
                    j = i - 2
                    pool.wait_ge(slot_in, j + 1)
                    for k in range(TOPK):
                        g.indirect_dma_start(
                            out=rows_d[:, :],
                            out_offset=bass.IndirectOffsetOnAxis(ap=slot[:, 8 * j + k:8 * j + k + 1], axis=0),
                            in_=x_sb[:, j, :], in_offset=None).then_inc(scat, 16)

            for i in range(-2, NT + 2):
                step(i)

            pool.wait_ge(pads, 16 * (2 * (T + P) // P + 1 + NE))

            def add_block(n, q):
                r = q % 2
                pool.wait_ge(b_y, n * XS + q + 1)
                wait(pool, added[r], n * 32 + 16 * (q // 2))
                pool.sem_inc(pool_waited, 1)
                g.indirect_dma_start(
                    out=acc_d[r][:, :], out_offset=bass.IndirectOffsetOnAxis(ap=toks[:, q:q + 1], axis=0),
                    in_=y_sb[:, q, :], in_offset=None, compute_op=ALU.add).then_inc(added[r], 16)

            for q in range(XS):
                add_block(0, q)
            with pool.Fori(1, NB // XS) as n:
                for q in range(XS):
                    add_block(n, q)

        @block.scalar
        def _(sc):
            a = nc.scalar
            sc.wait_ge(l_wqk, 64)
            for n in range(T // N512):
                for m in range(2 * KC):
                    dst, b = ((qT, bq_sb), (kT, bk_sb))[m // KC]
                    c = m % KC
                    sc.wait_ge(qk_mm, 4 * n + m + 1)
                    a.activation(dst[:, c, n * N512:(n + 1) * N512], ps[:, m, :], ACT.Identity,
                                 bias=b[:, c:c + 1]).then_inc(qk_ev, 1)

            def self_step(i, r):
                if there(i, -1):
                    j = i - 1
                    sc.wait_ge(ctx_t, j + 1)
                    wait(sc, o_mm, j - 1)
                    a.activation(ctxnT[:, 1 - r, :].rearrange("p (q b s) -> p b q s", q=2, b=2),
                                 ps[:, 6, 0:D].rearrange("p (b q s) -> p b q s", b=2, q=2), ACT.Copy).then_inc(ctx_ev, 1)
                if there(i, 1):
                    j = i + 1
                    sc.wait_ge(biased, j + 1)
                    a.activation(prob[:, 1 - r, :], prob[:, 1 - r, :], ACT.Tanh,
                                 scale=1.0 / (CAP * HD ** 0.5)).then_inc(tanhed, 1)
                    sc.wait_ge(tanhed, j + 1)
                    a.activation(prob[:, 1 - r, :], prob[:, 1 - r, :], ACT.Exp, scale=CAP).then_inc(exped, 1)

            tiles(sc, self_step, 1, 1)

            def cross_exp(i, r, c):
                sc.wait_ge(xs_sub, i * KC + c + 1)
                a.activation(xprob[:, r, c, :], xprob[:, r, c, :], ACT.Exp, scale=XD ** -0.5).then_inc(xs_exp, 1)

            def cross_evict(i, c):
                sc.wait_ge(xp_t, i * KC + c + 1)
                if not (isinstance(i, int) and i == 0):
                    sc.wait_ge(xv_mm, (i - 1) * KC + c + 1)
                a.activation(xpT[:, c, N512:2 * N512], ps[:, 5, :], ACT.Copy).then_inc(xp_eva, 1)

            def cross_step(i, r):
                if there(i, 1):
                    cross_exp(i + 1, 1 - r, 0)
                if there(i, -1):
                    j = i - 1
                    sc.wait_ge(x2_t, j + 1)
                    wait(sc, x2T_in, j - 1)
                    wait(sc, lg_mm, j - 1)
                    a.activation(x2Tr[:, 1 - r, :, :].rearrange("p c t -> p (c t)"), ps[:, 7, 0:D], ACT.Copy).then_inc(x2_ev, 1)
                if there(i):
                    cross_evict(i, 0)
                if there(i, 1):
                    cross_exp(i + 1, 1 - r, 1)
                if there(i):
                    cross_evict(i, 1)
                if there(i, 2):
                    j = i + 2
                    sc.wait_ge(x1_t, j + 1)
                    if not (isinstance(i, int) and i < 0):
                        sc.wait_ge(xs_mm, (j - 1) * KC)
                    a.activation(x1T[:, r, :, :].rearrange("p c t -> p (c t)"), ps[:, 7, 0:D], ACT.Copy).then_inc(x1_ev, 1)
                if there(i, -1):
                    j = i - 1
                    sc.wait_ge(lg_max, j + 1)
                    a.activation(pexp[:], logit[:], ACT.Exp, bias=lnmax[:, 0:1], accum_out=psum[:]).then_inc(lg_exp, 1)

            tiles(sc, cross_step, 2, 2)

            with sc.Fori(0, T // N512) as n:
                for f in range(3):
                    m, q = SFC[f][1], f % 2
                    sc.wait_ge(sg_mm, n * 3 + (f + 1))
                    if f >= 2:
                        sc.wait_ge(sh_in, n * 3 + (f - 1))
                    a.activation(sgate[0:m, q, :], ps[0:m, 2 * q, :], ACT.Silu).then_inc(sg_act, 1)

            sc.wait_ge(tb_in, 32)
            sc.wait_ge(scat, 16 * TOPK * NT)
            sc.wait_ge(pads, 16 * (2 * (T + P) // P + 1 + NE))
            sc.wait_ge(sc_mm, NT)

            def rows_in(b, q):
                at_row = sc.value_load(tab[0:1, bass.ds(b + 2 * P, 1)], min_val=0, max_val=PAD_ROW)
                if not (isinstance(b, int) and b < XS):
                    sc.wait_ge(b_t1, b - XS + 1)
                    sc.wait_ge(b_meta, (b - XS) * 3 + 3)
                sc.dma_start(xg[:, q, :], rows_d[bass.ds(at_row, P), :]).then_inc(xg_in[q], 16)

            for b in range(XS):
                rows_in(b, b)

            def block_step(b, r, q, first=False, more=True, rows=True):
                if not first:
                    sc.wait_ge(b_t2, b + 1)
                    wait(sc, b_dn, b)
                    a.activation(actT[0:FH, r, :], ps[0:FH, 4 + r, 0:2 * P], ACT.Copy).then_inc(b_actT, 1)
                if more:
                    sc.wait_ge(b_gu, b + 2)
                    wait(sc, b_act, b)
                    a.activation(gate[:, 1 - r, :], ps[:, 2 + (1 - r), 0:F], ACT.Silu).then_inc(b_silu, 1)
                if rows and not first:
                    rows_in(b + XS, q)

            block_step(-1, 1, 3, first=True)
            for b in range(XS):
                block_step(b, b % 2, b)
            with sc.Fori(1, NB // XS - 1) as n:
                for q in range(XS):
                    block_step(n * XS + q, q % 2, q)
            for b in range(NB - XS, NB):
                block_step(b, b % 2, b % XS, more=b + 1 < NB, rows=False)

            def out_tile(i, r):
                sc.wait_ge(f_out, i + 1)
                sc.dma_start(out[:, bass.ds(i, 1), :].rearrange("p i d -> p (i d)"), outr[:, r, :]).then_inc(stored[r], 16)

            with sc.Fori(0, NT // 2) as g2:
                for r in range(2):
                    out_tile(g2 * 2 + r, r)
            for r in range(2):
                sc.wait_ge(stored[r], 16 * (NT // 2))

        @block.tensor
        def _(pe):
            mm = pe.matmul
            pe.wait_ge(l_wqk, 64)
            pe.wait_ge(l_xT, 16)
            for n in range(T // N512):
                for m in range(2 * KC):
                    w, c = (wq_sb, wk_sb)[m // KC], m % KC
                    if n:
                        pe.wait_ge(qk_ev, 4 * (n - 1) + m + 1)
                    for k in range(KC):
                        last = mm(ps[:, m, :], w[:, k, c * P:(c + 1) * P], xT_sb[:, k, n * N512:(n + 1) * N512],
                                  start=(k == 0), stop=(k == KC - 1))
                    last.then_inc(qk_mm, 1)
                if n == 0:
                    pe.wait_ge(l_wv, 32)
                for j in range(GROUP):
                    i = n * GROUP + j
                    if n:
                        pe.wait_ge(v_ev, 2 * (i - GROUP) + 2)
                    for k in range(KC):
                        last = mm(ps[:, 4 + j, 0:D], xT_sb[:, k, i * P:(i + 1) * P], wv_sb[:, k, :],
                                  start=(k == 0), stop=(k == KC - 1))
                    last.then_inc(v_mm, 1)
            pe.wait_ge(const, 3)
            pe.wait_ge(l_wo, 16)
            pe.wait_ge(qk_ev, 16)
            pe.wait_ge(v_ev, 2 * NT)

            def self_step(i, r):
                if there(i, 1):
                    j, q = i + 1, 1 - r
                    pe.wait_ge(qd_in[q], ((j - q) // 2 + 1) * 160 if isinstance(j, int) else (j - q) * 80 + 160)
                    wait(pe, biased, j - 1)
                    for c in range(KC):
                        for b in range(2):
                            t = slice(b * S, (b + 1) * S)
                            last = mm(ps[t, 2 * q + c, :], kTr[:, q, c, t], qdiag[:, q, c, :, t], start=True, stop=True)
                    last.then_inc(sc_mm, 1)
                if there(i, -1):
                    j, q = i - 1, 1 - r
                    pe.wait_ge(ctx_n, j + 1)
                    wait(pe, ctx_ev, j)
                    for b in range(2):
                        last = pe.transpose(ps[:, 6, b * P:(b + 1) * P], ctxn[:, q, b * P:(b + 1) * P], ident[:])
                    last.then_inc(ctx_t, 1)
                if there(i):
                    pe.wait_ge(masked, i + 1)
                    wait(pe, ctx_n, i - 1)
                    for h in range(H):
                        last = mm(ps[(h % 2) * S:(h % 2 + 1) * S, 4 + r, (h // 2) * 34:(h // 2 + 1) * 34],
                                  prob[:, r, h * S:(h + 1) * S],
                                  vr[:, r, h, :],
                                  start=True, stop=True)
                    last.then_inc(pv_mm, 1)
                if there(i, -1):
                    j, q = i - 1, 1 - r
                    pe.wait_ge(ctx_ev, j + 1)
                    wait(pe, o_res, j)
                    for q2 in range(2):
                        last = mm(ps[:, 7, 0:D], ctxnT[:, q, q2 * P:(q2 + 1) * P], wo_sb[:, q2, :],
                                  start=(q2 == 0), stop=(q2 == 1))
                    last.then_inc(o_mm, 1)

            tiles(pe, self_step, 1, 1)
            pe.wait_ge(o_res, NT)
            pe.wait_ge(xinit, 4)
            pe.wait_ge(l_late, 64)

            def scores(i, r, c):
                if c == 0:
                    pe.wait_ge(xk_in[r], ((i - r) // 2 + 1) * 272 if isinstance(i, int) else (i - r) * 136 + 272)
                    pe.wait_ge(x1_ev, i + 1)
                if not (isinstance(i, int) and i == 0):
                    pe.wait_ge(xs_sub, (i - 1) * KC + c + 1)
                for b in range(2):
                    t = slice(b * S, (b + 1) * S)
                    for q in range(2):
                        last = mm(ps[t, 2 * c + q, :], x1T[:, r, c, t], xkey[:, r, c, 8 * q:8 * (q + 1), t],
                                  start=True, stop=True)
                last.then_inc(xs_mm, 1)

            def turn(i, r, c):
                pe.wait_ge(xs_exp, i * KC + c + 1)
                if not (isinstance(i, int) and i == 0 and c == 0):
                    pe.wait_ge(xp_evd, i * KC + c)
                    pe.wait_ge(xp_eva, i * KC + c)
                for n in range(8):
                    last = pe.transpose(ps[:, 4 + n // 4, (n % 4) * P:(n % 4 + 1) * P],
                                        xprob[:, r, c, n * P:(n + 1) * P], ident[:])
                last.then_inc(xp_t, 1)

            def values(i, r, c):
                pe.wait_ge(xp_evd, i * KC + c + 1)
                pe.wait_ge(xp_eva, i * KC + c + 1)
                if c == 0:
                    wait(pe, xc_free, i)
                for n in range(8):
                    for b in range(2):
                        k = c * (KV // KC) + n // 2
                        last = mm(ps[b * S:(b + 1) * S, 6, (8 * c + n) * 18:(8 * c + n + 1) * 18],
                                  xpT[:, c, n * P + b * S:n * P + (b + 1) * S],
                                  xvr[:, r, b, k, :],
                                  start=True, stop=True)
                last.then_inc(xv_mm, 1)

            def cross_step(i, r):
                if there(i, 1):
                    scores(i + 1, 1 - r, 0)
                if there(i, -1):
                    j = i - 1
                    pe.wait_ge(x2r_in, j + 1)
                    wait(pe, rk_free, i - 2)
                    wait(pe, x1_ev, i + 2 if not isinstance(i, int) else min(i + 2, NT))
                    for c in range(KC):
                        last = pe.transpose(ps[:, 7, c * P:(c + 1) * P], x2r[:, 1 - r, c * P:(c + 1) * P], ident[:])
                    last.then_inc(x2_t, 1)
                if there(i):
                    turn(i, r, 0)
                if there(i, 1):
                    scores(i + 1, 1 - r, 1)
                if there(i, -1):
                    j = i - 1
                    pe.wait_ge(x2_ev, j + 1)
                    for c in range(KC):
                        last = mm(ps[:, 7, 0:NE], x2Tr[:, 1 - r, c, :], gw_sb[:, c, :], start=(c == 0), stop=(c == KC - 1))
                    last.then_inc(lg_mm, 1)
                if there(i):
                    values(i, r, 0)
                    turn(i, r, 1)
                if there(i, 2):
                    j = i + 2
                    pe.wait_ge(x1r_in, j + 1)
                    wait(pe, lg_in, i)
                    if isinstance(i, int) and i < 1:
                        wait(pe, x1_ev, i + 2)
                    for c in range(KC):
                        last = pe.transpose(ps[:, 7, c * P:(c + 1) * P], x1r[:, r, c * P:(c + 1) * P], ident[:])
                    last.then_inc(x1_t, 1)
                if there(i):
                    values(i, r, 1)
                if there(i, -2):
                    pe.wait_ge(sel_in, i - 1)
                    if there(i, 2):
                        pe.wait_ge(x1_ev, i + 3)
                    elif there(i, -1):
                        pe.wait_ge(lg_in, i)
                    else:
                        pe.wait_ge(rk_free, i - 2)
                    mm(ps[:, 7, 0:NE], tri[:], sel[:, r, :], start=True, stop=True)
                    mm(ps[:, 7, NE:2 * NE], ones[:], sel[:, r, :], start=True, stop=True).then_inc(rk_mm, 1)

            tiles(pe, cross_step, 2, 2)

            pe.wait_ge(tb_cols, 1)
            pe.transpose(ps[0:8, 7, 0:P], cols[:, 0:8], ident[:]).then_inc(tb_t, 1)

            pe.wait_ge(x2T_in, NT)
            pe.wait_ge(xs_sub, KC * NT)
            with pe.Fori(0, T // N512) as n:
                for f in range(3):
                    f0, m = SFC[f]
                    q = f % 2
                    if f >= 2:
                        pe.wait_ge(sh_in, n * 3 + (f - 1))
                    for u in range(2):
                        for k in range(KC):
                            last = mm(ps[0:m, 2 * q + u, :], wsgu_sb[:, k, u * SF + f0:u * SF + f0 + m],
                                      x2T[:, k, bass.ds(n * N512, N512)], start=(k == 0), stop=(k == KC - 1))
                    last.then_inc(sg_mm, 1)
                pe.wait_ge(sh_in, n * 3 + 3)
                for j in range(GROUP):
                    if j >= 2:
                        pe.wait_ge(sd_ev, n * GROUP + (j - 1))
                    for f in range(3):
                        m = SFC[f][1]
                        last = mm(ps[:, 4 + j % 2, 0:D], shid[0:m, f, j * P:(j + 1) * P], wsd_sb[0:m, f, :],
                                  start=(f == 0), stop=(f == 2))
                    last.then_inc(sd_mm, 1)
                pe.wait_ge(sd_ev, n * GROUP + 4)

            pe.wait_ge(tb_in, 32)
            pe.wait_ge(tb_row, 2)
            pe.sem_inc(b_dn, 1)

            def turn_rows(b, r, q, n):
                pe.wait_ge(xg_in[q], n * 16 + 16)
                wait(pe, b_xgT, b - 1)
                for c in range(KC):
                    last = pe.transpose(ps[:, r, c * P:(c + 1) * P], xg[:, q, c * P:(c + 1) * P], ident[:])
                last.then_inc(b_t1, 1)

            def gate_up(b, r):
                ready = pe.value_load(tab[0:1, bass.ds(b + 6 * P, 1)], min_val=1, max_val=NE)
                w_slot = pe.value_load(tab[0:1, bass.ds(b + 4 * P, 1)], min_val=0, max_val=WS - 1)
                pe.wait_ge(w_ready, ready)
                pe.wait_ge(b_xgT, b + 1)
                wait(pe, b_act, b - 1)
                for c in range(KC):
                    last = mm(ps[:, 2 + r, 0:2 * F], xgT[:, r, c * P:(c + 1) * P],
                              wring[:, bass.ds(w_slot * W_SLOT + c * 2 * F, 2 * F)], start=(c == 0), stop=(c == KC - 1))
                last.then_inc(b_gu, 1)
                return w_slot

            def block_step(b, r, q, n, slots, ahead2=True, ahead1=True):
                pe.wait_ge(b_act, b + 1)
                wait(pe, b_actT, b - 1)
                for c in range(2):
                    last = pe.transpose(ps[0:FH, 4 + r, c * P:(c + 1) * P], act[:, r, c * FH:(c + 1) * FH], ident[:])
                last.then_inc(b_t2, 1)
                if ahead2:
                    turn_rows(b + 2, r, (q + 2) % XS, n + (1 if q >= 2 else 0))
                if ahead1:
                    gate_up(b + 1, 1 - r)
                w_slot = pe.value_load(tab[0:1, bass.ds(b + 4 * P, 1)], min_val=0, max_val=WS - 1)
                pe.wait_ge(b_actT, b + 1)
                wait(pe, b_y, b - 1)
                for c in range(2):
                    last = mm(ps[:, 6 + r, 0:D], actT[0:FH, r, c * P:(c + 1) * P],
                              wring[0:FH, bass.ds(w_slot * W_SLOT + WGU + c * D, D)], start=(c == 0), stop=(c == 1))
                last.then_inc(b_dn, 1)

            turn_rows(0, 0, 0, 0)
            turn_rows(1, 1, 1, 0)
            gate_up(0, 0)
            for b in range(XS):
                block_step(b, b % 2, b, 0, None)
            with pe.Fori(1, NB // XS - 1) as n:
                for q in range(XS):
                    block_step(n * XS + q, q % 2, q, n, None)
            for b in range(NB - XS, NB):
                block_step(b, b % 2, b % XS, NB // XS - 1, None, ahead2=b + 2 < NB, ahead1=b + 1 < NB)

        @block.vector
        def _(ve):
            v = nc.vector
            v.memset(reg_q[:, 0:NQ], 0.0).then_inc(vinit, 1)
            v.memset(reg_v[:], 0.0).then_inc(vinit, 1)
            ve.wait_ge(vinit, 2)
            v.memset(v_sb[0:S, :, :, 0, HD:HD + 1], 1.0).then_inc(vinit, 1)
            v.memset(v_sb[S:P, :, :, 1, HD:HD + 1], 1.0).then_inc(vinit, 1)
            ve.wait_ge(vinit, 4)
            con = Steps(ve, c_dve, 0, 20)
            ve.wait_ge(iotas, 3)
            con.then(v.tensor_copy(rel[:], rel_i[:]))
            con.then(v.tensor_scalar(rel[S:P, :], rel[S:P, :], float(-S), None, ALU.add))
            con.then(v.tensor_scalar(mask[:], rel[:], 0.0, None, ALU.is_le))
            ve.wait_ge(l_x, 48)
            con.then(v.tensor_tensor(bias[:], rel[:].unsqueeze(1).to_broadcast([P, H, S]),
                                     sl_sb[:].unsqueeze(2).to_broadcast([P, H, S]), ALU.mult))
            con.then(v.tensor_copy(ei[:], ei_i[:]))
            con.then(v.tensor_scalar(eo[:], ei[:], float(REGION), None, ALU.mult))
            con.then(v.tensor_copy(off[:], eo[:]))
            con.then(v.tensor_copy(bi[:], bi_i[:]))
            N_CON = con.n

            ve.wait_ge(l_wv, 32)
            for i in range(NT):
                ve.wait_ge(v_mm, i + 1)
                for b in range(2):
                    p = slice(b * S, (b + 1) * S)
                    v.tensor_tensor(v_sb[p, i, :, b, 0:HD], ps[p, 4 + i % GROUP, 0:D].rearrange("p (h e) -> p h e", h=H),
                                    bv_sb[p, :].rearrange("p (h e) -> p h e", h=H), ALU.add).then_inc(v_ev, 1)
            v.tensor_tensor(x_sb[:, :, 0:D], x_sb[:, :, 0:D],
                            bo_sb[:].unsqueeze(1).to_broadcast([P, NT, D]), ALU.add).then_inc(relc, 1)
            ve.wait_ge(relc, 1)

            def self_step(i, r):
                if there(i, 1):
                    j, q = i + 1, 1 - r
                    ve.wait_ge(sc_mm, j + 1)
                    wait(ve, pv_mm, j - 1)
                    v.tensor_tensor(prob[:, q, :].rearrange("p (c n) -> p c n", c=KC), ps[:, 2 * q:2 * q + 2, :],
                                    bias[:].rearrange("p (c h) s -> p c (h s)", c=KC), ALU.add).then_inc(biased, 1)
                if there(i):
                    ve.wait_ge(exped, i + 1)
                    pv = prob[:, r, :].rearrange("p (h s) -> p h s", h=H)
                    v.tensor_tensor(pv, pv, mask[:].unsqueeze(1).to_broadcast([P, H, S]), ALU.mult).then_inc(masked, 1)
                    ve.wait_ge(pv_mm, i + 1)
                    wait(ve, ctx_t, i - 1)
                    cp = ps[:, 4 + r, 0:8 * 34].rearrange("p (j b e) -> p j b e", j=8, b=2)
                    v.reciprocal(crec[:, r, :, :], cp[:, :, :, HD:HD + 1].rearrange("p j b e -> p j (b e)")).then_inc(ctx_rec, 1)
                    ve.wait_ge(ctx_rec, i + 1)
                    v.tensor_tensor(ctxn[:, r, :].rearrange("p (b j e) -> p j b e", b=2, j=8), cp[:, :, :, 0:HD],
                                    crec[:, r, :, :].unsqueeze(3).to_broadcast([P, 8, 2, HD]), ALU.mult).then_inc(ctx_n, 1)
                if there(i, -1):
                    j = i - 1
                    ve.wait_ge(o_mm, j + 1)
                    row = x_sb[:, bass.ds(j, 1), 0:D].rearrange("p i d -> p (i d)")
                    v.tensor_tensor(res[:, 0, :], ps[:, 7, 0:D], row, ALU.add).then_inc(o_res, 1)
                    ve.wait_ge(o_res, j + 1)
                    norm_steps(nc, Steps(ve, o_ln, j, LN_N, waited), res[:, 0, :], lstats[:], lmv[:], lrs[:], ltmp[:], ltmpi[:])
                    v.tensor_scalar(row, res[:, 0, :], lmv[:, 0:1], lrs[:, 0:1], ALU.subtract, ALU.mult).then_inc(x1_done, 1)
                    ve.wait_ge(x1_done, j + 1)

            tiles(ve, self_step, 1, 1)

            for q in range(2):
                ve.wait_ge(qd_in[q], 160 * (NT // 2))
            v.memset(reg_qk[:], 0.0).then_inc(xz, 1)

            def softmax_in(i, r, c):
                ve.wait_ge(xs_mm, i * KC + c + 1)
                if not (isinstance(i, int) and i < 2):
                    ve.wait_ge(xp_t, (i - 2) * KC + c + 1)
                wait(ve, xs_sub, i * KC + (c - 1))
                s = ps[:, 2 * c:2 * c + 2, :].rearrange("p a (h t) -> p (a h) t", t=S)
                v.tensor_reduce(xmax[:, c, :], s, AX, ALU.max).then_inc(xs_max, 1)
                ve.wait_ge(xs_max, i * KC + c + 1)
                v.tensor_tensor(xprob[:, r, c, :].rearrange("p (h t) -> p h t", t=S), s,
                                xmax[:, c, :].unsqueeze(2).to_broadcast([P, HC, S]), ALU.subtract).then_inc(xs_sub, 1)

            def evict(i, c):
                ve.wait_ge(xp_t, i * KC + c + 1)
                if not (isinstance(i, int) and i == 0):
                    ve.wait_ge(xv_mm, (i - 1) * KC + c + 1)
                v.tensor_copy(xpT[:, c, 0:N512], ps[:, 4, :]).then_inc(xp_evd, 1)

            def cross_step(i, r):
                if there(i, 1):
                    softmax_in(i + 1, 1 - r, 0)
                if there(i):
                    evict(i, 0)
                if there(i, 1):
                    softmax_in(i + 1, 1 - r, 1)
                if there(i, -1):
                    j = i - 1
                    ve.wait_ge(lg_mm, j + 1)
                    wait(ve, lg_exp, j)
                    v.tensor_copy(logit[:], ps[:, 7, 0:NE]).then_inc(lg_in, 1)
                    ve.wait_ge(lg_in, j + 1)
                    v.tensor_reduce(lmax[:], logit[:], AX, ALU.max).then_inc(lg_steps, 1)
                    ve.wait_ge(lg_steps, j + 1)
                    v.tensor_scalar(lnmax[:], lmax[:], -1.0, None, ALU.mult).then_inc(lg_max, 1)
                if there(i):
                    evict(i, 1)
                if there(i, -1):
                    j = i - 1
                    st = Steps(ve, ra_steps, j, RA_N, waited)
                    ve.wait_ge(lg_exp, j + 1)
                    extra = bass.ds(j, 1)
                    st.then(v.reciprocal(prs[:], psum[:]))
                    st.then(v.tensor_scalar(pr[:], pexp[:], prs[:, 0:1], None, ALU.mult), alone=True)
                    st.then(v.max(top[:], pr[:]), alone=True)
                    st.then(v.max_index(topi[:], top[:], pr[:]))
                    st.then(v.tensor_copy(topf[:], topi[:]))
                    v.tensor_copy(x_sb[:, extra, C_E:C_E + TOPK].rearrange("p i d -> p (i d)"), topf[:, 0:TOPK])
                    st.then(v.tensor_reduce(tsum[:], top[:, 0:TOPK], AX, ALU.add))
                    st.then(v.tensor_scalar(tsum[:], tsum[:], TOP_EPS, None, ALU.add))
                    v.tensor_tensor(hot[:, 1 - r, :, :], ei[:].unsqueeze(1).to_broadcast([P, TOPK, NE]),
                                    topf[:, 0:TOPK].unsqueeze(2).to_broadcast([P, TOPK, NE]), ALU.is_equal)
                    st.then(v.reciprocal(trec[:], tsum[:]))
                    v.tensor_scalar(x_sb[:, extra, C_W:C_W + TOPK].rearrange("p i d -> p (i d)"), top[:, 0:TOPK],
                                    trec[:, 0:1], None, ALU.mult).then_inc(row_in, 1)
                    ve.wait_ge(row_in, j + 1)
                    v.tensor_reduce(sel[:, 1 - r, :], hot[:, 1 - r, :, :].rearrange("p k e -> p e k"), AX,
                                    ALU.add).then_inc(sel_in, 1)
                if there(i):
                    ve.wait_ge(xv_mm, i * KC + KC)
                    st = Steps(ve, xn_steps, i, XN_N, waited)
                    cx = ps[:, 6, 0:XH * (XD + 1)].rearrange("p (h e) -> p h e", h=XH)
                    row = x_sb[:, bass.ds(i, 1), 0:D].rearrange("p i d -> p (i d)")
                    st.then(v.reciprocal(xrec[:], cx[:, :, XD:XD + 1].rearrange("p h e -> p (h e)")))
                    v.tensor_tensor(xtmp.rearrange("p (h e) -> p h e", h=XH), cx[:, :, 0:XD],
                                    xrec[:].unsqueeze(2).to_broadcast([P, XH, XD]), ALU.mult).then_inc(xc_free, 1)
                    ve.wait_ge(xc_free, i + 1)
                    st.then(v.tensor_tensor(res[:, 1, :], xtmp, row, ALU.add))
                    norm_steps(nc, st, res[:, 1, :], lstats[:], lmv[:], lrs[:], ltmp[:], ltmpi[:])
                    if there(i):
                        if isinstance(i, int):
                            ve.wait_ge(x1r_in, min(i + 1, NT))
                        else:
                            ve.wait_ge(x1r_in, i + 1)
                    st.then(v.tensor_scalar(row, res[:, 1, :], lmv[:, 0:1], lrs[:, 0:1], ALU.subtract, ALU.mult))
                    ve.sem_inc(x2_done, 1)
                if there(i, -2):
                    j = i - 2
                    ve.wait_ge(rk_mm, j + 1)
                    st = Steps(ve, rb_steps, j, RB_N)
                    st.then(v.tensor_tensor(pos[:], ps[:, 7, 0:NE], off[:], ALU.add))
                    v.tensor_tensor(off[:], off[:], ps[:, 7, NE:2 * NE], ALU.add).then_inc(rk_free, 1)
                    ve.wait_ge(rk_free, j + 1)
                    st.then(v.tensor_tensor(hpos, hot[:, r, :, :], pos[:].unsqueeze(1).to_broadcast([P, TOPK, NE]), ALU.mult))
                    st.then(v.tensor_reduce(slotf[:], hpos, AX, ALU.add))
                    v.tensor_copy(slot[:, bass.ds(j * 8, TOPK)], slotf[:]).then_inc(slot_in, 1)

            tiles(ve, cross_step, 2, 2)

            t = Steps(ve, c_dve, 0, 200)
            t.n = N_CON
            t.then(v.tensor_copy(offi, off[0:1, :]))
            ve.sem_inc(tb_off, 1)
            t.then(v.tensor_tensor(nblk, off[:], eo[:], ALU.subtract))
            t.then(v.tensor_scalar(nblk, nblk, float(P - 1), None, ALU.add))
            t.then(v.tensor_copy(nblki[:], nblk))
            t.then(v.tensor_scalar(nblki[:], nblki[:], P.bit_length() - 1, None, ALU.arith_shift_right))
            t.then(v.tensor_copy(nblk, nblki[:]))
            t.then(v.tensor_copy(pre[0], nblk))
            cur, d = 0, 1
            while d < NE:
                t.then(v.tensor_copy(pre[1 - cur][:, 0:d], pre[cur][:, 0:d]))
                t.then(v.tensor_tensor(pre[1 - cur][:, d:NE], pre[cur][:, d:NE], pre[cur][:, 0:NE - d], ALU.add))
                cur, d = 1 - cur, 2 * d
            end = pre[cur]
            t.then(v.tensor_copy(endi, end[0:1, :]))
            t.then(v.tensor_tensor(start, end, nblk, ALU.subtract))
            t.then(v.scalar_tensor_tensor(rowof, start, float(-P), eo[:], ALU.mult, ALU.add))
            for c in range(2):
                bcol = bi[:, c:c + 1]
                t.then(v.tensor_scalar(ge_end, end, bcol, None, ALU.is_le))
                t.then(v.tensor_scalar(ge_start, start, bcol, None, ALU.is_le))
                t.then(v.tensor_tensor(inb, ge_start, ge_end, ALU.subtract))
                t.then(v.tensor_reduce(cols[:, c:c + 1], ge_end, AX, ALU.add))
                t.then(v.tensor_scalar(cols[:, c:c + 1], cols[:, c:c + 1], float(NE - 1), None, ALU.min))
                t.then(v.tensor_copy(wsi[:, c:c + 1], cols[:, c:c + 1]))
                t.then(v.tensor_scalar(wsi[:, c:c + 1], wsi[:, c:c + 1], WS - 1, None, ALU.bitwise_and))
                t.then(v.tensor_copy(cols[:, 4 + c:5 + c], wsi[:, c:c + 1]))
                t.then(v.tensor_scalar(cols[:, 6 + c:7 + c], cols[:, c:c + 1], 1.0, None, ALU.add))
                t.then(v.tensor_reduce(ns[:, c:c + 1], inb, AX, ALU.add))
                t.then(v.tensor_tensor(inb, inb, rowof, ALU.mult))
                t.then(v.tensor_reduce(cols[:, 2 + c:3 + c], inb, AX, ALU.add))
                t.then(v.tensor_scalar(w6[:, c:c + 1], bcol, float(P), float(-PAD_ROW), ALU.mult, ALU.add))
                t.then(v.scalar_tensor_tensor(cols[:, 2 + c:3 + c], w6[:, c:c + 1], ns[:, c:c + 1],
                                              cols[:, 2 + c:3 + c], ALU.mult, ALU.add))
                t.then(v.tensor_scalar(cols[:, 2 + c:3 + c], cols[:, 2 + c:3 + c], float(PAD_ROW), None, ALU.add))
            ve.sem_inc(tb_cols, 1)
            ve.wait_ge(tb_t, 1)
            v.tensor_copy(tcol, ps[0:8, 7, 0:P]).then_inc(tb_row, 1)
            v.tensor_copy(tcoli, ps[0:8, 7, 0:P]).then_inc(tb_row, 1)

            with ve.Fori(0, T // N512) as n:
                for f in range(3):
                    m, q = SFC[f][1], f % 2
                    ve.wait_ge(sg_act, n * 3 + (f + 1))
                    v.tensor_tensor(shid[0:m, f, :], sgate[0:m, q, :], ps[0:m, 2 * q + 1, :], ALU.mult).then_inc(sh_in, 1)
                for j in range(GROUP):
                    ve.wait_ge(sd_mm, n * GROUP + (j + 1))
                    v.tensor_tensor(share[:, bass.ds(n * GROUP + j, 1), :].rearrange("p i d -> p (i d)"),
                                    ps[:, 4 + j % 2, 0:D],
                                    x_sb[:, bass.ds(n * GROUP + j, 1), 0:D].rearrange("p i d -> p (i d)"),
                                    ALU.add).then_inc(sd_ev, 1)

            ve.wait_ge(tb_in, 32)

            def copy_rows(b, r):
                ve.wait_ge(b_t1, b + 1)
                wait(ve, b_gu, b - 1)
                v.tensor_copy(xgT[:, r, :], ps[:, r, 0:D]).then_inc(b_xgT, 1)

            def multiply(b, r):
                ve.wait_ge(b_silu, b + 1)
                wait(ve, b_t2, b - 1)
                v.tensor_tensor(act[:, r, :], gate[:, r, :], ps[:, 2 + r, F:2 * F], ALU.mult).then_inc(b_act, 1)

            def block_step(b, r, q, n, ahead2=True, ahead1=True):
                if ahead2:
                    copy_rows(b + 2, r)
                ve.wait_ge(xg_in[q], n * 16 + 16)
                wait(ve, added[r], n * 32 + 16 * (q // 2) - 16)
                v.tensor_copy(toks[:, q:q + 1], xg[:, q, C_TOK:C_TOK + 1].bitcast(I32)).then_inc(b_meta, 1)
                v.scalar_tensor_tensor(w6[:], xg[:, q, C_E:C_E + TOPK], ebc[:, bass.ds(b, 1)],
                                       xg[:, q, C_W:C_W + TOPK], ALU.is_equal, ALU.mult).then_inc(b_meta, 1)
                ve.wait_ge(b_meta, b * 3 + 2)
                v.tensor_reduce(wcol[:, r:r + 1], w6[:], AX, ALU.add).then_inc(b_meta, 1)
                if ahead1:
                    multiply(b + 1, 1 - r)
                ve.wait_ge(b_meta, b * 3 + 3)
                ve.wait_ge(b_dn, b + 2)
                v.tensor_scalar(y_sb[:, q, :], ps[:, 6 + r, 0:D], wcol[:, r:r + 1], None, ALU.mult).then_inc(b_y, 1)

            copy_rows(0, 0)
            copy_rows(1, 1)
            multiply(0, 0)
            for b in range(XS):
                block_step(b, b % 2, b, 0)
            with ve.Fori(1, NB // XS - 1) as n:
                for q in range(XS):
                    block_step(n * XS + q, q % 2, q, n)
            for b in range(NB - XS, NB):
                block_step(b, b % 2, b % XS, NB // XS - 1, ahead2=b + 2 < NB, ahead1=b + 1 < NB)

            def finish(i, r, g):
                st = Steps(ve, f_steps, i, FIN_N, waited)
                ve.wait_ge(ac_in[r], g * 32 + 32)
                if not (isinstance(g, int) and g == 0):
                    ve.wait_ge(stored[r], g * 16)
                st.then(v.tensor_tensor(res[:, 0, :], accl[:, r, 0:D], accl[:, r, D:2 * D], ALU.add))
                st.then(v.tensor_tensor(res[:, 0, :], res[:, 0, :],
                                        share[:, bass.ds(i, 1), :].rearrange("p i d -> p (i d)"), ALU.add))
                norm_steps(nc, st, res[:, 0, :], lstats[:], lmv[:], lrs[:], ltmp[:], ltmpi[:])
                v.tensor_scalar(outr[:, r, :], res[:, 0, :], lmv[:, 0:1], lrs[:, 0:1],
                                ALU.subtract, ALU.mult).then_inc(f_out, 1)
                ve.wait_ge(f_out, i + 1)

            finish(0, 0, 0)
            finish(1, 1, 0)
            with ve.Fori(1, NT // 2) as g:
                for r in range(2):
                    finish(g * 2 + r, r, g)


_INS = ["x", "xT", "ctxT", "ctx", "wqT", "wkT", "wvT", "woT", "bq", "bk", "bv", "bo", "slopes", "gwT", "wgu", "wdn",
        "wsgu", "wsda", "wsdb"]


def kernel(x, ctx_512, L0_attn_Wq, L0_attn_bq, L0_attn_Wk, L0_attn_bk, L0_attn_Wv, L0_attn_bv, L0_attn_Wo, L0_attn_bo,
           L0_attn_alibi_slopes, L0_ffn_gate_w, L0_ffn_w_gate_up, L0_ffn_w_down, L0_ffn_ws_gate_up, L0_ffn_ws_down):
    import numpy as np
    from concourse import bacc
    from concourse.bass_utils import run_bass_kernel_spmd

    tok = np.asarray(x).reshape(T, D)
    c = np.asarray(ctx_512)
    chunks = lambda w: np.asarray(w).T.reshape(KC, P, -1).transpose(1, 0, 2)
    sdown = np.asarray(L0_ffn_ws_down).T
    laid = {
        "x": tok.reshape(NT, P, D).transpose(1, 0, 2),
        "xT": chunks(tok),
        "ctxT": c.reshape(T, -1).T,
        "ctx": c.transpose(1, 0, 2).reshape(S, -1),
        "wqT": chunks(L0_attn_Wq), "wkT": chunks(L0_attn_Wk), "wvT": chunks(L0_attn_Wv),
        "woT": np.asarray(L0_attn_Wo).T.reshape(H // 2, 2, HD, D).transpose(0, 2, 1, 3).reshape(P, 2, D),
        "bq": np.asarray(L0_attn_bq).reshape(KC, P).T, "bk": np.asarray(L0_attn_bk).reshape(KC, P).T,
        "bv": np.asarray(L0_attn_bv).reshape(1, D), "bo": np.asarray(L0_attn_bo).reshape(1, D),
        "slopes": np.asarray(L0_attn_alibi_slopes).reshape(1, H),
        "gwT": chunks(L0_ffn_gate_w),
        "wgu": np.asarray(L0_ffn_w_gate_up).transpose(0, 2, 1).reshape(NE, KC, P, 2 * F).transpose(0, 2, 1, 3).reshape(NE, P, WGU),
        "wdn": np.asarray(L0_ffn_w_down).transpose(0, 2, 1).reshape(NE, 2, FH, D).transpose(0, 2, 1, 3).reshape(NE, FH, WDN),
        "wsgu": chunks(L0_ffn_ws_gate_up),
        "wsda": sdown[0:2 * P].reshape(2, P, D).transpose(1, 0, 2),
        "wsdb": sdown[2 * P:],
    }
    nc = bacc.Bacc("TRN2", target_bir_lowering=False, num_devices=1)
    arrays, args = {}, []
    for name in _INS:
        a = np.ascontiguousarray(laid[name])
        arrays[f"in_{name}"] = a
        args.append(nc.dram_tensor(f"in_{name}", a.shape, mybir.dt.from_np(a.dtype), kind="ExternalInput").ap())
    args.append(nc.dram_tensor("out_dram", (P, NT, D), F32, kind="ExternalOutput").ap())
    decoder(nc, *args)
    r = run_bass_kernel_spmd(nc, [arrays], core_ids=[0])
    return np.ascontiguousarray(r.results[0]["out_dram"].transpose(1, 0, 2)).reshape(B, S, D)
```

```python
from contextlib import ExitStack

import concourse.bass as bass
from concourse import mybir

ALU = mybir.AluOpType
ACT = mybir.ActivationFunctionType
AX = mybir.AxisListType.X
F32 = mybir.dt.float32
I32 = mybir.dt.int32
U32 = mybir.dt.uint32

P = 128
D = 256
KC = D // P
B, S = 32, 64
T = B * S
NT = T // P
H, HD = 16, 16
XH, XD, KV = 32, 8, 8
XG = XH // KV
HC = XH // KC
NE, F, TOPK = 64, 176, 6
FH = F // 2
SF = 352
SFC = ((0, 128), (128, 128), (256, 96))
LN_EPS, TOP_EPS = 1e-5, 1e-20
CAP = 30.0

ROW = 272
C_TOK, C_W, C_E = D, D + 1, D + 1 + TOPK
REGION = T + P
PAD_ROW = NE * REGION
NB = 160
WS = 4
WGU, WDN = KC * 2 * F, 2 * D
W_SLOT = WGU + WDN
XS = 4
GROUP = 4
N512 = 512


def wait(eng, sem, value):
    if isinstance(value, int) and value <= 0:
        return
    eng.wait_ge(sem, value)


class Steps:

    def __init__(self, eng, sem, run, total, spare=None):
        self.eng, self.sem, self.base, self.total, self.n = eng, sem, run * total, total, 0
        self.spare = spare

    def then(self, instruction, alone=False):
        self.n += 1
        assert self.n <= self.total
        instruction.then_inc(self.sem, 1)
        self.eng.wait_ge(self.sem, self.base + self.n)
        if alone:
            self.eng.sem_inc(self.spare, 1)


NEWTON = 3
GUESS = 0x5F3759DF
NEWTON_STEPS = 2 + 2 * NEWTON


def newton_steps(g, steps, mv, rstd, tmp, alone):
    v = tmp[:, 0:1]
    steps.then(g.tensor_scalar(v, mv[:, 1:2], LN_EPS, -8192.0 ** 2, ALU.add, ALU.mult), alone)
    steps.then(g.tensor_scalar(rstd.bitcast(I32), v.bitcast(I32), -0.5, float(GUESS - (1 << 30)), ALU.mult, ALU.add), alone)
    for grown in (1, 2, 16):
        steps.then(g.tensor_scalar(tmp[:, 1:2], rstd, rstd, v, ALU.mult, ALU.mult), alone)
        steps.then(g.tensor_scalar(rstd, tmp[:, 1:2], 3.0 * grown ** 2, rstd, ALU.add, ALU.mult), alone)


def decoder(nc, x, xT, ctxT, ctx, wqT, wkT, wvT, woT, bq, bk, bv, bo, slopes, gwT, wgu, wdn, wsgu, wsda, wsdb, out):
    with ExitStack() as stack:
        def sb(name, shape, dt=F32):
            return stack.enter_context(nc.sbuf_tensor(name, shape, dt))

        def sem(name):
            return stack.enter_context(nc.semaphore(name))

        rows_d = nc.dram_tensor("rows_d", [PAD_ROW + P, ROW], F32, kind="Internal").ap()
        acc_d = [nc.dram_tensor(f"acc{q}_d", [T + P, D], F32, kind="Internal").ap() for q in range(XS)]
        tab_d = nc.dram_tensor("tab_d", [8, P], F32, kind="Internal").ap()
        tabi_d = nc.dram_tensor("tabi_d", [8, P], I32, kind="Internal").ap()

        ps = stack.enter_context(nc.psum_tensor("ps", [P, 8, N512], F32))

        xT_ps, rk_ps, lg_ps = ps[:, 7, 0:D], ps[:, 7, 0:2 * NE], ps[:, 7, 0:NE]

        x_sb = sb("x_sb", [P, NT, ROW])
        xT_sb = sb("xT_sb", [P, KC, T])
        share = xT_sb[:, :, :].rearrange("p c t -> p (c t)").rearrange("p (i d) -> p i d", i=NT)
        reg_qk = sb("reg_qk", [P, 2 * KC * T])
        qT = reg_qk[:, 0:KC * T].rearrange("p (c t) -> p c t", c=KC)
        kT = reg_qk[:, KC * T:].rearrange("p (c t) -> p c t", c=KC)
        xkey = reg_qk[:, :].rearrange("p (r c h t) -> p r c h t", r=2, c=KC, h=HC)
        NV = NT * H * 2 * (HD + 1)
        reg_v = sb("reg_v", [P, NV])
        v_sb = reg_v[:, :].rearrange("p (i h b e) -> p i h b e", i=NT, h=H, b=2)
        XP = HC * S
        xprob = reg_v[:, 0:4 * XP].rearrange("p (r c n) -> p r c n", r=2, c=KC)
        x2T = reg_v[:, 4 * XP:4 * XP + KC * T].rearrange("p (c t) -> p c t", c=KC)
        NQ = 2 * KC * 8 * P
        reg_q = sb("reg_q", [P, NQ + 2 * KC * P])
        qdiag = reg_q[:, 0:NQ].rearrange("p (r c h t) -> p r c h t", r=2, c=KC, h=8)
        kTr = reg_q[:, NQ:].rearrange("p (r c t) -> p r c t", r=2, c=KC)
        at = [0]

        def carve(n):
            at[0] += n
            return reg_q[:, at[0] - n:at[0]]

        xg = carve(XS * ROW).rearrange("p (r n) -> p r n", r=XS)
        xgT = carve(2 * D).rearrange("p (r n) -> p r n", r=2)
        gate = carve(2 * F).rearrange("p (r n) -> p r n", r=2)
        act = carve(2 * F).rearrange("p (r n) -> p r n", r=2)
        actT = carve(2 * 2 * P).rearrange("p (r n) -> p r n", r=2)
        y_sb = carve(XS * D).rearrange("p (r n) -> p r n", r=XS)
        wring = sb("wring", [P, WS * W_SLOT])
        ctx_st = wring[:, 0:B * S]
        prob = sb("prob", [P, 2, H * S])
        bias = sb("bias", [P, H, S])
        cbuf = sb("cbuf", [P, 4 * D])
        ctxn, ctxnT = (cbuf[:, q * 2 * D:(q + 1) * 2 * D].rearrange("p (r n) -> p r n", r=2) for q in range(2))
        NXV = 2 * KV * 2 * (XD + 1)
        xvr = cbuf[:, 0:2 * NXV].rearrange("p (r b k n) -> p r b k n", r=2, b=2, k=KV)
        x1r = sb("x1r", [P, 2, D])
        x1T = sb("x1T", [P, 2, KC, P])
        xpT = prob
        xval = sb("xval", [P, B, KV, 2, XD + 1])
        NVR = 2 * H * (HD + 1)
        vbuf = sb("vbuf", [P, 2 * NVR])
        vr = vbuf[:, :].rearrange("p (r h n) -> p r h n", r=2, h=H)
        x2r = vbuf[:, 0:2 * D].rearrange("p (r n) -> p r n", r=2)
        x2Tr = vbuf[:, 2 * D:4 * D].rearrange("p (r c t) -> p r c t", r=2, c=KC)
        res = sb("res", [P, 2, D])
        wq_sb, wk_sb, wv_sb, wo_sb = (sb(n, [P, KC, D]) for n in ("wq_sb", "wk_sb", "wv_sb", "wo_sb"))
        bq_sb, bk_sb = sb("bq_sb", [P, KC]), sb("bk_sb", [P, KC])
        bv_sb, bo_sb = sb("bv_sb", [P, D]), sb("bo_sb", [P, D])
        sl_sb = sb("sl_sb", [P, H])
        gw_sb = sb("gw_sb", [P, KC, NE])
        wsgu_sb = sb("wsgu_sb", [P, KC, 2 * SF])
        wsd_sb = sb("wsd_sb", [P, 3, D])
        sgate = prob[:, 0, 0:2 * N512].rearrange("p (r n) -> p r n", r=2)
        shid = reg_v[:, 0:3 * N512].rearrange("p (f n) -> p f n", f=3)
        ident, ones, tri = sb("ident", [P, P]), sb("ones", [P, P]), sb("tri", [P, P])
        rel_i, rel, mask = sb("rel_i", [P, S], I32), sb("rel", [P, S]), sb("mask", [P, S])
        ei_i, ei, eo = sb("ei_i", [P, NE], I32), sb("ei", [P, NE]), sb("eo", [P, NE])
        bi_i, bi = sb("bi_i", [P, 2], I32), sb("bi", [P, 2])
        pad = sb("pad", [P, ROW])
        crec = sb("crec", [P, 2, 8, 2])
        xmax = sb("xmax", [P, KC, HC])
        xrec = sb("xrec", [P, XH])
        lstats, lmv, lrs = sb("lstats", [P, 6]), sb("lmv", [P, 2]), sb("lrs", [P, 1])
        ltmp, ltmpi, nblki, wsi = sb("ltmp", [P, 2]), sb("ltmpi", [P, 1], I32), sb("nblki", [P, NE], I32), sb("wsi", [P, 2], I32)
        logit, lmax, lnmax = sb("logit", [P, NE]), sb("lmax", [P, 1]), sb("lnmax", [P, 1])
        pexp, psum, prs, pr = sb("pexp", [P, NE]), sb("psum", [P, 1]), sb("prs", [P, 1]), sb("pr", [P, NE])
        top, topi, topf = sb("top", [P, 8]), sb("topi", [P, 8], U32), sb("topf", [P, 8])
        tsum, trec = sb("tsum", [P, 1]), sb("trec", [P, 1])
        hot = reg_q[:, 0:2 * TOPK * NE].rearrange("p (r k e) -> p r k e", r=2, k=TOPK)
        hpos = reg_q[:, 2 * TOPK * NE:3 * TOPK * NE].rearrange("p (k e) -> p k e", k=TOPK)
        xtmp = reg_q[:, 3 * TOPK * NE:3 * TOPK * NE + D]
        sel, pos, slotf = sb("sel", [P, 2, NE]), sb("pos", [P, NE]), sb("slotf", [P, TOPK])
        slot = sb("slot", [P, NT * 8], I32)
        off = sb("off", [P, NE])
        at_tables = 3 * TOPK * NE + D
        nblk, pre0, pre1, start, rowof, ge_end, ge_start, inb = (
            reg_q[:, at_tables + n * NE:at_tables + (n + 1) * NE] for n in range(8))
        pre = [pre0, pre1]
        cols, ns = sb("cols", [P, 8]), sb("ns", [P, 2])
        tcol, tcoli = x1r[0:8, 0, 0:P], x1r[0:8, 0, P:2 * P].bitcast(I32)
        tab = bias[0:1, :, :].rearrange("p h s -> p (h s)").bitcast(I32)
        offi, endi = (x1r[0:1, 1, n * NE:(n + 1) * NE].bitcast(I32) for n in range(2))
        ebc = carve(2 * P)
        wcol, w6 = sb("wcol", [P, 2]), sb("w6", [P, TOPK])
        fmv, fvar, ftmp, ftmpi = sb("fmv", [P, XS, 2]), sb("fvar", [P, XS]), sb("ftmp", [P, XS]), sb("ftmpi", [P, XS], I32)
        frsl, frs, fnm = sb("frsl", [P, XS]), sb("frs", [P, NT]), sb("fnm", [P, NT])
        toks = sb("toks", [P, XS], I32)
        accl = wring[:, 0:XS * XS * D].rearrange("p (q a d) -> p q a d", q=XS, a=XS)
        outr = prob[:, 0, 0:XS * D].rearrange("p (q d) -> p q d", q=XS)
        f2 = prob[:, 1, 0:XS * D].rearrange("p (q d) -> p q d", q=XS)

        l_x, l_xT, l_wqk, l_wv, l_wo, l_ctx, l_late = (sem(n) for n in ("l_x", "l_xT", "l_wqk", "l_wv", "l_wo", "l_ctx", "l_late"))
        const, vinit, xinit, relc, dinit = sem("const"), sem("vinit"), sem("xinit"), sem("relc"), sem("dinit")
        c_pool, row_in, waited, pool_waited = sem("c_pool"), sem("row_in"), sem("waited"), sem("pool_waited")
        iotas = sem("iotas")
        c_dve = sem("c_dve")
        qk_mm, qk_ev, v_mm, v_ev = sem("qk_mm"), sem("qk_ev"), sem("v_mm"), sem("v_ev")
        qd_in, vr_in = [sem("qd_in0"), sem("qd_in1")], [sem("vr_in0"), sem("vr_in1")]
        sc_mm, biased, tanhed, exped, masked = sem("sc_mm"), sem("biased"), sem("tanhed"), sem("exped"), sem("masked")
        pv_mm, ctx_rec, ctx_n, ctx_t, ctx_ev, o_mm, o_res, x1_done = (
            sem(n) for n in ("pv_mm", "ctx_rec", "ctx_n", "ctx_t", "ctx_ev", "o_mm", "o_res", "x1_done"))
        ln_part, ln_stat, ln_steps, ln_rs = (sem(n) for n in ("ln_part", "ln_stat", "ln_steps", "ln_rs"))
        kr_in = [sem("kr_in0"), sem("kr_in1")]
        xz, xk_in, xvr_in = sem("xz"), [sem("xk_in0"), sem("xk_in1")], [sem("xvr_in0"), sem("xvr_in1")]
        x1r_in, x1_t, x1_ev = sem("x1r_in"), sem("x1_t"), sem("x1_ev")
        xs_mm, xs_max, xs_sub, xs_exp, xp_t, xp_ev = (
            sem(n) for n in ("xs_mm", "xs_max", "xs_sub", "xs_exp", "xp_t", "xp_ev"))
        xv_mm, xn_steps, xc_free, x2_done, x2r_out, x2_t, x2_ev, x2T_in = (
            sem(n) for n in ("xv_mm", "xn_steps", "xc_free", "x2_done", "x2r_out", "x2_t", "x2_ev", "x2T_in"))
        lg_mm, lg_in, lg_steps, lg_max, lg_exp, ra_steps, sel_in = (
            sem(n) for n in ("lg_mm", "lg_in", "lg_steps", "lg_max", "lg_exp", "ra_steps", "sel_in"))
        rk_mm, rb_steps, rk_free, slot_in, scat = sem("rk_mm"), sem("rb_steps"), sem("rk_free"), sem("slot_in"), sem("scat")
        tb_cols, tb_t, tb_row, tb_d, tb_in, tb_off, pads, pool_pads = (
            sem(n) for n in ("tb_cols", "tb_t", "tb_row", "tb_d", "tb_in", "tb_off", "pads", "pool_pads"))
        sg_mm, sg_act, sh_in, sd_mm, sd_ev = sem("sg_mm"), sem("sg_act"), sem("sh_in"), sem("sd_mm"), sem("sd_ev")
        w_in, w_ready = [sem(f"w_in{q}") for q in range(WS)], sem("w_ready")
        xg_in = [sem(f"xg_in{q}") for q in range(XS)]
        b_t1, b_xgT, b_gu, b_silu, b_act, b_t2, b_actT, b_dn, b_y, b_meta, b_w = (
            sem(n) for n in ("b_t1", "b_xgT", "b_gu", "b_silu", "b_act", "b_t2", "b_actT", "b_dn", "b_y", "b_meta", "b_w"))
        added = [sem(f"added{q}") for q in range(XS)]
        ac_in, stored = ([sem(f"{n}{q}") for q in range(XS)] for n in ("ac_in", "stored"))
        f_part, f_sum, f_steps, f_aggr, f_newton, f_stat, f_out = (
            sem(n) for n in ("f_part", "f_sum", "f_steps", "f_aggr", "f_newton", "f_stat", "f_out"))

        N_PADS = XS * (T + P) // P + 1 + NE // 2
        RA_N, RB_N, XN_N = 8, 3, 3

        block = stack.enter_context(nc.Block())

        def tiles(eng, step, ahead, behind):
            lo = 4
            hi = NT - 2 * ((ahead + 1) // 2)
            for i in range(-ahead, lo):
                step(i, i % 2)
            with eng.Fori(lo // 2, hi // 2) as g:
                for r in range(2):
                    step(g * 2 + r, r)
            for i in range(hi, NT + behind):
                step(i, i % 2)

        def there(i, shift=0):
            return not isinstance(i, int) or 0 <= i + shift < NT

        def half(i, r):
            return (i - r) // 2 if isinstance(i, int) else None

        @block.sync
        def _(sp):
            sp.dma_start(wq_sb[:], wqT).then_inc(l_wqk, 16)
            sp.dma_start(wk_sb[:], wkT).then_inc(l_wqk, 16)
            sp.dma_start(bq_sb[:], bq).then_inc(l_wqk, 16)
            sp.dma_start(bk_sb[:], bk).then_inc(l_wqk, 16)
            sp.dma_start(xT_sb[:], xT).then_inc(l_xT, 16)
            sp.dma_start(wv_sb[:], wvT).then_inc(l_wv, 16)
            sp.dma_start(bv_sb[:], bv.to_broadcast([P, D])).then_inc(l_wv, 16)
            sp.dma_start(sl_sb[:], slopes.to_broadcast([P, H])).then_inc(l_x, 16)
            sp.dma_start(x_sb[:, :, 0:D], x).then_inc(l_x, 16)
            sp.dma_start(bo_sb[:], bo.to_broadcast([P, D])).then_inc(l_x, 16)
            sp.dma_start(wo_sb[:], woT).then_inc(l_wo, 16)
            for q in range(2):
                sp.dma_start(ctx_st[q * S:(q + 1) * S, :], ctx).then_inc(l_ctx, 16)
            sp.dma_start(gw_sb[:], gwT).then_inc(l_late, 16)
            sp.dma_start(wsgu_sb[:], wsgu).then_inc(l_late, 16)
            sp.dma_start(wsd_sb[:, 0:2, :], wsda).then_inc(l_late, 16)
            sp.dma_start(wsd_sb[0:SFC[2][1], 2, :], wsdb).then_inc(l_late, 16)
            sp.wait_ge(dinit, 3)
            for q in range(XS):
                for j in range((T + P) // P):
                    sp.dma_start(acc_d[q][j * P:(j + 1) * P, :], pad[:, 0:D]).then_inc(pads, 16)
            sp.dma_start(rows_d[PAD_ROW:PAD_ROW + P, :], pad[:]).then_inc(pads, 16)

            sp.wait_ge(v_ev, 2 * NT)
            sp.wait_ge(qk_ev, 4 * KC * 2)
            sp.wait_ge(vinit, 4)

            def q_tile(i, r, n):
                wait(sp, sc_mm, i - 1)
                for h in range(8):
                    p = slice(HD * h, HD * (h + 1))
                    sp.dma_start(qdiag[p, r, :, h, :], qT[p, :, bass.ds(i * P, P)]).then_inc(qd_in[r], 16)

            for i in range(2):
                q_tile(i, i, 0)
            with sp.Fori(1, NT // 2) as g:
                for r in range(2):
                    q_tile(g * 2 + r, r, g)

            key_rows = ctxT.rearrange("(c k d) t -> k d c t", c=KC, d=XD)
            sp.wait_ge(xz, 1)
            sp.wait_ge(xinit, 4)

            def key_tile(i, r):
                if not (isinstance(i, int) and i < 2):
                    sp.wait_ge(xs_mm, (i - 1) * KC)
                for h in range(HC):
                    sp.dma_start(xkey[XD * h:XD * (h + 1), r, :, h, :],
                                 key_rows[h // XG, :, :, bass.ds(i * P, P)]).then_inc(xk_in[r], 16)

            for i in range(2):
                key_tile(i, i)
            with sp.Fori(1, NT // 2) as g:
                for r in range(2):
                    key_tile(g * 2 + r, r)

            def weights(e, q):
                w = wring[:, q * W_SLOT:(q + 1) * W_SLOT]
                sp.dma_start(w[:, 0:WGU], wgu[bass.ds(e, 1), :, :].rearrange("e p n -> (e p) n")).then_inc(w_in[q], 16)
                sp.dma_start(w[0:FH, WGU:], wdn[bass.ds(e, 1), :, :].rearrange("e p n -> (e p) n")).then_inc(w_in[q], 16)

            sp.wait_ge(xinit, 4)
            for e in range(WS):
                weights(e, e)
            sp.wait_ge(tb_off, 1)
            with sp.Fori(0, NE // 2) as e:
                at_row = sp.value_load(offi[0:1, bass.ds(e, 1)], min_val=0, max_val=PAD_ROW)
                sp.dma_start(rows_d[bass.ds(at_row, P), :], pad[:]).then_inc(pads, 16)
            sp.wait_ge(tb_row, 2)
            sp.dma_start(tabi_d, tcoli).then_inc(tb_d, 16)
            sp.dma_start(tab_d, tcol).then_inc(tb_d, 16)
            sp.wait_ge(tb_d, 32)
            sp.dma_start(tab, tabi_d.rearrange("(o a) n -> o (a n)", o=1)).then_inc(tb_in, 16)
            sp.dma_start(ebc, tab_d[0:2, :].rearrange("(o a) n -> o (a n)", o=1).to_broadcast([P, 2 * P])).then_inc(tb_in, 16)
            for e in range(2):
                sp.wait_ge(w_in[e], 32)
                sp.sem_inc(w_ready, 1)
            with sp.Fori(1, NE // WS) as g:
                for q in range(WS):
                    done = sp.value_load(endi[0:1, bass.ds((g - 1) * WS + q, 1)], min_val=0, max_val=NB)
                    sp.wait_ge(b_dn, done + 1)
                    weights(g * WS + q, q)
                    u = (q + 2) % WS
                    sp.wait_ge(w_in[u], g * 32 if q < 2 else (g + 1) * 32)
                    sp.sem_inc(w_ready, 1)
            for q in range(2, WS):
                sp.wait_ge(w_in[q], 32 * (NE // WS))
                sp.sem_inc(w_ready, 1)

            for q in range(XS):
                sp.wait_ge(added[q], 16 * (NB // XS))

            def acc_tile(i, q):
                wait(sp, f_sum, i - XS + 1)
                for a in range(XS):
                    sp.dma_start(accl[:, q, a, :], acc_d[a][bass.ds(i * P, P), :]).then_inc(ac_in[q], 16)

            for i in range(XS):
                acc_tile(i, i)
            with sp.Fori(1, NT // XS) as g:
                for q in range(XS):
                    acc_tile(g * XS + q, q)

        @block.gpsimd
        def _(pool):
            g = nc.gpsimd
            g.memset(ident[:], 0.0).then_inc(c_pool, 1)
            g.memset(tri[:], 1.0).then_inc(c_pool, 1)
            g.memset(ones[:], 1.0).then_inc(const, 1)
            pool.wait_ge(c_pool, 2)
            g.affine_select(out=ident[:], in_=ident[:], compare_op=ALU.not_equal, fill=1.0, base=0,
                            pattern=[[-1, P]], channel_multiplier=1).then_inc(const, 1)
            g.affine_select(out=tri[:], in_=tri[:], compare_op=ALU.is_gt, fill=0.0, base=0,
                            pattern=[[1, P]], channel_multiplier=-1).then_inc(const, 1)
            g.iota(rel_i[:], pattern=[[-1, S]], base=0, channel_multiplier=1).then_inc(iotas, 1)
            g.iota(ei_i[:], pattern=[[1, NE]], base=0, channel_multiplier=0).then_inc(iotas, 1)
            g.iota(bi_i[:], pattern=[[P, 2]], base=0, channel_multiplier=1).then_inc(iotas, 1)
            g.iota(pad[:, C_TOK:C_TOK + 1].bitcast(I32), pattern=[[0, 1]], base=T, channel_multiplier=1).then_inc(c_pool, 1)
            g.memset(pad[:, 0:D], 0.0).then_inc(dinit, 1)
            g.memset(pad[:, C_W:ROW], -1.0).then_inc(dinit, 1)
            pool.wait_ge(c_pool, 3)
            pool.sem_inc(dinit, 1)
            g.iota(x_sb[:, :, C_TOK:C_TOK + 1].bitcast(I32), pattern=[[P, NT], [0, 1]], base=0,
                   channel_multiplier=1).then_inc(xinit, 1)
            g.memset(x_sb[:, :, C_E + TOPK:ROW], 0.0).then_inc(xinit, 1)
            g.memset(xval[:], 0.0).then_inc(c_pool, 1)
            pool.wait_ge(c_pool, 4)
            pool.wait_ge(l_ctx, 32)
            for q in range(2):
                p = slice(q * S, (q + 1) * S)
                g.memset(xval[p, :, :, q, XD:XD + 1], 1.0).then_inc(c_pool, 1)
                g.tensor_copy(xval[p, :, :, q, 0:XD],
                              ctx_st[p, :].rearrange("p (b k d) -> p b k d", b=B, k=KV)).then_inc(xinit, 1)
                pool.wait_ge(c_pool, 5 + q)
                pool.wait_ge(xinit, 3 + q)

            pool.wait_ge(v_ev, 2 * NT)
            pool.wait_ge(qk_ev, 4 * KC * 2)

            def key_tile(i, r):
                if not (isinstance(i, int) and i < 2):
                    pool.wait_ge(sc_mm, i - 1)
                    pool.sem_inc(pool_waited, 1)
                pool.dma_start(kTr[:, r, :, :], kT[:, :, bass.ds(i * P, P)]).then_inc(kr_in[r], 16)

            def value_tile(i, r):
                if not (isinstance(i, int) and i < 2):
                    pool.wait_ge(pv_mm, i - 1)
                    pool.sem_inc(pool_waited, 1)
                pool.dma_start(vr[:, r, :, :], v_sb[:, bass.ds(i, 1), :, :, :].rearrange("p i h b e -> p (i h) (b e)")).then_inc(vr_in[r], 16)

            def norm(n):
                pool.wait_ge(ln_stat, n + 1)
                alone = not isinstance(n, int)
                if alone:
                    pool.sem_inc(pool_waited, 1)
                newton_steps(g, Steps(pool, ln_steps, n, NEWTON_STEPS, pool_waited), lmv[:], lrs[:], ltmp[:], alone)
                pool.sem_inc(ln_rs, 1)

            def self_step(i, r):
                if there(i, 2):
                    key_tile(i + 2, r)
                if there(i, -1):
                    norm(i - 1)
                if there(i, 2):
                    value_tile(i + 2, r)

            tiles(pool, self_step, 2, 1)

            def cross_values(i):
                if i >= 2:
                    pool.wait_ge(xv_mm, (i - 1) * KC)
                pool.dma_start(xvr[:, i % 2, :, :, :].rearrange("p b k n -> p b (k n)"),
                               xval[:, 2 * i:2 * i + 2, :, :, :].rearrange("p b k q e -> p b (k q e)")).then_inc(xvr_in[i % 2], 16)

            def step(i):
                if there(i, -1):
                    j = i - 1
                    pool.wait_ge(x2_done, j + 1)
                    g.tensor_copy(x_sb[:, j, 0:D], x2r[:, j % 2, :]).then_inc(x2r_out, 1)
                if there(i, 3):
                    j = i + 3
                    pool.wait_ge(x1_done, j + 1)
                    wait(pool, x1_t, j - 1)
                    g.tensor_copy(x1r[:, j % 2, :], x_sb[:, j, 0:D]).then_inc(x1r_in, 1)
                if there(i, -1):
                    j = i - 1
                    pool.wait_ge(x2_ev, j + 1)
                    g.tensor_copy(x2T[:, :, j * P:(j + 1) * P], x2Tr[:, j % 2, :, :]).then_inc(x2T_in, 1)
                if there(i, -2):
                    j = i - 2
                    pool.wait_ge(slot_in, j + 1)
                    pool.wait_ge(x2r_out, j + 1)
                    for k in range(TOPK):
                        g.indirect_dma_start(
                            out=rows_d[:, :],
                            out_offset=bass.IndirectOffsetOnAxis(ap=slot[:, 8 * j + k:8 * j + k + 1], axis=0),
                            in_=x_sb[:, j, :], in_offset=None).then_inc(scat, 16)
                if there(i):
                    norm(NT + i)
                if there(i, 2):
                    cross_values(i + 2)

            pool.wait_ge(o_mm, NT)
            for i in range(-3, NT + 2):
                step(i)

            pool.wait_ge(tb_off, 1)
            with pool.Fori(NE // 2, NE) as e:
                at_row = pool.value_load(offi[0:1, bass.ds(e, 1)], min_val=0, max_val=PAD_ROW)
                pool.dma_start(rows_d[bass.ds(at_row, P), :], pad[:]).then_inc(pool_pads, 16)

            pool.wait_ge(pads, 16 * N_PADS)

            def add_block(n, q):
                pool.wait_ge(b_y, n * XS + q + 1)
                wait(pool, added[q], n * 16)
                pool.sem_inc(pool_waited, 1)
                g.indirect_dma_start(
                    out=acc_d[q][:, :], out_offset=bass.IndirectOffsetOnAxis(ap=toks[:, q:q + 1], axis=0),
                    in_=y_sb[:, q, :], in_offset=None, compute_op=ALU.add).then_inc(added[q], 16)

            for q in range(XS):
                add_block(0, q)
            with pool.Fori(1, NB // XS) as n:
                for q in range(XS):
                    add_block(n, q)

        @block.scalar
        def _(sc):
            a = nc.scalar
            sc.wait_ge(l_wqk, 64)
            for n in range(T // N512):
                for m in range(2 * KC):
                    dst, b = ((qT, bq_sb), (kT, bk_sb))[m // KC]
                    c = m % KC
                    sc.wait_ge(qk_mm, 4 * n + m + 1)
                    a.activation(dst[:, c, n * N512:(n + 1) * N512], ps[:, m, :], ACT.Identity,
                                 bias=b[:, c:c + 1]).then_inc(qk_ev, 1)

            def self_step(i, r):
                if there(i, -1):
                    j = i - 1
                    sc.wait_ge(ctx_t, j + 1)
                    wait(sc, o_mm, j - 1)
                    a.activation(ctxnT[:, 1 - r, :].rearrange("p (q b s) -> p b q s", q=2, b=2),
                                 ps[:, 6, 0:D].rearrange("p (b q s) -> p b q s", b=2, q=2), ACT.Copy).then_inc(ctx_ev, 1)
                if there(i, 1):
                    j = i + 1
                    sc.wait_ge(biased, j + 1)
                    a.activation(prob[:, 1 - r, :], prob[:, 1 - r, :], ACT.Tanh,
                                 scale=1.0 / (CAP * HD ** 0.5)).then_inc(tanhed, 1)
                    sc.wait_ge(tanhed, j + 1)
                    a.activation(prob[:, 1 - r, :], prob[:, 1 - r, :], ACT.Exp, scale=CAP).then_inc(exped, 1)

            tiles(sc, self_step, 1, 1)

            def cross_exp(i, r, c):
                sc.wait_ge(xs_sub, i * KC + c + 1)
                a.activation(xprob[:, r, c, :], xprob[:, r, c, :], ACT.Exp, scale=XD ** -0.5).then_inc(xs_exp, 1)

            def cross_evict(i, c):
                sc.wait_ge(xp_t, i * KC + c + 1)
                if not (isinstance(i, int) and i == 0):
                    sc.wait_ge(xv_mm, (i - 1) * KC + c + 1)
                a.activation(xpT[:, c, :].rearrange("p (a n) -> p a n", a=2), ps[:, 4:6, :], ACT.Copy).then_inc(xp_ev, 1)

            def cross_step(i, r):
                if there(i, 2):
                    j = i + 2
                    sc.wait_ge(x1_t, j + 1)
                    if not (isinstance(i, int) and i < 0):
                        sc.wait_ge(xs_mm, j * KC - KC)
                    a.activation(x1T[:, r, :, :].rearrange("p c t -> p (c t)"), xT_ps, ACT.Copy).then_inc(x1_ev, 1)
                if there(i):
                    cross_evict(i, 0)
                if there(i, 1):
                    cross_exp(i + 1, 1 - r, 0)
                if there(i, -1):
                    j = i - 1
                    sc.wait_ge(x2_t, j + 1)
                    wait(sc, x2T_in, j - 1)
                    wait(sc, lg_mm, j - 1)
                    a.activation(x2Tr[:, 1 - r, :, :].rearrange("p c t -> p (c t)"), xT_ps, ACT.Copy).then_inc(x2_ev, 1)
                if there(i, 1):
                    cross_exp(i + 1, 1 - r, 1)
                if there(i):
                    cross_evict(i, 1)
                if there(i, -1):
                    j = i - 1
                    sc.wait_ge(lg_max, j + 1)
                    a.activation(pexp[:], logit[:], ACT.Exp, bias=lnmax[:, 0:1], accum_out=psum[:]).then_inc(lg_exp, 1)

            tiles(sc, cross_step, 2, 2)

            with sc.Fori(0, T // N512) as n:
                for f in range(3):
                    m, q = SFC[f][1], f % 2
                    sc.wait_ge(sg_mm, n * 3 + (f + 1))
                    if f >= 2:
                        sc.wait_ge(sh_in, n * 3 + (f - 1))
                    a.activation(sgate[0:m, q, :], ps[0:m, 2 * q, :], ACT.Silu).then_inc(sg_act, 1)

            sc.wait_ge(tb_in, 32)
            sc.wait_ge(scat, 16 * TOPK * NT)
            sc.wait_ge(pads, 16 * N_PADS)
            sc.wait_ge(pool_pads, 16 * (NE // 2))
            sc.wait_ge(sc_mm, NT)

            def rows_in(b, q):
                at_row = sc.value_load(tab[0:1, bass.ds(b + 2 * P, 1)], min_val=0, max_val=PAD_ROW)
                if not (isinstance(b, int) and b < XS):
                    sc.wait_ge(b_t1, b - XS + 1)
                    sc.wait_ge(b_meta, (b - XS) * 3 + 3)
                sc.dma_start(xg[:, q, :], rows_d[bass.ds(at_row, P), :]).then_inc(xg_in[q], 16)

            for b in range(XS):
                rows_in(b, b)

            def block_step(b, r, q, first=False, more=True, rows=True):
                if not first:
                    sc.wait_ge(b_t2, b + 1)
                    wait(sc, b_dn, b)
                    a.activation(actT[0:FH, r, :], ps[0:FH, 4 + r, 0:2 * P], ACT.Copy).then_inc(b_actT, 1)
                if more:
                    sc.wait_ge(b_gu, b + 2)
                    wait(sc, b_act, b)
                    a.activation(gate[:, 1 - r, :], ps[:, 2 + (1 - r), 0:F], ACT.Silu).then_inc(b_silu, 1)
                if rows and not first:
                    rows_in(b + XS, q)

            block_step(-1, 1, 3, first=True)
            for b in range(XS):
                block_step(b, b % 2, b)
            with sc.Fori(1, NB // XS - 1) as n:
                for q in range(XS):
                    block_step(n * XS + q, q % 2, q)
            for b in range(NB - XS, NB):
                block_step(b, b % 2, b % XS, more=b + 1 < NB, rows=False)

            def out_tile(g, q):
                i = g * XS + q
                sc.wait_ge(f_stat, g * 2 + 2)
                wait(sc, stored[q], g * 16)
                a.activation(outr[:, q, :], share[:, bass.ds(i, 1), :].rearrange("p i d -> p (i d)"), ACT.Identity,
                             bias=fnm[:, bass.ds(i, 1)], scale=frs[:, bass.ds(i, 1)]).then_inc(f_out, 1)
                sc.wait_ge(f_out, i + 1)
                sc.dma_start(out[:, bass.ds(i, 1), :].rearrange("p i d -> p (i d)"), outr[:, q, :]).then_inc(stored[q], 16)

            for q in range(XS):
                out_tile(0, q)
            with sc.Fori(1, NT // XS) as g:
                for q in range(XS):
                    out_tile(g, q)
            for q in range(XS):
                sc.wait_ge(stored[q], 16 * (NT // XS))

        @block.tensor
        def _(pe):
            mm = pe.matmul
            pe.wait_ge(l_wqk, 64)
            pe.wait_ge(l_xT, 16)
            for n in range(T // N512):
                for m in range(2 * KC):
                    w, c = (wq_sb, wk_sb)[m // KC], m % KC
                    if n:
                        pe.wait_ge(qk_ev, 4 * (n - 1) + m + 1)
                    for k in range(KC):
                        last = mm(ps[:, m, :], w[:, k, c * P:(c + 1) * P], xT_sb[:, k, n * N512:(n + 1) * N512],
                                  start=(k == 0), stop=(k == KC - 1))
                    last.then_inc(qk_mm, 1)
                if n == 0:
                    pe.wait_ge(l_wv, 32)
                for j in range(GROUP):
                    i = n * GROUP + j
                    if n:
                        pe.wait_ge(v_ev, 2 * (i - GROUP) + 2)
                    for k in range(KC):
                        last = mm(ps[:, 4 + j, 0:D], xT_sb[:, k, i * P:(i + 1) * P], wv_sb[:, k, :],
                                  start=(k == 0), stop=(k == KC - 1))
                    last.then_inc(v_mm, 1)
            pe.wait_ge(const, 3)
            pe.wait_ge(l_wo, 16)
            pe.wait_ge(qk_ev, 16)
            pe.wait_ge(v_ev, 2 * NT)

            def self_step(i, r):
                if there(i, -1):
                    j, q = i - 1, 1 - r
                    pe.wait_ge(ctx_n, j + 1)
                    wait(pe, ctx_ev, j)
                    for b in range(2):
                        last = pe.transpose(ps[:, 6, b * P:(b + 1) * P], ctxn[:, q, b * P:(b + 1) * P], ident[:])
                    last.then_inc(ctx_t, 1)
                if there(i, 1):
                    j, q = i + 1, 1 - r
                    pe.wait_ge(qd_in[q], ((j - q) // 2 + 1) * 128 if isinstance(j, int) else (j - q) * 64 + 128)
                    pe.wait_ge(kr_in[q], ((j - q) // 2 + 1) * 16 if isinstance(j, int) else (j - q) * 8 + 16)
                    wait(pe, biased, j - 1)
                    for c in range(KC):
                        for b in range(2):
                            t = slice(b * S, (b + 1) * S)
                            last = mm(ps[t, 2 * q + c, :], kTr[:, q, c, t], qdiag[:, q, c, :, t], start=True, stop=True)
                    last.then_inc(sc_mm, 1)
                if there(i, -1):
                    j, q = i - 1, 1 - r
                    pe.wait_ge(ctx_ev, j + 1)
                    wait(pe, o_res, j)
                    for q2 in range(2):
                        last = mm(ps[:, 7, 0:D], ctxnT[:, q, q2 * P:(q2 + 1) * P], wo_sb[:, q2, :],
                                  start=(q2 == 0), stop=(q2 == 1))
                    last.then_inc(o_mm, 1)
                if there(i):
                    pe.wait_ge(vr_in[r], ((i - r) // 2 + 1) * 16 if isinstance(i, int) else (i - r) * 8 + 16)
                    pe.wait_ge(masked, i + 1)
                    wait(pe, ctx_n, i - 1)
                    for h in range(H):
                        last = mm(ps[(h % 2) * S:(h % 2 + 1) * S, 4 + r, (h // 2) * 34:(h // 2 + 1) * 34],
                                  prob[:, r, h * S:(h + 1) * S],
                                  vr[:, r, h, :],
                                  start=True, stop=True)
                    last.then_inc(pv_mm, 1)

            tiles(pe, self_step, 1, 1)
            pe.wait_ge(o_res, NT)
            pe.wait_ge(xinit, 4)
            pe.wait_ge(l_late, 64)

            def scores(i, r, c):
                if c == 0:
                    pe.wait_ge(xk_in[r], ((i - r) // 2 + 1) * 256 if isinstance(i, int) else (i - r) * 128 + 256)
                    pe.wait_ge(x1_ev, i + 1)
                if not (isinstance(i, int) and i == 0):
                    pe.wait_ge(xs_sub, (i - 1) * KC + c + 1)
                for q in range(2):
                    for b in range(2):
                        t = slice(b * S, (b + 1) * S)
                        last = mm(ps[t, 2 * c + q, :], x1T[:, r, c, t], xkey[:, r, c, 8 * q:8 * (q + 1), t],
                                  start=True, stop=True)
                last.then_inc(xs_mm, 1)

            def turn(i, r, c):
                pe.wait_ge(xs_exp, i * KC + c + 1)
                if not (isinstance(i, int) and i == 0 and c == 0):
                    pe.wait_ge(xp_ev, i * KC + c)
                for n in range(8):
                    last = pe.transpose(ps[:, 4 + n // 4, (n % 4) * P:(n % 4 + 1) * P],
                                        xprob[:, r, c, n * P:(n + 1) * P], ident[:])
                last.then_inc(xp_t, 1)

            def values(i, r, c):
                pe.wait_ge(xp_ev, i * KC + c + 1)
                if c == 0:
                    wait(pe, xc_free, i)
                    pe.wait_ge(xvr_in[r], ((i - r) // 2 + 1) * 16 if isinstance(i, int) else (i - r) * 8 + 16)
                for n in range(8):
                    for b in range(2):
                        k = c * (KV // KC) + n // 2
                        last = mm(ps[b * S:(b + 1) * S, 6, (8 * c + n) * 18:(8 * c + n + 1) * 18],
                                  xpT[:, c, n * P + b * S:n * P + (b + 1) * S],
                                  xvr[:, r, b, k, :],
                                  start=True, stop=True)
                last.then_inc(xv_mm, 1)

            def cross_step(i, r):
                if there(i, 1):
                    scores(i + 1, 1 - r, 0)
                if there(i, 2):
                    j = i + 2
                    pe.wait_ge(x1r_in, j + 1)
                    if there(i, -2):
                        pe.wait_ge(lg_in, i - 1)
                    else:
                        wait(pe, x1_ev, j)
                    for c in range(KC):
                        last = pe.transpose(xT_ps[:, c * P:(c + 1) * P], x1r[:, r, c * P:(c + 1) * P], ident[:])
                    last.then_inc(x1_t, 1)
                if there(i):
                    turn(i, r, 0)
                if there(i, -2):
                    pe.wait_ge(sel_in, i - 1)
                    if there(i, 2):
                        pe.wait_ge(x1_ev, i + 3)
                    else:
                        pe.wait_ge(lg_in, i - 1)
                    mm(rk_ps[:, 0:NE], tri[:], sel[:, r, :], start=True, stop=True)
                    mm(rk_ps[:, NE:2 * NE], ones[:], sel[:, r, :], start=True, stop=True).then_inc(rk_mm, 1)
                if there(i, 1):
                    scores(i + 1, 1 - r, 1)
                if there(i, -1):
                    pe.wait_ge(x2_done, i)
                    if there(i, -2):
                        pe.wait_ge(rk_free, i - 1)
                    elif there(i, 2):
                        pe.wait_ge(x1_ev, i + 3)
                    for c in range(KC):
                        last = pe.transpose(xT_ps[:, c * P:(c + 1) * P], x2r[:, 1 - r, c * P:(c + 1) * P], ident[:])
                    last.then_inc(x2_t, 1)
                if there(i):
                    values(i, r, 0)
                    turn(i, r, 1)
                if there(i, -1):
                    pe.wait_ge(x2_ev, i)
                    for c in range(KC):
                        last = mm(lg_ps, x2Tr[:, 1 - r, c, :], gw_sb[:, c, :], start=(c == 0), stop=(c == KC - 1))
                    last.then_inc(lg_mm, 1)
                if there(i):
                    values(i, r, 1)

            tiles(pe, cross_step, 2, 2)

            pe.wait_ge(tb_cols, 1)
            pe.transpose(ps[0:8, 7, 0:P], cols[:, 0:8], ident[:]).then_inc(tb_t, 1)

            pe.wait_ge(x2T_in, NT)
            pe.wait_ge(xs_sub, KC * NT)
            with pe.Fori(0, T // N512) as n:
                for f in range(3):
                    f0, m = SFC[f]
                    q = f % 2
                    if f >= 2:
                        pe.wait_ge(sh_in, n * 3 + (f - 1))
                    for u in range(2):
                        for k in range(KC):
                            last = mm(ps[0:m, 2 * q + u, :], wsgu_sb[:, k, u * SF + f0:u * SF + f0 + m],
                                      x2T[:, k, bass.ds(n * N512, N512)], start=(k == 0), stop=(k == KC - 1))
                    last.then_inc(sg_mm, 1)
                pe.wait_ge(sh_in, n * 3 + 3)
                for j in range(GROUP):
                    if j >= 2:
                        pe.wait_ge(sd_ev, n * GROUP + (j - 1))
                    for f in range(3):
                        m = SFC[f][1]
                        last = mm(ps[:, 4 + j % 2, 0:D], shid[0:m, f, j * P:(j + 1) * P], wsd_sb[0:m, f, :],
                                  start=(f == 0), stop=(f == 2))
                    last.then_inc(sd_mm, 1)
                pe.wait_ge(sd_ev, n * GROUP + 4)

            pe.wait_ge(tb_in, 32)
            pe.wait_ge(tb_row, 2)
            pe.sem_inc(b_dn, 1)

            def turn_rows(b, r, q, n):
                pe.wait_ge(xg_in[q], n * 16 + 16)
                for c in range(KC):
                    last = pe.transpose(ps[:, r, c * P:(c + 1) * P], xg[:, q, c * P:(c + 1) * P], ident[:])
                last.then_inc(b_t1, 1)

            def weights_at(b):
                return pe.value_load(tab[0:1, bass.ds(b + 4 * P, 1)], min_val=0, max_val=WS - 1)

            def gate_up(b, r, w_slot):
                pe.wait_ge(b_xgT, b + 1)
                for c in range(KC):
                    last = mm(ps[:, 2 + r, 0:2 * F], xgT[:, r, c * P:(c + 1) * P],
                              wring[:, bass.ds(w_slot * W_SLOT + c * 2 * F, 2 * F)], start=(c == 0), stop=(c == KC - 1))
                last.then_inc(b_gu, 1)

            def block_step(b, r, q, n, w_slot, ahead2=True, ahead1=True):
                next_slot = weights_at(b + 1) if ahead1 else None
                pe.wait_ge(b_act, b + 1)
                for c in range(2):
                    last = pe.transpose(ps[0:FH, 4 + r, c * P:(c + 1) * P], act[:, r, c * FH:(c + 1) * FH], ident[:])
                last.then_inc(b_t2, 1)
                if ahead2:
                    turn_rows(b + 2, r, (q + 2) % XS, n + (1 if q >= 2 else 0))
                if ahead1:
                    gate_up(b + 1, 1 - r, next_slot)
                pe.wait_ge(b_actT, b + 1)
                for c in range(2):
                    last = mm(ps[:, 6 + r, 0:D], actT[0:FH, r, c * P:(c + 1) * P],
                              wring[0:FH, bass.ds(w_slot * W_SLOT + WGU + c * D, D)], start=(c == 0), stop=(c == 1))
                last.then_inc(b_dn, 1)
                return next_slot

            turn_rows(0, 0, 0, 0)
            turn_rows(1, 1, 1, 0)
            slot_of = weights_at(0)
            gate_up(0, 0, slot_of)
            for b in range(XS):
                slot_of = block_step(b, b % 2, b, 0, slot_of)
            with pe.Fori(1, NB // XS - 1) as n:
                slot_of = weights_at(n * XS)
                for q in range(XS):
                    slot_of = block_step(n * XS + q, q % 2, q, n, slot_of)
            slot_of = weights_at(NB - XS)
            for b in range(NB - XS, NB):
                slot_of = block_step(b, b % 2, b % XS, NB // XS - 1, slot_of, ahead2=b + 2 < NB, ahead1=b + 1 < NB)

        @block.vector
        def _(ve):
            v = nc.vector
            v.memset(reg_q[:, 0:NQ], 0.0).then_inc(vinit, 1)
            v.memset(reg_v[:], 0.0).then_inc(vinit, 1)
            ve.wait_ge(vinit, 2)
            v.memset(v_sb[0:S, :, :, 0, HD:HD + 1], 1.0).then_inc(vinit, 1)
            v.memset(v_sb[S:P, :, :, 1, HD:HD + 1], 1.0).then_inc(vinit, 1)
            ve.wait_ge(vinit, 4)
            con = Steps(ve, c_dve, 0, 20)
            ve.wait_ge(iotas, 3)
            con.then(v.tensor_copy(rel[:], rel_i[:]))
            con.then(v.tensor_scalar(rel[S:P, :], rel[S:P, :], float(-S), None, ALU.add))
            con.then(v.tensor_scalar(mask[:], rel[:], 0.0, None, ALU.is_le))
            ve.wait_ge(l_x, 48)
            con.then(v.tensor_tensor(bias[:], rel[:].unsqueeze(1).to_broadcast([P, H, S]),
                                     sl_sb[:].unsqueeze(2).to_broadcast([P, H, S]), ALU.mult))
            con.then(v.tensor_copy(ei[:], ei_i[:]))
            con.then(v.tensor_scalar(eo[:], ei[:], float(REGION), None, ALU.mult))
            con.then(v.tensor_copy(off[:], eo[:]))
            con.then(v.tensor_copy(bi[:], bi_i[:]))
            N_CON = con.n

            ve.wait_ge(l_wv, 32)
            for i in range(NT):
                ve.wait_ge(v_mm, i + 1)
                for b in range(2):
                    p = slice(b * S, (b + 1) * S)
                    v.tensor_tensor(v_sb[p, i, :, b, 0:HD], ps[p, 4 + i % GROUP, 0:D].rearrange("p (h e) -> p h e", h=H),
                                    bv_sb[p, :].rearrange("p (h e) -> p h e", h=H), ALU.add).then_inc(v_ev, 1)
            v.tensor_tensor(x_sb[:, :, 0:D], x_sb[:, :, 0:D],
                            bo_sb[:].unsqueeze(1).to_broadcast([P, NT, D]), ALU.add).then_inc(relc, 1)
            ve.wait_ge(relc, 1)

            def self_step(i, r):
                if there(i):
                    ve.wait_ge(exped, i + 1)
                    pv = prob[:, r, :].rearrange("p (h s) -> p h s", h=H)
                    v.tensor_tensor(pv, pv, mask[:].unsqueeze(1).to_broadcast([P, H, S]), ALU.mult).then_inc(masked, 1)
                if there(i, 1):
                    j, q = i + 1, 1 - r
                    ve.wait_ge(sc_mm, j + 1)
                    wait(ve, pv_mm, j - 1)
                    v.tensor_tensor(prob[:, q, :].rearrange("p (c n) -> p c n", c=KC), ps[:, 2 * q:2 * q + 2, :],
                                    bias[:].rearrange("p (c h) s -> p c (h s)", c=KC), ALU.add).then_inc(biased, 1)
                if there(i, -2):
                    j = i - 2
                    ve.wait_ge(ln_rs, j + 1)
                    v.tensor_scalar(x_sb[:, bass.ds(j, 1), 0:D].rearrange("p i d -> p (i d)"), res[:, 0, :],
                                    lmv[:, 0:1], lrs[:, 0:1], ALU.subtract, ALU.mult).then_inc(x1_done, 1)
                    ve.wait_ge(x1_done, j + 1)
                if there(i, -1):
                    j = i - 1
                    ve.wait_ge(o_mm, j + 1)
                    row = x_sb[:, bass.ds(j, 1), 0:D].rearrange("p i d -> p (i d)")
                    v.tensor_tensor(res[:, 0, :], ps[:, 7, 0:D], row, ALU.add).then_inc(o_res, 1)
                    ve.wait_ge(o_res, j + 1)
                    ve.sem_inc(waited, 1)
                    v.bn_stats(lstats[:], res[:, 0, :]).then_inc(ln_part, 1)
                    ve.wait_ge(ln_part, j + 1)
                    ve.sem_inc(waited, 1)
                    v.bn_aggr(lmv[:], lstats[:]).then_inc(ln_stat, 1)
                if there(i):
                    ve.wait_ge(pv_mm, i + 1)
                    wait(ve, ctx_t, i - 1)
                    cp = ps[:, 4 + r, 0:8 * 34].rearrange("p (j b e) -> p j b e", j=8, b=2)
                    v.reciprocal(crec[:, r, :, :], cp[:, :, :, HD:HD + 1].rearrange("p j b e -> p j (b e)")).then_inc(ctx_rec, 1)
                    ve.wait_ge(ctx_rec, i + 1)
                    v.tensor_tensor(ctxn[:, r, :].rearrange("p (b j e) -> p j b e", b=2, j=8), cp[:, :, :, 0:HD],
                                    crec[:, r, :, :].unsqueeze(3).to_broadcast([P, 8, 2, HD]), ALU.mult).then_inc(ctx_n, 1)

            tiles(ve, self_step, 1, 2)

            for q in range(2):
                ve.wait_ge(qd_in[q], 128 * (NT // 2))
                ve.wait_ge(kr_in[q], 16 * (NT // 2))
            v.memset(reg_qk[:], 0.0).then_inc(xz, 1)

            def softmax_in(i, r, c):
                ve.wait_ge(xs_mm, i * KC + c + 1)
                if not (isinstance(i, int) and i < 2):
                    ve.wait_ge(xp_t, (i - 2) * KC + c + 1)
                wait(ve, xs_sub, i * KC + (c - 1))
                s = ps[:, 2 * c:2 * c + 2, :].rearrange("p a (h t) -> p (a h) t", t=S)
                v.tensor_reduce(xmax[:, c, :], s, AX, ALU.max).then_inc(xs_max, 1)
                ve.wait_ge(xs_max, i * KC + c + 1)
                v.tensor_tensor(xprob[:, r, c, :].rearrange("p (h t) -> p h t", t=S), s,
                                xmax[:, c, :].unsqueeze(2).to_broadcast([P, HC, S]), ALU.subtract).then_inc(xs_sub, 1)

            def cross_step(i, r):
                if there(i, 1):
                    softmax_in(i + 1, 1 - r, 0)
                if there(i, -1):
                    j = i - 1
                    ve.wait_ge(ln_rs, j + (NT + 1))
                    wait(ve, x2_t, j - 1)
                    wait(ve, x2r_out, j - 1)
                    v.tensor_scalar(x2r[:, 1 - r, :], res[:, 1, :], lmv[:, 0:1], lrs[:, 0:1],
                                    ALU.subtract, ALU.mult).then_inc(x2_done, 1)
                    ve.wait_ge(x2_done, j + 1)
                if there(i, -2):
                    j = i - 2
                    ve.wait_ge(rk_mm, j + 1)
                    ranks = Steps(ve, rb_steps, j, RB_N)
                    ranks.then(v.tensor_tensor(pos[:], rk_ps[:, 0:NE], off[:], ALU.add))
                    v.tensor_tensor(off[:], off[:], rk_ps[:, NE:2 * NE], ALU.add).then_inc(rk_free, 1)
                    ve.wait_ge(rk_free, j + 1)
                if there(i, 1):
                    softmax_in(i + 1, 1 - r, 1)
                if there(i, -2):
                    ranks.then(v.tensor_tensor(hpos, hot[:, r, :, :], pos[:].unsqueeze(1).to_broadcast([P, TOPK, NE]), ALU.mult))
                    ranks.then(v.tensor_reduce(slotf[:], hpos, AX, ALU.add))
                    v.tensor_copy(slot[:, bass.ds(j * 8, TOPK)], slotf[:]).then_inc(slot_in, 1)
                if there(i, -1):
                    j = i - 1
                    ve.wait_ge(lg_mm, j + 1)
                    wait(ve, lg_exp, j)
                    v.tensor_copy(logit[:], lg_ps).then_inc(lg_in, 1)
                    ve.wait_ge(lg_in, j + 1)
                    v.tensor_reduce(lmax[:], logit[:], AX, ALU.max).then_inc(lg_steps, 1)
                    ve.wait_ge(lg_steps, j + 1)
                    v.tensor_scalar(lnmax[:], lmax[:], -1.0, None, ALU.mult).then_inc(lg_max, 1)
                if there(i, -1):
                    j = i - 1
                    st = Steps(ve, ra_steps, j, RA_N, waited)
                    ve.wait_ge(lg_exp, j + 1)
                    extra = bass.ds(j, 1)
                    st.then(v.reciprocal(prs[:], psum[:]))
                    st.then(v.tensor_scalar(pr[:], pexp[:], prs[:, 0:1], None, ALU.mult), alone=True)
                    st.then(v.max(top[:], pr[:]), alone=True)
                    st.then(v.max_index(topi[:], top[:], pr[:]))
                    st.then(v.tensor_copy(topf[:], topi[:]))
                    v.tensor_copy(x_sb[:, extra, C_E:C_E + TOPK].rearrange("p i d -> p (i d)"), topf[:, 0:TOPK])
                    st.then(v.tensor_reduce(tsum[:], top[:, 0:TOPK], AX, ALU.add))
                    st.then(v.tensor_scalar(tsum[:], tsum[:], TOP_EPS, None, ALU.add))
                    v.tensor_tensor(hot[:, 1 - r, :, :], ei[:].unsqueeze(1).to_broadcast([P, TOPK, NE]),
                                    topf[:, 0:TOPK].unsqueeze(2).to_broadcast([P, TOPK, NE]), ALU.is_equal)
                    st.then(v.reciprocal(trec[:], tsum[:]))
                    v.tensor_scalar(x_sb[:, extra, C_W:C_W + TOPK].rearrange("p i d -> p (i d)"), top[:, 0:TOPK],
                                    trec[:, 0:1], None, ALU.mult).then_inc(row_in, 1)
                    ve.wait_ge(row_in, j + 1)
                    v.tensor_reduce(sel[:, 1 - r, :], hot[:, 1 - r, :, :].rearrange("p k e -> p e k"), AX,
                                    ALU.add).then_inc(sel_in, 1)
                if there(i):
                    ve.wait_ge(xv_mm, i * KC + KC)
                    st = Steps(ve, xn_steps, i, XN_N, waited)
                    cx = ps[:, 6, 0:XH * (XD + 1)].rearrange("p (h e) -> p h e", h=XH)
                    row = x_sb[:, bass.ds(i, 1), 0:D].rearrange("p i d -> p (i d)")
                    st.then(v.reciprocal(xrec[:], cx[:, :, XD:XD + 1].rearrange("p h e -> p (h e)")))
                    v.tensor_tensor(xtmp.rearrange("p (h e) -> p h e", h=XH), cx[:, :, 0:XD],
                                    xrec[:].unsqueeze(2).to_broadcast([P, XH, XD]), ALU.mult).then_inc(xc_free, 1)
                    ve.wait_ge(xc_free, i + 1)
                    st.then(v.tensor_tensor(res[:, 1, :], xtmp, row, ALU.add), alone=True)
                    st.then(v.bn_stats(lstats[:], res[:, 1, :]), alone=True)
                    v.bn_aggr(lmv[:], lstats[:]).then_inc(ln_stat, 1)

            tiles(ve, cross_step, 2, 2)

            t = Steps(ve, c_dve, 0, 200)
            t.n = N_CON
            t.then(v.tensor_copy(offi, off[0:1, :]))
            ve.sem_inc(tb_off, 1)
            t.then(v.tensor_tensor(nblk, off[:], eo[:], ALU.subtract))
            t.then(v.tensor_scalar(nblk, nblk, float(P - 1), None, ALU.add))
            t.then(v.tensor_copy(nblki[:], nblk))
            t.then(v.tensor_scalar(nblki[:], nblki[:], P.bit_length() - 1, None, ALU.arith_shift_right))
            t.then(v.tensor_copy(nblk, nblki[:]))
            t.then(v.tensor_copy(pre[0], nblk))
            cur, d = 0, 1
            while d < NE:
                t.then(v.tensor_copy(pre[1 - cur][:, 0:d], pre[cur][:, 0:d]))
                t.then(v.tensor_tensor(pre[1 - cur][:, d:NE], pre[cur][:, d:NE], pre[cur][:, 0:NE - d], ALU.add))
                cur, d = 1 - cur, 2 * d
            end = pre[cur]
            t.then(v.tensor_copy(endi, end[0:1, :]))
            t.then(v.tensor_tensor(start, end, nblk, ALU.subtract))
            t.then(v.scalar_tensor_tensor(rowof, start, float(-P), eo[:], ALU.mult, ALU.add))
            for c in range(2):
                bcol = bi[:, c:c + 1]
                t.then(v.tensor_scalar(ge_end, end, bcol, None, ALU.is_le))
                t.then(v.tensor_scalar(ge_start, start, bcol, None, ALU.is_le))
                t.then(v.tensor_tensor(inb, ge_start, ge_end, ALU.subtract))
                t.then(v.tensor_reduce(cols[:, c:c + 1], ge_end, AX, ALU.add))
                t.then(v.tensor_scalar(cols[:, c:c + 1], cols[:, c:c + 1], float(NE - 1), None, ALU.min))
                t.then(v.tensor_copy(wsi[:, c:c + 1], cols[:, c:c + 1]))
                t.then(v.tensor_scalar(wsi[:, c:c + 1], wsi[:, c:c + 1], WS - 1, None, ALU.bitwise_and))
                t.then(v.tensor_copy(cols[:, 4 + c:5 + c], wsi[:, c:c + 1]))
                t.then(v.tensor_scalar(cols[:, 6 + c:7 + c], cols[:, c:c + 1], 1.0, None, ALU.add))
                t.then(v.tensor_reduce(ns[:, c:c + 1], inb, AX, ALU.add))
                t.then(v.tensor_tensor(inb, inb, rowof, ALU.mult))
                t.then(v.tensor_reduce(cols[:, 2 + c:3 + c], inb, AX, ALU.add))
                t.then(v.tensor_scalar(w6[:, c:c + 1], bcol, float(P), float(-PAD_ROW), ALU.mult, ALU.add))
                t.then(v.scalar_tensor_tensor(cols[:, 2 + c:3 + c], w6[:, c:c + 1], ns[:, c:c + 1],
                                              cols[:, 2 + c:3 + c], ALU.mult, ALU.add))
                t.then(v.tensor_scalar(cols[:, 2 + c:3 + c], cols[:, 2 + c:3 + c], float(PAD_ROW), None, ALU.add))
            ve.sem_inc(tb_cols, 1)
            ve.wait_ge(tb_t, 1)
            v.tensor_copy(tcol, ps[0:8, 7, 0:P]).then_inc(tb_row, 1)
            v.tensor_copy(tcoli, ps[0:8, 7, 0:P]).then_inc(tb_row, 1)

            ve.wait_ge(x2r_out, NT)
            with ve.Fori(0, T // N512) as n:
                for f in range(3):
                    m, q = SFC[f][1], f % 2
                    ve.wait_ge(sg_act, n * 3 + (f + 1))
                    v.tensor_tensor(shid[0:m, f, :], sgate[0:m, q, :], ps[0:m, 2 * q + 1, :], ALU.mult).then_inc(sh_in, 1)
                for j in range(GROUP):
                    ve.wait_ge(sd_mm, n * GROUP + (j + 1))
                    v.tensor_tensor(share[:, bass.ds(n * GROUP + j, 1), :].rearrange("p i d -> p (i d)"),
                                    ps[:, 4 + j % 2, 0:D],
                                    x_sb[:, bass.ds(n * GROUP + j, 1), 0:D].rearrange("p i d -> p (i d)"),
                                    ALU.add).then_inc(sd_ev, 1)

            ve.wait_ge(tb_in, 32)

            def copy_rows(b, r):
                ready = ve.value_load(tab[0:1, bass.ds(b + 6 * P, 1)], min_val=1, max_val=NE)
                ve.wait_ge(w_ready, ready)
                ve.wait_ge(b_t1, b + 1)
                v.tensor_copy(xgT[:, r, :], ps[:, r, 0:D]).then_inc(b_xgT, 1)

            def multiply(b, r):
                ve.wait_ge(b_silu, b + 1)
                if not isinstance(b, int) or b >= 2:
                    ve.wait_ge(b_t2, b - 1)
                v.tensor_tensor(act[:, r, :], gate[:, r, :], ps[:, 2 + r, F:2 * F], ALU.mult).then_inc(b_act, 1)

            def block_step(b, r, q, n, ahead2=True, ahead1=True):
                if ahead2:
                    copy_rows(b + 2, r)
                ve.wait_ge(xg_in[q], n * 16 + 16)
                wait(ve, added[q], n * 16)
                v.tensor_copy(toks[:, q:q + 1], xg[:, q, C_TOK:C_TOK + 1].bitcast(I32)).then_inc(b_meta, 1)
                v.scalar_tensor_tensor(w6[:], xg[:, q, C_E:C_E + TOPK], ebc[:, bass.ds(b, 1)],
                                       xg[:, q, C_W:C_W + TOPK], ALU.is_equal, ALU.mult).then_inc(b_meta, 1)
                ve.wait_ge(b_meta, b * 3 + 2)
                v.tensor_reduce(wcol[:, r:r + 1], w6[:], AX, ALU.add).then_inc(b_meta, 1)
                if ahead1:
                    multiply(b + 1, 1 - r)
                ve.wait_ge(b_meta, b * 3 + 3)
                ve.wait_ge(b_dn, b + 2)
                v.tensor_scalar(y_sb[:, q, :], ps[:, 6 + r, 0:D], wcol[:, r:r + 1], None, ALU.mult).then_inc(b_y, 1)

            copy_rows(0, 0)
            copy_rows(1, 1)
            multiply(0, 0)
            for b in range(XS):
                block_step(b, b % 2, b, 0)
            with ve.Fori(1, NB // XS - 1) as n:
                for q in range(XS):
                    block_step(n * XS + q, q % 2, q, n)
            for b in range(NB - XS, NB):
                block_step(b, b % 2, b % XS, NB // XS - 1, ahead2=b + 2 < NB, ahead1=b + 1 < NB)

            def finish(g, q):
                i = g * XS + q
                row = share[:, bass.ds(i, 1), :].rearrange("p i d -> p (i d)")
                ve.wait_ge(ac_in[q], g * 16 * XS + 16 * XS)
                v.tensor_tensor(f2[:, q, :], accl[:, q, 0, :], accl[:, q, 1, :], ALU.add).then_inc(f_part, 1)
                st = Steps(ve, f_steps, i, 4, waited)
                st.then(v.tensor_tensor(accl[:, q, 2, :], accl[:, q, 2, :], accl[:, q, 3, :], ALU.add))
                st.then(v.tensor_tensor(f2[:, q, :], f2[:, q, :], accl[:, q, 2, :], ALU.add))
                ve.sem_inc(f_sum, 1)
                st.then(v.tensor_tensor(row, row, f2[:, q, :], ALU.add), alone=True)
                st.then(v.bn_stats(lstats[:], row), alone=True)
                v.bn_aggr(fmv[:, q, :], lstats[:]).then_inc(f_aggr, 1)
                ve.wait_ge(f_aggr, i + 1)

            def finish_group(g):
                for q in range(XS):
                    finish(g, q)
                st = Steps(ve, f_newton, g, 3 + 3 * NEWTON)
                mean, var = fmv[:, :, 0:1], fmv[:, :, 1:2]
                st.then(v.tensor_scalar(fvar[:].unsqueeze(2), var, LN_EPS, None, ALU.add))
                st.then(v.tensor_scalar(ftmpi[:], fvar[:].bitcast(I32), 1, None, ALU.arith_shift_right))
                st.then(v.tensor_scalar(frsl[:].bitcast(I32), ftmpi[:], -1.0, float(0x5F3759DF), ALU.mult, ALU.add))
                for _ in range(NEWTON):
                    st.then(v.tensor_tensor(ftmp[:], frsl[:], frsl[:], ALU.mult))
                    st.then(v.scalar_tensor_tensor(ftmp[:], ftmp[:], -0.5, fvar[:], ALU.mult, ALU.mult))
                    st.then(v.scalar_tensor_tensor(frsl[:], ftmp[:], 1.5, frsl[:], ALU.add, ALU.mult))
                v.tensor_copy(frs[:, bass.ds(g * XS, XS)], frsl[:]).then_inc(f_stat, 1)
                v.scalar_tensor_tensor(fnm[:, bass.ds(g * XS, XS)].unsqueeze(2), mean, -1.0, frsl[:].unsqueeze(2),
                                       ALU.mult, ALU.mult).then_inc(f_stat, 1)
                ve.wait_ge(f_stat, g * 2 + 2)

            finish_group(0)
            with ve.Fori(1, NT // XS) as g:
                finish_group(g)


_INS = ["x", "xT", "ctxT", "ctx", "wqT", "wkT", "wvT", "woT", "bq", "bk", "bv", "bo", "slopes", "gwT", "wgu", "wdn",
        "wsgu", "wsda", "wsdb"]


def kernel(x, ctx_512, L0_attn_Wq, L0_attn_bq, L0_attn_Wk, L0_attn_bk, L0_attn_Wv, L0_attn_bv, L0_attn_Wo, L0_attn_bo,
           L0_attn_alibi_slopes, L0_ffn_gate_w, L0_ffn_w_gate_up, L0_ffn_w_down, L0_ffn_ws_gate_up, L0_ffn_ws_down):
    import numpy as np
    from concourse import bacc
    from concourse.bass_utils import run_bass_kernel_spmd

    tok = np.asarray(x).reshape(T, D)
    c = np.asarray(ctx_512)
    chunks = lambda w: np.asarray(w).T.reshape(KC, P, -1).transpose(1, 0, 2)
    sdown = np.asarray(L0_ffn_ws_down).T
    laid = {
        "x": tok.reshape(NT, P, D).transpose(1, 0, 2),
        "xT": chunks(tok),
        "ctxT": c.reshape(T, -1).T,
        "ctx": c.transpose(1, 0, 2).reshape(S, -1),
        "wqT": chunks(L0_attn_Wq), "wkT": chunks(L0_attn_Wk), "wvT": chunks(L0_attn_Wv),
        "woT": np.asarray(L0_attn_Wo).T.reshape(H // 2, 2, HD, D).transpose(0, 2, 1, 3).reshape(P, 2, D),
        "bq": np.asarray(L0_attn_bq).reshape(KC, P).T, "bk": np.asarray(L0_attn_bk).reshape(KC, P).T,
        "bv": np.asarray(L0_attn_bv).reshape(1, D), "bo": np.asarray(L0_attn_bo).reshape(1, D),
        "slopes": np.asarray(L0_attn_alibi_slopes).reshape(1, H),
        "gwT": chunks(L0_ffn_gate_w),
        "wgu": np.asarray(L0_ffn_w_gate_up).transpose(0, 2, 1).reshape(NE, KC, P, 2 * F).transpose(0, 2, 1, 3).reshape(NE, P, WGU),
        "wdn": np.asarray(L0_ffn_w_down).transpose(0, 2, 1).reshape(NE, 2, FH, D).transpose(0, 2, 1, 3).reshape(NE, FH, WDN),
        "wsgu": chunks(L0_ffn_ws_gate_up),
        "wsda": sdown[0:2 * P].reshape(2, P, D).transpose(1, 0, 2),
        "wsdb": sdown[2 * P:],
    }
    nc = bacc.Bacc("TRN2", target_bir_lowering=False, num_devices=1)
    arrays, args = {}, []
    for name in _INS:
        a = np.ascontiguousarray(laid[name])
        arrays[f"in_{name}"] = a
        args.append(nc.dram_tensor(f"in_{name}", a.shape, mybir.dt.from_np(a.dtype), kind="ExternalInput").ap())
    args.append(nc.dram_tensor("out_dram", (P, NT, D), F32, kind="ExternalOutput").ap())
    decoder(nc, *args)
    r = run_bass_kernel_spmd(nc, [arrays], core_ids=[0])
    return np.ascontiguousarray(r.results[0]["out_dram"].transpose(1, 0, 2)).reshape(B, S, D)
```

```python
from contextlib import ExitStack

import concourse.bass as bass
from concourse import mybir

ALU = mybir.AluOpType
ACT = mybir.ActivationFunctionType
AX = mybir.AxisListType.X
F32 = mybir.dt.float32
I32 = mybir.dt.int32
U32 = mybir.dt.uint32

P = 128
D = 256
KC = D // P
B, S = 32, 64
T = B * S
NT = T // P
H, HD = 16, 16
XH, XD, KV = 32, 8, 8
XG = XH // KV
HC = XH // KC
NE, F, TOPK = 64, 176, 6
FH = F // 2
SF = 352
SFC = ((0, 128), (128, 128), (256, 96))
LN_EPS, TOP_EPS = 1e-5, 1e-20
CAP = 30.0

ROW = 272
C_TOK, C_W, C_E = D, D + 1, D + 1 + TOPK
REGION = T + P
PAD_ROW = NE * REGION
NB = 160
WS = 4
WGU, WDN = KC * 2 * F, 2 * D
W_SLOT = WGU + WDN
XS = 4
GROUP = 4
N512 = 512


def wait(eng, sem, value):
    if isinstance(value, int) and value <= 0:
        return
    eng.wait_ge(sem, value)


class Steps:

    def __init__(self, eng, sem, run, total, spare=None):
        self.eng, self.sem, self.base, self.total, self.n = eng, sem, run * total, total, 0
        self.spare = spare

    def then(self, instruction, alone=False):
        self.done(self.start(instruction), alone)

    def start(self, instruction):
        self.n += 1
        assert self.n <= self.total
        instruction.then_inc(self.sem, 1)
        return self.n

    def done(self, n, alone=False):
        self.eng.wait_ge(self.sem, self.base + n)
        if alone:
            self.eng.sem_inc(self.spare, 1)


NEWTON = 3
GUESS = 0x5F3759DF
NEWTON_STEPS = 2 + 2 * NEWTON


def newton_steps(g, steps, mv, rstd, tmp, alone):
    v = tmp[:, 0:1]
    steps.then(g.tensor_scalar(v, mv[:, 1:2], LN_EPS, -8192.0 ** 2, ALU.add, ALU.mult), alone)
    steps.then(g.tensor_scalar(rstd.bitcast(I32), v.bitcast(I32), -0.5, float(GUESS - (1 << 30)), ALU.mult, ALU.add), alone)
    for grown in (1, 2, 16):
        steps.then(g.tensor_scalar(tmp[:, 1:2], rstd, rstd, v, ALU.mult, ALU.mult), alone)
        steps.then(g.tensor_scalar(rstd, tmp[:, 1:2], 3.0 * grown ** 2, rstd, ALU.add, ALU.mult), alone)


def decoder(nc, x, xT, ctxT, ctx, wqT, wkT, wvT, woT, bq, bk, bv, bo, slopes, gwT, wgu, wdn, wsgu, wsda, wsdb, out):
    with ExitStack() as stack:
        def sb(name, shape, dt=F32):
            return stack.enter_context(nc.sbuf_tensor(name, shape, dt))

        def sem(name):
            return stack.enter_context(nc.semaphore(name))

        rows_d = nc.dram_tensor("rows_d", [PAD_ROW + P, ROW], F32, kind="Internal").ap()
        acc_d = nc.dram_tensor("acc_d", [XS * (T + P), D], F32, kind="Internal").ap()
        tab_d = nc.dram_tensor("tab_d", [8, P], F32, kind="Internal").ap()
        tabi_d = nc.dram_tensor("tabi_d", [8, P], I32, kind="Internal").ap()

        ps = stack.enter_context(nc.psum_tensor("ps", [P, 8, N512], F32))

        xT_ps, rk_ps, lg_ps = ps[:, 7, 0:D], ps[:, 7, 0:2 * NE], ps[:, 7, 0:NE]

        def x1T_ps(i):
            return ps[:, 6 + i, 0:D] if isinstance(i, int) and i < 0 else xT_ps

        x_sb = sb("x_sb", [P, NT, ROW])
        xT_sb = sb("xT_sb", [P, KC, T])
        share = xT_sb[:, :, :].rearrange("p c t -> p (c t)").rearrange("p (i d) -> p i d", i=NT)
        reg_qk = sb("reg_qk", [P, 2 * KC * T])
        qT = reg_qk[:, 0:KC * T].rearrange("p (c t) -> p c t", c=KC)
        kT = reg_qk[:, KC * T:].rearrange("p (c t) -> p c t", c=KC)
        NV = NT * H * 2 * (HD + 1)
        reg_v = sb("reg_v", [P, NV])
        v_sb = reg_v[:, :].rearrange("p (i h b e) -> p i h b e", i=NT, h=H, b=2)
        XP = HC * S
        xprob = reg_v[:, 0:4 * XP].rearrange("p (r c n) -> p r c n", r=2, c=KC)
        x2T = reg_v[:, 4 * XP:4 * XP + KC * T].rearrange("p (c t) -> p c t", c=KC)
        NQ = 2 * KC * 8 * P
        reg_q = sb("reg_q", [P, NQ + 2 * KC * P])
        qdiag = reg_q[:, 0:NQ].rearrange("p (r c h t) -> p r c h t", r=2, c=KC, h=8)
        kTr = reg_q[:, NQ:].rearrange("p (r c t) -> p r c t", r=2, c=KC)
        at = [0]

        def carve(n):
            at[0] += n
            return reg_q[:, at[0] - n:at[0]]

        xg = carve(XS * ROW).rearrange("p (r n) -> p r n", r=XS)
        xgT = carve(2 * D).rearrange("p (r n) -> p r n", r=2)
        gate = carve(2 * F).rearrange("p (r n) -> p r n", r=2)
        act = carve(2 * F).rearrange("p (r n) -> p r n", r=2)
        actT = carve(2 * 2 * P).rearrange("p (r n) -> p r n", r=2)
        y_sb = carve(XS * D).rearrange("p (r n) -> p r n", r=XS)
        wring = sb("wring", [P, WS * W_SLOT])
        ctx_st = wring[:, 0:B * S]
        XK = KC * HC * P
        xkeys = [a[:, 0:XK].rearrange("p (c h t) -> p c h t", c=KC, h=HC) for a in (wring, reg_qk)]
        prob = sb("prob", [P, 2, H * S])
        bias = sb("bias", [P, H, S])
        cbuf = sb("cbuf", [P, 4 * D])
        ctxn, ctxnT = (cbuf[:, q * 2 * D:(q + 1) * 2 * D].rearrange("p (r n) -> p r n", r=2) for q in range(2))
        NXV = 2 * KV * 2 * (XD + 1)
        xvr = cbuf[:, 0:2 * NXV].rearrange("p (r b k n) -> p r b k n", r=2, b=2, k=KV)
        x1r = sb("x1r", [P, 2, D])
        x1T = sb("x1T", [P, 2, KC, P])
        xpT = prob
        xval = sb("xval", [P, B, KV, 2, XD + 1])
        NVR = 2 * H * (HD + 1)
        vbuf = sb("vbuf", [P, 2 * NVR])
        vr = vbuf[:, :].rearrange("p (r h n) -> p r h n", r=2, h=H)
        x2r = vbuf[:, 0:2 * D].rearrange("p (r n) -> p r n", r=2)
        x2Tr = vbuf[:, 2 * D:4 * D].rearrange("p (r c t) -> p r c t", r=2, c=KC)
        res = sb("res", [P, 2, D])
        wq_sb, wk_sb, wv_sb, wo_sb = (sb(n, [P, KC, D]) for n in ("wq_sb", "wk_sb", "wv_sb", "wo_sb"))
        bq_sb, bk_sb = sb("bq_sb", [P, KC]), sb("bk_sb", [P, KC])
        bv_sb, bo_sb = sb("bv_sb", [P, D]), sb("bo_sb", [P, D])
        sl_sb = sb("sl_sb", [P, H])
        gw_sb = sb("gw_sb", [P, KC, NE])
        wsgu_sb = sb("wsgu_sb", [P, KC, 2 * SF])
        wsd_sb = sb("wsd_sb", [P, 3, D])
        sgate = prob[:, :, :].rearrange("p r n -> p (r n)")[:, 0:3 * N512].rearrange("p (f n) -> p f n", f=3)
        shid = reg_v[:, 0:2 * 3 * N512].rearrange("p (r f n) -> p r f n", r=2, f=3)
        SBANK = (0, 2, 6)
        ident, ones, tri = sb("ident", [P, P]), sb("ones", [P, P]), sb("tri", [P, P])
        rel_i, rel, mask = sb("rel_i", [P, S], I32), sb("rel", [P, S]), sb("mask", [P, S])
        ei_i, ei, eo = sb("ei_i", [P, NE], I32), sb("ei", [P, NE]), sb("eo", [P, NE])
        bi_i, bi = sb("bi_i", [P, 2], I32), sb("bi", [P, 2])
        pad = sb("pad", [P, ROW])
        crec = sb("crec", [P, 2, 8, 2])
        xmax = sb("xmax", [P, KC, HC])
        xrec = sb("xrec", [P, XH])
        lstats, lmv, lrs = sb("lstats", [P, 6]), sb("lmv", [P, 2]), sb("lrs", [P, 1])
        ltmp, nblki, wsi = sb("ltmp", [P, 2]), sb("nblki", [P, NE], I32), sb("wsi", [P, 2], I32)
        logit, lmax, lnmax = sb("logit", [P, NE]), sb("lmax", [P, 1]), sb("lnmax", [P, 1])
        pexp, psum, prs, pr = sb("pexp", [P, NE]), sb("psum", [P, 1]), sb("prs", [P, 1]), sb("pr", [P, NE])
        top, topi = sb("top", [P, 8]), sb("topi", [P, 8], U32)
        tsum, trec = sb("tsum", [P, 1]), sb("trec", [P, 1])
        hot = reg_q[:, 0:2 * TOPK * NE].rearrange("p (r k e) -> p r k e", r=2, k=TOPK)
        hpos = reg_q[:, 2 * TOPK * NE:3 * TOPK * NE].rearrange("p (k e) -> p k e", k=TOPK)
        xtmp = reg_q[:, 3 * TOPK * NE:3 * TOPK * NE + D]
        sel, pos, slotf = sb("sel", [P, 2, NE]), sb("pos", [P, NE]), sb("slotf", [P, TOPK])
        slot = sb("slot", [P, NT * 8], I32)
        off = sb("off", [P, NE])
        at_tables = 3 * TOPK * NE + D
        nblk, pre0, pre1, start, rowof, ge_end, ge_start, inb = (
            reg_q[:, at_tables + n * NE:at_tables + (n + 1) * NE] for n in range(8))
        pre = [pre0, pre1]
        cols, ns = sb("cols", [P, 8]), sb("ns", [P, 2])
        tcol, tcoli = x1r[0:8, 0, 0:P], x1r[0:8, 0, P:2 * P].bitcast(I32)
        tab = bias[0:1, :, :].rearrange("p h s -> p (h s)").bitcast(I32)
        offi, endi = (x1r[0:1, 1, n * NE:(n + 1) * NE].bitcast(I32) for n in range(2))
        ebc = carve(2 * P)
        wcol, w6 = sb("wcol", [P, 2]), sb("w6", [P, TOPK])
        fmv, fvar, ftmp, ftmpi = sb("fmv", [P, XS, 2]), sb("fvar", [P, XS]), sb("ftmp", [P, XS]), sb("ftmpi", [P, XS], I32)
        frsl, frs, fnm = sb("frsl", [P, XS]), sb("frs", [P, NT]), sb("fnm", [P, NT])
        lastf, lastg = sb("lastf", [1, 1]), sb("lastg", [1, 1], I32)
        toks = sb("toks", [P, XS], I32)
        accl = wring[:, 0:XS * XS * D].rearrange("p (q a d) -> p q a d", q=XS, a=XS)
        outr = prob[:, 0, 0:XS * D].rearrange("p (q d) -> p q d", q=XS)

        l_xT = [sem(f"l_xT{n}") for n in range(T // N512)]
        l_x, l_wq, l_wk, l_bqk, l_wv, l_wo, l_ctx, l_late = (sem(n) for n in ("l_x", "l_wq", "l_wk", "l_bqk", "l_wv", "l_wo", "l_ctx", "l_late"))
        const, vinit, xinit, relc, dinit = sem("const"), sem("vinit"), sem("xinit"), sem("relc"), sem("dinit")
        c_pool, row_in, waited, pool_waited = sem("c_pool"), sem("row_in"), sem("waited"), sem("pool_waited")
        iotas = sem("iotas")
        c_dve = sem("c_dve")
        qk_mm, qk_ev, v_mm, v_ev = sem("qk_mm"), sem("qk_ev"), sem("v_mm"), sem("v_ev")
        qd_in, vr_in = [sem("qd_in0"), sem("qd_in1")], [sem("vr_in0"), sem("vr_in1")]
        sc_mm, biased, tanhed, exped, masked = sem("sc_mm"), sem("biased"), sem("tanhed"), sem("exped"), sem("masked")
        pv_mm, ctx_rec, ctx_n, ctx_t, ctx_ev, o_mm, o_res, x1_done = (
            sem(n) for n in ("pv_mm", "ctx_rec", "ctx_n", "ctx_t", "ctx_ev", "o_mm", "o_res", "x1_done"))
        ln_part, ln_stat, ln_steps, ln_rs = (sem(n) for n in ("ln_part", "ln_stat", "ln_steps", "ln_rs"))
        kr_in = [sem("kr_in0"), sem("kr_in1")]
        xz, xk_in, xvr_in = [sem("xz0"), sem("xz1")], [sem("xk_in0"), sem("xk_in1")], [sem("xvr_in0"), sem("xvr_in1")]
        x1r_in, x1_t, x1_ev = sem("x1r_in"), sem("x1_t"), sem("x1_ev")
        xs_mm, xs_max, xs_sub, xs_exp, xp_t, xp_ev = (
            sem(n) for n in ("xs_mm", "xs_max", "xs_sub", "xs_exp", "xp_t", "xp_ev"))
        xv_mm, xn_steps, xc_free, x2_done, x2r_out, x2_t, x2_ev, x2T_in = (
            sem(n) for n in ("xv_mm", "xn_steps", "xc_free", "x2_done", "x2r_out", "x2_t", "x2_ev", "x2T_in"))
        lg_mm, lg_in, lg_steps, lg_max, lg_exp, ra_steps, hot_in, sel_in = (
            sem(n) for n in ("lg_mm", "lg_in", "lg_steps", "lg_max", "lg_exp", "ra_steps", "hot_in", "sel_in"))
        rk_mm, rb_steps, rk_free, slot_in, scat = sem("rk_mm"), sem("rb_steps"), sem("rk_free"), sem("slot_in"), sem("scat")
        tb_cols, tb_t, tb_row, tb_d, tb_in, tb_off, pads, pool_pads = (
            sem(n) for n in ("tb_cols", "tb_t", "tb_row", "tb_d", "tb_in", "tb_off", "pads", "pool_pads"))
        sg_mm, sg_act, sh_in, sd_mm, sd_ev = sem("sg_mm"), sem("sg_act"), sem("sh_in"), sem("sd_mm"), sem("sd_ev")
        w_in, w_ready = [sem(f"w_in{q}") for q in range(WS)], sem("w_ready")
        xg_in = [sem(f"xg_in{q}") for q in range(XS)]
        b_t1, b_xgT, b_gu, b_silu, b_act, b_t2, b_actT, b_dn, b_y, b_meta, b_w = (
            sem(n) for n in ("b_t1", "b_xgT", "b_gu", "b_silu", "b_act", "b_t2", "b_actT", "b_dn", "b_y", "b_meta", "b_w"))
        added = [sem(f"added{q}") for q in range(XS)]
        ac_in, stored = [sem(f"ac_in{q}") for q in range(XS)], [sem(f"stored{pair}") for pair in range(XS // 2)]
        f_pair, f_sum, f_steps, f_aggr, f_newton, f_stat, f_out = (
            sem(n) for n in ("f_pair", "f_sum", "f_steps", "f_aggr", "f_newton", "f_stat", "f_out"))

        N_PADS = XS * (T + P) // P + 1 + NE // 2
        RA_N, RB_N, XN_N = 8, 3, 3

        block = stack.enter_context(nc.Block())

        def tiles(eng, step, ahead, behind):
            lo = 4
            hi = NT - 2 * ((ahead + 1) // 2)
            for i in range(-ahead, lo):
                step(i, i % 2)
            with eng.Fori(lo // 2, hi // 2) as g:
                for r in range(2):
                    step(g * 2 + r, r)
            for i in range(hi, NT + behind):
                step(i, i % 2)

        def last_group(eng):
            return eng.value_load(lastg[0:1, 0:1], min_val=1, max_val=NB // XS - 1)

        def groups(eng, last, step):
            sure = T * TOPK // P // XS - 1
            assert sure % 2 == 1
            with eng.Fori(0, sure // 2) as pair:
                for h in range(2):
                    step(pair * 2 + (1 + h))
            with eng.Fori(sure, NB // XS - 1) as n:
                with eng.If_lt(eng.to_reg(n), last):
                    step(n)

        def there(i, shift=0):
            return not isinstance(i, int) or 0 <= i + shift < NT

        @block.sync
        def _(sp):
            def columns_in(n):
                cols512 = slice(n * N512, (n + 1) * N512)
                sp.dma_start(xT_sb[:, :, cols512], xT[:, :, cols512]).then_inc(l_xT[n], 16)

            sp.dma_start(wq_sb[:], wqT).then_inc(l_wq, 16)
            columns_in(0)
            sp.dma_start(wk_sb[:], wkT).then_inc(l_wk, 16)
            sp.dma_start(bq_sb[:], bq).then_inc(l_bqk, 16)
            sp.dma_start(bk_sb[:], bk).then_inc(l_bqk, 16)
            for n in range(1, T // N512):
                columns_in(n)
            sp.dma_start(wv_sb[:], wvT).then_inc(l_wv, 16)
            sp.dma_start(bv_sb[:], bv.to_broadcast([P, D])).then_inc(l_wv, 16)
            sp.dma_start(sl_sb[:], slopes.to_broadcast([P, H])).then_inc(l_x, 16)
            sp.dma_start(x_sb[:, :, 0:D], x).then_inc(l_x, 16)
            sp.dma_start(bo_sb[:], bo.to_broadcast([P, D])).then_inc(l_x, 16)
            sp.dma_start(wo_sb[:], woT).then_inc(l_wo, 16)
            for q in range(2):
                sp.dma_start(ctx_st[q * S:(q + 1) * S, :], ctx).then_inc(l_ctx, 16)
            sp.dma_start(gw_sb[:], gwT).then_inc(l_late, 16)
            sp.dma_start(wsgu_sb[:], wsgu).then_inc(l_late, 16)
            sp.dma_start(wsd_sb[:, 0:2, :], wsda).then_inc(l_late, 16)
            sp.dma_start(wsd_sb[0:SFC[2][1], 2, :], wsdb).then_inc(l_late, 16)
            sp.wait_ge(dinit, 3)
            for j in range(XS * (T + P) // P):
                sp.dma_start(acc_d[j * P:(j + 1) * P, :], pad[:, 0:D]).then_inc(pads, 16)
            sp.dma_start(rows_d[PAD_ROW:PAD_ROW + P, :], pad[:]).then_inc(pads, 16)

            sp.wait_ge(vinit, 4)
            sp.wait_ge(qk_ev, 2 * KC)

            def q_tile(i, r, n):
                wait(sp, sc_mm, i - 1)
                for h in range(8):
                    p = slice(HD * h, HD * (h + 1))
                    sp.dma_start(qdiag[p, r, :, h, :], qT[p, :, bass.ds(i * P, P)]).then_inc(qd_in[r], 16)

            for i in range(2):
                q_tile(i, i, 0)
            sp.wait_ge(qk_ev, 2 * KC * (T // N512))
            with sp.Fori(1, NT // 2) as g:
                for r in range(2):
                    q_tile(g * 2 + r, r, g)

            key_rows = ctxT.rearrange("(c k d) t -> k d c t", c=KC, d=XD)

            def key_tile(i, r):
                if not (isinstance(i, int) and i < 2):
                    sp.wait_ge(xs_mm, (i - 1) * KC)
                for h in range(HC):
                    sp.dma_start(xkeys[r][XD * h:XD * (h + 1), :, h, :],
                                 key_rows[h // XG, :, :, bass.ds(i * P, P)]).then_inc(xk_in[r], 16)

            for i in range(2):
                sp.wait_ge(xz[i], 1)
                key_tile(i, i)
            with sp.Fori(1, NT // 2) as g:
                for r in range(2):
                    key_tile(g * 2 + r, r)

            def weights(e, q):
                w = wring[:, q * W_SLOT:(q + 1) * W_SLOT]
                sp.dma_start(w[:, 0:WGU], wgu[bass.ds(e, 1), :, :].rearrange("e p n -> (e p) n")).then_inc(w_in[q], 16)
                sp.dma_start(w[0:FH, WGU:], wdn[bass.ds(e, 1), :, :].rearrange("e p n -> (e p) n")).then_inc(w_in[q], 16)

            sp.wait_ge(xs_mm, KC * NT)
            for e in range(WS):
                weights(e, e)
            sp.wait_ge(tb_off, 1)
            with sp.Fori(0, NE // 2) as e:
                at_row = sp.value_load(offi[0:1, bass.ds(e, 1)], min_val=0, max_val=PAD_ROW)
                sp.dma_start(rows_d[bass.ds(at_row, P), :], pad[:]).then_inc(pads, 16)
            sp.wait_ge(tb_row, 2)
            sp.dma_start(tabi_d, tcoli).then_inc(tb_d, 16)
            sp.dma_start(tab_d, tcol).then_inc(tb_d, 16)
            sp.wait_ge(tb_d, 32)
            sp.dma_start(tab, tabi_d.rearrange("(o a) n -> o (a n)", o=1)).then_inc(tb_in, 16)
            sp.dma_start(ebc, tab_d[0:2, :].rearrange("(o a) n -> o (a n)", o=1).to_broadcast([P, 2 * P])).then_inc(tb_in, 16)
            for e in range(WS - 1):
                sp.wait_ge(w_in[e], 32)
                sp.sem_inc(w_ready, 1)
            with sp.Fori(1, NE // WS) as g:
                for q in range(WS):
                    u = (q - 1) % WS
                    sp.wait_ge(w_in[u], (g + 1) * 32 if q else g * 32)
                    sp.sem_inc(w_ready, 1)
                    done = sp.value_load(endi[0:1, bass.ds((g - 1) * WS + q, 1)], min_val=0, max_val=NB)
                    sp.wait_ge(b_dn, done + 1)
                    weights(g * WS + q, q)
            sp.wait_ge(w_in[WS - 1], 32 * (NE // WS))
            sp.sem_inc(w_ready, 1)

            last = last_group(sp)
            for q in range(XS):
                sp.wait_ge(added[q], last * 16 + 16)

            acc_tiles = acc_d.rearrange("(a t) d -> a t d", a=XS)

            def acc_tile(i, q):
                wait(sp, f_sum, i - XS + 1)
                sp.dma_start(accl[:, q, :, :], acc_tiles[:, bass.ds(i * P, P), :].rearrange("a p d -> p a d")).then_inc(ac_in[q], 16)

            for i in range(XS):
                acc_tile(i, i)
            with sp.Fori(1, NT // XS) as g:
                for q in range(XS):
                    acc_tile(g * XS + q, q)

        @block.gpsimd
        def _(pool):
            g = nc.gpsimd
            g.memset(ident[:], 0.0).then_inc(c_pool, 1)
            g.memset(tri[:], 1.0).then_inc(c_pool, 1)
            g.memset(ones[:], 1.0).then_inc(const, 1)
            pool.wait_ge(c_pool, 2)
            g.affine_select(out=ident[:], in_=ident[:], compare_op=ALU.not_equal, fill=1.0, base=0,
                            pattern=[[-1, P]], channel_multiplier=1).then_inc(const, 1)
            g.affine_select(out=tri[:], in_=tri[:], compare_op=ALU.is_gt, fill=0.0, base=0,
                            pattern=[[1, P]], channel_multiplier=-1).then_inc(const, 1)
            g.iota(rel_i[:], pattern=[[-1, S]], base=0, channel_multiplier=1).then_inc(iotas, 1)
            g.iota(ei_i[:], pattern=[[1, NE]], base=0, channel_multiplier=0).then_inc(iotas, 1)
            g.iota(bi_i[:], pattern=[[P, 2]], base=0, channel_multiplier=1).then_inc(iotas, 1)
            g.iota(pad[:, C_TOK:C_TOK + 1].bitcast(I32), pattern=[[0, 1]], base=T, channel_multiplier=1).then_inc(c_pool, 1)
            g.memset(pad[:, 0:D], 0.0).then_inc(dinit, 1)
            g.memset(pad[:, C_W:ROW], -1.0).then_inc(dinit, 1)
            pool.wait_ge(c_pool, 3)
            pool.sem_inc(dinit, 1)
            g.iota(x_sb[:, :, C_TOK:C_TOK + 1].bitcast(I32), pattern=[[P, NT], [0, 1]], base=0,
                   channel_multiplier=1).then_inc(xinit, 1)
            g.memset(x_sb[:, :, C_E + TOPK:ROW], 0.0).then_inc(xinit, 1)
            g.memset(xval[:], 0.0).then_inc(c_pool, 1)
            pool.wait_ge(c_pool, 4)
            pool.wait_ge(l_ctx, 32)
            for q in range(2):
                p = slice(q * S, (q + 1) * S)
                g.memset(xval[p, :, :, q, XD:XD + 1], 1.0).then_inc(c_pool, 1)
                g.tensor_copy(xval[p, :, :, q, 0:XD],
                              ctx_st[p, :].rearrange("p (b k d) -> p b k d", b=B, k=KV)).then_inc(xinit, 1)
                pool.wait_ge(c_pool, 5 + q)
                pool.wait_ge(xinit, 3 + q)

            g.memset(wring[:, 0:XK], 0.0).then_inc(xz[0], 1)

            pool.wait_ge(qk_ev, 2 * KC)
            pool.wait_ge(v_ev, 2 * GROUP)

            def key_tile(i, r):
                if not (isinstance(i, int) and i < 2):
                    pool.wait_ge(sc_mm, i - 1)
                    pool.sem_inc(pool_waited, 1)
                pool.dma_start(kTr[:, r, :, :], kT[:, :, bass.ds(i * P, P)]).then_inc(kr_in[r], 16)

            def value_tile(i, r):
                if not (isinstance(i, int) and i < 2):
                    pool.wait_ge(pv_mm, i - 1)
                    pool.sem_inc(pool_waited, 1)
                pool.dma_start(vr[:, r, :, :], v_sb[:, bass.ds(i, 1), :, :, :].rearrange("p i h b e -> p (i h) (b e)")).then_inc(vr_in[r], 16)

            def norm(n):
                pool.wait_ge(ln_stat, n + 1)
                alone = not isinstance(n, int)
                if alone:
                    pool.sem_inc(pool_waited, 1)
                newton_steps(g, Steps(pool, ln_steps, n, NEWTON_STEPS, pool_waited), lmv[:], lrs[:], ltmp[:], alone)
                pool.sem_inc(ln_rs, 1)

            def self_step(i, r):
                if isinstance(i, int) and i == 0:
                    pool.wait_ge(qk_ev, 2 * KC * (T // N512))
                    pool.wait_ge(v_ev, 2 * NT)
                if there(i, 2):
                    key_tile(i + 2, r)
                if there(i, -2):
                    norm(i - 2)
                if there(i, 2):
                    value_tile(i + 2, r)

            tiles(pool, self_step, 2, 2)

            def cross_values(i):
                if i >= 2:
                    pool.wait_ge(xv_mm, (i - 1) * KC)
                pool.dma_start(xvr[:, i % 2, :, :, :].rearrange("p b k n -> p b (k n)"),
                               xval[:, 2 * i:2 * i + 2, :, :, :].rearrange("p b k q e -> p b (k q e)")).then_inc(xvr_in[i % 2], 16)

            def step(i):
                if there(i):
                    norm(NT + i)
                if there(i, 2):
                    if i == -2:
                        pool.wait_ge(o_mm, NT)
                    cross_values(i + 2)
                if there(i, -2):
                    j = i - 2
                    pool.wait_ge(slot_in, j + 1)
                    pool.wait_ge(row_in, j + 1)
                    pool.wait_ge(x2r_out, j + 1)
                    for k in range(TOPK):
                        g.indirect_dma_start(
                            out=rows_d[:, :],
                            out_offset=bass.IndirectOffsetOnAxis(ap=slot[:, 8 * j + k:8 * j + k + 1], axis=0),
                            in_=x_sb[:, j, :], in_offset=None).then_inc(scat, 16)

            for i in range(-2, NT + 2):
                step(i)

            pool.wait_ge(tb_off, 1)
            with pool.Fori(NE // 2, NE) as e:
                at_row = pool.value_load(offi[0:1, bass.ds(e, 1)], min_val=0, max_val=PAD_ROW)
                pool.dma_start(rows_d[bass.ds(at_row, P), :], pad[:]).then_inc(pool_pads, 16)

            pool.wait_ge(pads, 16 * N_PADS)

            def add_block(n, q):
                pool.wait_ge(b_y, n * XS + q + 1)
                wait(pool, added[q], n * 16)
                pool.sem_inc(pool_waited, 1)
                g.indirect_dma_start(
                    out=acc_d[:, :], out_offset=bass.IndirectOffsetOnAxis(ap=toks[:, q:q + 1], axis=0),
                    in_=y_sb[:, q, :], in_offset=None, compute_op=ALU.add).then_inc(added[q], 16)

            def group(n):
                for q in range(XS):
                    add_block(n, q)

            group(0)
            last = last_group(pool)
            groups(pool, last, group)
            group(last)

        @block.scalar
        def _(sc):
            a = nc.scalar
            sc.wait_ge(l_bqk, 32)
            for n in range(T // N512):
                for m in range(2 * KC):
                    dst, b = ((qT, bq_sb), (kT, bk_sb))[m // KC]
                    c = m % KC
                    sc.wait_ge(qk_mm, 4 * n + m + 1)
                    a.activation(dst[:, c, n * N512:(n + 1) * N512], ps[:, m, :], ACT.Identity,
                                 bias=b[:, c:c + 1]).then_inc(qk_ev, 1)

            def self_step(i, r):
                if there(i, -1):
                    j = i - 1
                    sc.wait_ge(ctx_t, j + 1)
                    wait(sc, o_mm, j - 1)
                    a.activation(ctxnT[:, 1 - r, :].rearrange("p (q b s) -> p b q s", q=2, b=2),
                                 ps[:, 6, 0:D].rearrange("p (b q s) -> p b q s", b=2, q=2), ACT.Copy).then_inc(ctx_ev, 1)
                if there(i, 1):
                    j = i + 1
                    sc.wait_ge(biased, j + 1)
                    a.activation(prob[:, 1 - r, :], prob[:, 1 - r, :], ACT.Tanh,
                                 scale=1.0 / (CAP * HD ** 0.5)).then_inc(tanhed, 1)
                    sc.wait_ge(tanhed, j + 1)
                    a.activation(prob[:, 1 - r, :], prob[:, 1 - r, :], ACT.Exp, scale=CAP).then_inc(exped, 1)

            tiles(sc, self_step, 1, 1)

            def cross_exp(i, r, c):
                sc.wait_ge(xs_sub, i * KC + c + 1)
                a.activation(xprob[:, r, c, :], xprob[:, r, c, :], ACT.Exp, scale=XD ** -0.5).then_inc(xs_exp, 1)

            def cross_evict(i, c):
                sc.wait_ge(xp_t, i * KC + c + 1)
                if not (isinstance(i, int) and i == 0):
                    sc.wait_ge(xv_mm, (i - 1) * KC + c + 1)
                a.activation(xpT[:, c, :].rearrange("p (a n) -> p a n", a=2), ps[:, 4:6, :], ACT.Copy).then_inc(xp_ev, 1)

            def cross_step(i, r):
                if there(i, 2):
                    j = i + 2
                    sc.wait_ge(x1_t, j + 1)
                    if not (isinstance(i, int) and i < 0):
                        sc.wait_ge(xs_mm, j * KC - KC)
                    a.activation(x1T[:, r, :, :].rearrange("p c t -> p (c t)"), x1T_ps(i), ACT.Copy).then_inc(x1_ev, 1)
                if there(i):
                    cross_evict(i, 0)
                if there(i, 1):
                    cross_exp(i + 1, 1 - r, 0)
                if there(i, -1):
                    j = i - 1
                    sc.wait_ge(x2_done, j + 1)
                    a.activation(x_sb[:, bass.ds(j, 1), 0:D].rearrange("p i d -> p (i d)"), x2r[:, 1 - r, :],
                                 ACT.Copy).then_inc(x2r_out, 1)
                    sc.wait_ge(x2_t, j + 1)
                    wait(sc, lg_mm, j - 1)
                    a.activation(x2Tr[:, 1 - r, :, :].rearrange("p c t -> p (c t)"), xT_ps, ACT.Copy).then_inc(x2_ev, 1)
                    a.activation(x2T[:, :, bass.ds(j * P, P)], xT_ps.rearrange("p (c t) -> p c t", c=KC),
                                 ACT.Copy).then_inc(x2T_in, 1)
                if there(i):
                    cross_evict(i, 1)
                if there(i, 1):
                    cross_exp(i + 1, 1 - r, 1)
                if there(i, -1):
                    j = i - 1
                    sc.wait_ge(lg_max, j + 1)
                    a.activation(pexp[:], logit[:], ACT.Exp, bias=lnmax[:, 0:1], accum_out=psum[:]).then_inc(lg_exp, 1)
                if there(i, 3):
                    j = i + 3
                    sc.wait_ge(x1_done, j + 1)
                    wait(sc, x1_t, j - 1)
                    a.activation(x1r[:, 1 - r, :], x_sb[:, bass.ds(j, 1), 0:D].rearrange("p i d -> p (i d)"),
                                 ACT.Copy).then_inc(x1r_in, 1)

            tiles(sc, cross_step, 3, 2)

            def shared_silu(n):
                for f in range(3):
                    m = SFC[f][1]
                    sc.wait_ge(sg_mm, n * 3 + (f + 1))
                    wait(sc, sh_in, n * 3 + (f - 2))
                    a.activation(sgate[0:m, f, :], ps[0:m, SBANK[f], :], ACT.Silu).then_inc(sg_act, 1)

            shared_silu(0)
            with sc.Fori(1, T // N512) as n:
                shared_silu(n)

            sc.wait_ge(tb_in, 32)
            sc.wait_ge(scat, 16 * TOPK * NT)
            sc.wait_ge(pads, 16 * N_PADS)
            sc.wait_ge(pool_pads, 16 * (NE // 2))
            sc.wait_ge(sc_mm, NT)

            def rows_in(b, q):
                at_row = sc.value_load(tab[0:1, bass.ds(b + 2 * P, 1)], min_val=0, max_val=PAD_ROW)
                if not (isinstance(b, int) and b < XS):
                    sc.wait_ge(b_t1, b - XS + 1)
                    sc.wait_ge(b_meta, (b - XS) * 3 + 3)
                sc.dma_start(xg[:, q, :], rows_d[bass.ds(at_row, P), :]).then_inc(xg_in[q], 16)

            for b in range(XS):
                rows_in(b, b)

            def block_step(b, r, q, first=False, more=True, rows=True):
                if not first:
                    sc.wait_ge(b_t2, b + 1)
                    wait(sc, b_dn, b)
                    a.activation(actT[0:FH, r, :], ps[0:FH, 4 + r, 0:2 * P], ACT.Copy).then_inc(b_actT, 1)
                if more:
                    sc.wait_ge(b_gu, b + 2)
                    wait(sc, b_act, b)
                    a.activation(gate[:, 1 - r, :], ps[:, 2 + (1 - r), 0:F], ACT.Silu).then_inc(b_silu, 1)
                if rows and not first:
                    rows_in(b + XS, q)

            def group(n, last=False):
                for q in range(XS):
                    block_step(n * XS + q, q % 2, q, more=not last or q + 1 < XS, rows=not last)

            block_step(-1, 1, 3, first=True)
            group(0)
            last = last_group(sc)
            groups(sc, last, group)
            group(last, last=True)

            def out_tiles(g, bank):
                sc.wait_ge(f_stat, g * 2 + 2)
                for pair in range(XS // 2):
                    first = g * XS + 2 * pair
                    wait(sc, stored[pair], g * 16)
                    for q in (2 * pair, 2 * pair + 1):
                        i = g * XS + q
                        a.activation(outr[:, q, :], ps[:, bank + q, 0:D], ACT.Identity,
                                     bias=fnm[:, bass.ds(i, 1)], scale=frs[:, bass.ds(i, 1)]).then_inc(f_out, 1)
                    sc.wait_ge(f_out, first + 2)
                    sc.dma_start(out[:, bass.ds(first, 2), :], outr[:, 2 * pair:2 * pair + 2, :]).then_inc(stored[pair], 16)

            for g in range(2):
                out_tiles(g, g * XS)
            with sc.Fori(1, NT // XS // 2) as g2:
                for h in range(2):
                    out_tiles(g2 * 2 + h, h * XS)
            for pair in range(XS // 2):
                sc.wait_ge(stored[pair], 16 * (NT // XS))

        @block.tensor
        def _(pe):
            mm = pe.matmul
            pe.wait_ge(l_wq, 16)
            for n in range(T // N512):
                pe.wait_ge(l_xT[n], 16)
                for m in range(2 * KC):
                    if n == 0 and m == KC:
                        pe.wait_ge(l_wk, 16)
                    w, c = (wq_sb, wk_sb)[m // KC], m % KC
                    if n:
                        pe.wait_ge(qk_ev, 4 * (n - 1) + m + 1)
                    for k in range(KC):
                        last = mm(ps[:, m, :], w[:, k, c * P:(c + 1) * P], xT_sb[:, k, n * N512:(n + 1) * N512],
                                  start=(k == 0), stop=(k == KC - 1))
                    last.then_inc(qk_mm, 1)
                if n == 0:
                    pe.wait_ge(l_wv, 32)
                for j in range(GROUP):
                    i = n * GROUP + j
                    if n:
                        pe.wait_ge(v_ev, 2 * (i - GROUP) + 2)
                    for k in range(KC):
                        last = mm(ps[:, 4 + j, 0:D], xT_sb[:, k, i * P:(i + 1) * P], wv_sb[:, k, :],
                                  start=(k == 0), stop=(k == KC - 1))
                    last.then_inc(v_mm, 1)
            pe.wait_ge(const, 3)
            pe.wait_ge(l_wo, 16)
            pe.wait_ge(qk_ev, 16)
            pe.wait_ge(v_ev, 2 * NT)

            def self_step(i, r):
                if there(i, 1):
                    j, q = i + 1, 1 - r
                    pe.wait_ge(qd_in[q], ((j - q) // 2 + 1) * 128 if isinstance(j, int) else (j - q) * 64 + 128)
                    pe.wait_ge(kr_in[q], ((j - q) // 2 + 1) * 16 if isinstance(j, int) else (j - q) * 8 + 16)
                    wait(pe, biased, j - 1)
                    for c in range(KC):
                        for b in range(2):
                            t = slice(b * S, (b + 1) * S)
                            last = mm(ps[t, 2 * q + c, :], kTr[:, q, c, t], qdiag[:, q, c, :, t], start=True, stop=True)
                    last.then_inc(sc_mm, 1)
                if there(i, -1):
                    j, q = i - 1, 1 - r
                    pe.wait_ge(ctx_n, j + 1)
                    wait(pe, ctx_ev, j)
                    for b in range(2):
                        last = pe.transpose(ps[:, 6, b * P:(b + 1) * P], ctxn[:, q, b * P:(b + 1) * P], ident[:])
                    last.then_inc(ctx_t, 1)
                if there(i):
                    pe.wait_ge(vr_in[r], ((i - r) // 2 + 1) * 16 if isinstance(i, int) else (i - r) * 8 + 16)
                    pe.wait_ge(masked, i + 1)
                    wait(pe, ctx_n, i - 1)
                    for h in range(H):
                        last = mm(ps[(h % 2) * S:(h % 2 + 1) * S, 4 + r, (h // 2) * 34:(h // 2 + 1) * 34],
                                  prob[:, r, h * S:(h + 1) * S],
                                  vr[:, r, h, :],
                                  start=True, stop=True)
                    last.then_inc(pv_mm, 1)
                if there(i, -1):
                    j, q = i - 1, 1 - r
                    pe.wait_ge(ctx_ev, j + 1)
                    wait(pe, o_res, j)
                    for q2 in range(2):
                        last = mm(ps[:, 7, 0:D], ctxnT[:, q, q2 * P:(q2 + 1) * P], wo_sb[:, q2, :],
                                  start=(q2 == 0), stop=(q2 == 1))
                    last.then_inc(o_mm, 1)

            tiles(pe, self_step, 1, 1)
            pe.wait_ge(ctx_n, NT)
            pe.wait_ge(biased, NT)
            pe.wait_ge(xinit, 4)
            pe.wait_ge(l_late, 64)

            def scores(i, r, c):
                if c == 0:
                    pe.wait_ge(xk_in[r], ((i - r) // 2 + 1) * 256 if isinstance(i, int) else (i - r) * 128 + 256)
                    pe.wait_ge(x1_ev, i + 1)
                if not (isinstance(i, int) and i == 0):
                    pe.wait_ge(xs_sub, (i - 1) * KC + c + 1)
                for q in range(2):
                    for b in range(2):
                        t = slice(b * S, (b + 1) * S)
                        last = mm(ps[t, 2 * c + q, :], x1T[:, r, c, t], xkeys[r][:, c, 8 * q:8 * (q + 1), t],
                                  start=True, stop=True)
                last.then_inc(xs_mm, 1)

            def turn(i, r, c):
                pe.wait_ge(xs_exp, i * KC + c + 1)
                if not (isinstance(i, int) and i == 0 and c == 0):
                    pe.wait_ge(xp_ev, i * KC + c)
                for n in range(8):
                    last = pe.transpose(ps[:, 4 + n // 4, (n % 4) * P:(n % 4 + 1) * P],
                                        xprob[:, r, c, n * P:(n + 1) * P], ident[:])
                last.then_inc(xp_t, 1)

            def values(i, r, c):
                pe.wait_ge(xp_ev, i * KC + c + 1)
                if c == 0:
                    wait(pe, xc_free, i)
                    pe.wait_ge(xvr_in[r], ((i - r) // 2 + 1) * 16 if isinstance(i, int) else (i - r) * 8 + 16)
                for n in range(8):
                    for b in range(2):
                        k = c * (KV // KC) + n // 2
                        last = mm(ps[b * S:(b + 1) * S, 6, (8 * c + n) * 18:(8 * c + n + 1) * 18],
                                  xpT[:, c, n * P + b * S:n * P + (b + 1) * S],
                                  xvr[:, r, b, k, :],
                                  start=True, stop=True)
                last.then_inc(xv_mm, 1)

            def shared_up(n, f):
                f0, m = SFC[f]
                wait(pe, sh_in, n * 3 + (f - 2))
                for u in range(2):
                    for k in range(KC):
                        last = mm(ps[0:m, SBANK[f] + u, :], wsgu_sb[:, k, u * SF + f0:u * SF + f0 + m],
                                  x2T[:, k, bass.ds(n * N512, N512)], start=(k == 0), stop=(k == KC - 1))
                last.then_inc(sg_mm, 1)

            def cross_step(i, r):
                if there(i, 1):
                    scores(i + 1, 1 - r, 0)
                if there(i, 2):
                    j = i + 2
                    pe.wait_ge(x1r_in, j + 1)
                    if there(i, -2):
                        pe.wait_ge(lg_in, i - 1)
                    else:
                        wait(pe, x1_ev, j)
                    if isinstance(i, int) and i == 0:
                        pe.wait_ge(o_res, NT)
                    for c in range(KC):
                        last = pe.transpose(x1T_ps(i)[:, c * P:(c + 1) * P], x1r[:, r, c * P:(c + 1) * P], ident[:])
                    last.then_inc(x1_t, 1)
                if there(i):
                    turn(i, r, 0)
                if there(i, -2):
                    pe.wait_ge(sel_in, i - 1)
                    if there(i, 2):
                        pe.wait_ge(x1_ev, i + 3)
                    else:
                        pe.wait_ge(lg_in, i - 1)
                    mm(rk_ps[:, 0:NE], tri[:], sel[:, r, :], start=True, stop=True)
                    mm(rk_ps[:, NE:2 * NE], ones[:], sel[:, r, :], start=True, stop=True).then_inc(rk_mm, 1)
                if there(i, 1):
                    scores(i + 1, 1 - r, 1)
                if isinstance(i, int) and i == NT:
                    pe.wait_ge(x2T_in, GROUP)
                    pe.wait_ge(xs_sub, KC * NT)
                    shared_up(0, 0)
                if there(i):
                    values(i, r, 0)
                if there(i, -1):
                    pe.wait_ge(x2_done, i)
                    if there(i, -2):
                        pe.wait_ge(rk_free, i - 1)
                    elif there(i, 2):
                        pe.wait_ge(x1_ev, i + 3)
                    for c in range(KC):
                        last = pe.transpose(xT_ps[:, c * P:(c + 1) * P], x2r[:, 1 - r, c * P:(c + 1) * P], ident[:])
                    last.then_inc(x2_t, 1)
                if there(i):
                    turn(i, r, 1)
                if there(i, -1):
                    pe.wait_ge(x2_ev, i)
                    pe.wait_ge(x2T_in, i)
                    for c in range(KC):
                        last = mm(lg_ps, x2Tr[:, 1 - r, c, :], gw_sb[:, c, :], start=(c == 0), stop=(c == KC - 1))
                    last.then_inc(lg_mm, 1)
                if isinstance(i, int) and i == NT:
                    shared_up(0, 1)
                if there(i):
                    values(i, r, 1)

            tiles(pe, cross_step, 2, 2)

            pe.wait_ge(x2T_in, NT)
            pe.wait_ge(xc_free, NT)
            pe.wait_ge(rk_free, NT)
            def shared_down(n, r):
                pe.wait_ge(sh_in, n * 3 + 3)
                for j in range(GROUP):
                    wait(pe, sd_ev, n * GROUP + (j - 1))
                    for f in range(3):
                        m = SFC[f][1]
                        last = mm(ps[:, 4 + j % 2, 0:D], shid[0:m, r, f, j * P:(j + 1) * P], wsd_sb[0:m, f, :],
                                  start=(f == 0), stop=(f == 2))
                    last.then_inc(sd_mm, 1)

            def shared_step(n, r, more=True):
                if more:
                    shared_up(n + 1, 0)
                shared_down(n, r)
                if more:
                    shared_up(n + 1, 1)
                    shared_up(n + 1, 2)

            shared_up(0, 2)
            shared_step(0, 0)
            shared_step(1, 1)
            pe.wait_ge(tb_cols, 1)
            pe.wait_ge(sd_ev, 2 * GROUP)
            pe.transpose(ps[0:8, 4, 0:P], cols[:, 0:8], ident[:]).then_inc(tb_t, 1)
            pe.wait_ge(tb_row, 2)
            shared_step(2, 0)
            shared_step(3, 1, more=False)
            pe.wait_ge(sd_ev, NT)

            pe.wait_ge(tb_in, 32)
            pe.wait_ge(tb_row, 2)
            pe.sem_inc(b_dn, 1)

            def turn_rows(b, r, q, n):
                pe.wait_ge(xg_in[q], n * 16 + 16)
                for c in range(KC):
                    last = pe.transpose(ps[:, r, c * P:(c + 1) * P], xg[:, q, c * P:(c + 1) * P], ident[:])
                last.then_inc(b_t1, 1)

            def weights_at(b):
                return pe.value_load(tab[0:1, bass.ds(b + 4 * P, 1)], min_val=0, max_val=WS - 1)

            def gate_up(b, r, w_slot):
                pe.wait_ge(b_xgT, b + 1)
                for c in range(KC):
                    last = mm(ps[:, 2 + r, 0:2 * F], xgT[:, r, c * P:(c + 1) * P],
                              wring[:, bass.ds(w_slot * W_SLOT + c * 2 * F, 2 * F)], start=(c == 0), stop=(c == KC - 1))
                last.then_inc(b_gu, 1)

            def block_step(b, r, q, n, slots, ahead2=True, ahead1=True):
                pe.wait_ge(b_act, b + 1)
                for c in range(2):
                    last = pe.transpose(ps[0:FH, 4 + r, c * P:(c + 1) * P], act[:, r, c * FH:(c + 1) * FH], ident[:])
                last.then_inc(b_t2, 1)
                if ahead2:
                    turn_rows(b + 2, r, (q + 2) % XS, n + (1 if q >= 2 else 0))
                if ahead1:
                    gate_up(b + 1, 1 - r, slots[1])
                after = weights_at(b + 2) if ahead2 else None
                pe.wait_ge(b_actT, b + 1)
                for c in range(2):
                    last = mm(ps[:, 6 + r, 0:D], actT[0:FH, r, c * P:(c + 1) * P],
                              wring[0:FH, bass.ds(slots[0] * W_SLOT + WGU + c * D, D)], start=(c == 0), stop=(c == 1))
                last.then_inc(b_dn, 1)
                return slots[1], after

            turn_rows(0, 0, 0, 0)
            turn_rows(1, 1, 1, 0)
            carried = [pe.alloc_register(f"carried{c}") for c in range(2)]

            def carry(slots):
                for register, w_slot in zip(carried, slots):
                    pe.reg_mov(register, w_slot)

            def group(n, last=False):
                slots = [pe.snap(register, min_val=0, max_val=WS - 1) for register in carried]
                for q in range(XS):
                    slots = block_step(n * XS + q, q % 2, q, n, slots, ahead2=not last or q + 2 < XS,
                                       ahead1=not last or q + 1 < XS)
                if not last:
                    carry(slots)

            first_slots = [weights_at(b) for b in range(2)]
            gate_up(0, 0, first_slots[0])
            carry(first_slots)
            group(0)
            last_g = last_group(pe)
            groups(pe, last_g, group)
            group(last_g, last=True)

            def sum_tile(i, q, bank):
                pe.wait_ge(f_pair, i + 1)
                wait(pe, f_out, i - 2 * XS + 1)
                parts = [accl[:, q, a, :] for a in range(1, XS)] + [share[:, bass.ds(i, 1), :].rearrange("p i d -> p (i d)")]
                for a, part in enumerate(parts):
                    last = mm(ps[:, bank + q, 0:D], ident[:], part, start=(a == 0), stop=(a == XS - 1))
                last.then_inc(f_sum, 1)

            pe.wait_ge(b_y, last_g * XS + XS)
            for i in range(2 * XS):
                sum_tile(i, i % XS, i // XS * XS)
            with pe.Fori(1, NT // XS // 2) as g:
                for i in range(2 * XS):
                    sum_tile(g * (2 * XS) + i, i % XS, i // XS * XS)

        @block.vector
        def _(ve):
            v = nc.vector
            v.memset(reg_q[:, 0:NQ], 0.0).then_inc(vinit, 1)
            v.memset(reg_v[:], 0.0).then_inc(vinit, 1)
            ve.wait_ge(vinit, 2)
            v.memset(v_sb[0:S, :, :, 0, HD:HD + 1], 1.0).then_inc(vinit, 1)
            v.memset(v_sb[S:P, :, :, 1, HD:HD + 1], 1.0).then_inc(vinit, 1)
            ve.wait_ge(vinit, 4)
            con = Steps(ve, c_dve, 0, 20)
            ve.wait_ge(iotas, 3)
            con.then(v.tensor_copy(rel[:], rel_i[:]))
            con.then(v.tensor_scalar(rel[S:P, :], rel[S:P, :], float(-S), None, ALU.add))
            con.then(v.tensor_scalar(mask[:], rel[:], 0.0, None, ALU.is_le))
            ve.wait_ge(l_x, 48)
            con.then(v.tensor_tensor(bias[:], rel[:].unsqueeze(1).to_broadcast([P, H, S]),
                                     sl_sb[:].unsqueeze(2).to_broadcast([P, H, S]), ALU.mult))
            con.then(v.tensor_copy(ei[:], ei_i[:]))
            con.then(v.tensor_scalar(eo[:], ei[:], float(REGION), None, ALU.mult))
            con.then(v.tensor_copy(off[:], eo[:]))
            con.then(v.tensor_copy(bi[:], bi_i[:]))
            N_CON = con.n

            ve.wait_ge(l_wv, 32)
            for i in range(NT):
                ve.wait_ge(v_mm, i + 1)
                for b in range(2):
                    p = slice(b * S, (b + 1) * S)
                    v.tensor_tensor(v_sb[p, i, :, b, 0:HD], ps[p, 4 + i % GROUP, 0:D].rearrange("p (h e) -> p h e", h=H),
                                    bv_sb[p, :].rearrange("p (h e) -> p h e", h=H), ALU.add).then_inc(v_ev, 1)
            v.tensor_tensor(x_sb[:, :, 0:D], x_sb[:, :, 0:D],
                            bo_sb[:].unsqueeze(1).to_broadcast([P, NT, D]), ALU.add).then_inc(relc, 1)
            ve.wait_ge(relc, 1)

            def self_step(i, r):
                if there(i):
                    ve.wait_ge(exped, i + 1)
                    pv = prob[:, r, :].rearrange("p (h s) -> p h s", h=H)
                    v.tensor_tensor(pv, pv, mask[:].unsqueeze(1).to_broadcast([P, H, S]), ALU.mult).then_inc(masked, 1)
                if there(i, 1):
                    j, q = i + 1, 1 - r
                    ve.wait_ge(sc_mm, j + 1)
                    wait(ve, pv_mm, j - 1)
                    v.tensor_tensor(prob[:, q, :].rearrange("p (c n) -> p c n", c=KC), ps[:, 2 * q:2 * q + 2, :],
                                    bias[:].rearrange("p (c h) s -> p c (h s)", c=KC), ALU.add).then_inc(biased, 1)
                if there(i, -3):
                    j = i - 3
                    ve.wait_ge(ln_rs, j + 1)
                    v.tensor_scalar(x_sb[:, bass.ds(j, 1), 0:D].rearrange("p i d -> p (i d)"), res[:, 0, :],
                                    lmv[:, 0:1], lrs[:, 0:1], ALU.subtract, ALU.mult).then_inc(x1_done, 1)
                    ve.wait_ge(x1_done, j + 1)
                if there(i, -2):
                    j = i - 2
                    ve.wait_ge(o_mm, j + 1)
                    row = x_sb[:, bass.ds(j, 1), 0:D].rearrange("p i d -> p (i d)")
                    v.tensor_tensor(res[:, 0, :], ps[:, 7, 0:D], row, ALU.add).then_inc(o_res, 1)
                    ve.wait_ge(o_res, j + 1)
                    ve.sem_inc(waited, 1)
                    v.bn_stats(lstats[:], res[:, 0, :]).then_inc(ln_part, 1)
                    ve.wait_ge(ln_part, j + 1)
                    ve.sem_inc(waited, 1)
                    v.bn_aggr(lmv[:], lstats[:]).then_inc(ln_stat, 1)
                if there(i):
                    ve.wait_ge(pv_mm, i + 1)
                    wait(ve, ctx_t, i - 1)
                    cp = ps[:, 4 + r, 0:8 * 34].rearrange("p (j b e) -> p j b e", j=8, b=2)
                    v.reciprocal(crec[:, r, :, :], cp[:, :, :, HD:HD + 1].rearrange("p j b e -> p j (b e)")).then_inc(ctx_rec, 1)
                    ve.wait_ge(ctx_rec, i + 1)
                    v.tensor_tensor(ctxn[:, r, :].rearrange("p (b j e) -> p j b e", b=2, j=8), cp[:, :, :, 0:HD],
                                    crec[:, r, :, :].unsqueeze(3).to_broadcast([P, 8, 2, HD]), ALU.mult).then_inc(ctx_n, 1)

                if isinstance(i, int) and i == NT - 1:
                    for q in range(2):
                        ve.wait_ge(qd_in[q], 128 * (NT // 2))
                    v.memset(reg_qk[:, 0:XK], 0.0).then_inc(xz[1], 1)

            tiles(ve, self_step, 1, 3)

            def softmax_in(i, r, c):
                ve.wait_ge(xs_mm, i * KC + c + 1)
                if not (isinstance(i, int) and i < 2):
                    ve.wait_ge(xp_t, (i - 2) * KC + c + 1)
                wait(ve, xs_sub, i * KC + (c - 1))
                s = ps[:, 2 * c:2 * c + 2, :].rearrange("p a (h t) -> p (a h) t", t=S)
                v.tensor_reduce(xmax[:, c, :], s, AX, ALU.max).then_inc(xs_max, 1)
                ve.wait_ge(xs_max, i * KC + c + 1)
                v.tensor_tensor(xprob[:, r, c, :].rearrange("p (h t) -> p h t", t=S), s,
                                xmax[:, c, :].unsqueeze(2).to_broadcast([P, HC, S]), ALU.subtract).then_inc(xs_sub, 1)

            def cross_step(i, r):
                if there(i, 1):
                    softmax_in(i + 1, 1 - r, 0)
                if there(i, -1):
                    j = i - 1
                    ve.wait_ge(ln_rs, j + (NT + 1))
                    wait(ve, x2_t, j - 1)
                    wait(ve, x2r_out, j - 1)
                    v.tensor_scalar(x2r[:, 1 - r, :], res[:, 1, :], lmv[:, 0:1], lrs[:, 0:1],
                                    ALU.subtract, ALU.mult).then_inc(x2_done, 1)
                    ve.wait_ge(x2_done, j + 1)
                if there(i, -2):
                    j = i - 2
                    ve.wait_ge(rk_mm, j + 1)
                    ranks = Steps(ve, rb_steps, j, RB_N)
                    ranks.then(v.tensor_tensor(pos[:], rk_ps[:, 0:NE], off[:], ALU.add))
                    v.tensor_tensor(off[:], off[:], rk_ps[:, NE:2 * NE], ALU.add).then_inc(rk_free, 1)
                    ve.wait_ge(rk_free, j + 1)
                if there(i, 1):
                    softmax_in(i + 1, 1 - r, 1)
                if there(i, -2):
                    by_choice = ranks.start(v.tensor_tensor(hpos, hot[:, r, :, :], pos[:].unsqueeze(1).to_broadcast([P, TOPK, NE]),
                                                            ALU.mult))
                if there(i, -1):
                    j = i - 1
                    ve.wait_ge(lg_mm, j + 1)
                    wait(ve, lg_exp, j)
                    v.tensor_copy(logit[:], lg_ps).then_inc(lg_in, 1)
                if there(i, -2):
                    ranks.done(by_choice)
                    in_slotf = ranks.start(v.tensor_reduce(slotf[:], hpos, AX, ALU.add))
                if there(i, -1):
                    ve.wait_ge(lg_in, j + 1)
                    v.tensor_reduce(lmax[:], logit[:], AX, ALU.max).then_inc(lg_steps, 1)
                if there(i, -2):
                    ranks.done(in_slotf)
                    v.tensor_copy(slot[:, bass.ds((i - 2) * 8, TOPK)], slotf[:]).then_inc(slot_in, 1)
                if there(i, -1):
                    ve.wait_ge(lg_steps, j + 1)
                    v.tensor_scalar(lnmax[:], lmax[:], -1.0, None, ALU.mult).then_inc(lg_max, 1)

                if there(i, -1):
                    rt = Steps(ve, ra_steps, j, RA_N, waited)
                    choice = x_sb[:, bass.ds(j, 1), C_E:C_E + TOPK].rearrange("p i d -> p (i d)")
                    weight = x_sb[:, bass.ds(j, 1), C_W:C_W + TOPK].rearrange("p i d -> p (i d)")
                    ve.wait_ge(lg_exp, j + 1)
                    rt.then(v.reciprocal(prs[:], psum[:]))
                    rt.then(v.tensor_scalar(pr[:], pexp[:], prs[:, 0:1], None, ALU.mult), alone=True)
                    rt.then(v.max(top[:], pr[:]), alone=True)
                    numbers = rt.start(v.max_index(topi[:], top[:], pr[:]))
                    sums = rt.start(v.tensor_reduce(tsum[:], top[:, 0:TOPK], AX, ALU.add))
                if there(i):
                    ve.wait_ge(xv_mm, i * KC + KC)
                    xo = Steps(ve, xn_steps, i, XN_N, waited)
                    cx = ps[:, 6, 0:XH * (XD + 1)].rearrange("p (h e) -> p h e", h=XH)
                    shares = xo.start(v.reciprocal(xrec[:], cx[:, :, XD:XD + 1].rearrange("p h e -> p (h e)")))
                if there(i, -1):
                    rt.done(numbers)
                    chosen = rt.start(v.tensor_copy(choice, topi[:, 0:TOPK]))
                    rt.done(sums)
                    guarded = rt.start(v.tensor_scalar(tsum[:], tsum[:], TOP_EPS, None, ALU.add))
                if there(i):
                    xo.done(shares)
                    v.tensor_tensor(xtmp.rearrange("p (h e) -> p h e", h=XH), cx[:, :, 0:XD],
                                    xrec[:].unsqueeze(2).to_broadcast([P, XH, XD]), ALU.mult).then_inc(xc_free, 1)
                if there(i, -1):
                    rt.done(chosen)
                    v.tensor_tensor(hot[:, 1 - r, :, :], ei[:].unsqueeze(1).to_broadcast([P, TOPK, NE]),
                                    choice.unsqueeze(2).to_broadcast([P, TOPK, NE]), ALU.is_equal).then_inc(hot_in, 1)
                    rt.done(guarded)
                    inverse = rt.start(v.reciprocal(trec[:], tsum[:]))
                if there(i):
                    ve.wait_ge(xc_free, i + 1)
                    summed = xo.start(v.tensor_tensor(res[:, 1, :], xtmp, x_sb[:, bass.ds(i, 1), 0:D].rearrange("p i d -> p (i d)"),
                                                      ALU.add))
                if there(i, -1):
                    rt.done(inverse)
                    v.tensor_scalar(weight, top[:, 0:TOPK], trec[:, 0:1], None, ALU.mult).then_inc(row_in, 1)
                if there(i):
                    xo.done(summed, alone=True)
                    xo.then(v.bn_stats(lstats[:], res[:, 1, :]), alone=True)
                    v.bn_aggr(lmv[:], lstats[:]).then_inc(ln_stat, 1)
                if there(i, -1):
                    ve.wait_ge(row_in, j + 1)
                    ve.wait_ge(hot_in, j + 1)
                    v.tensor_reduce(sel[:, 1 - r, :], hot[:, 1 - r, :, :].rearrange("p k e -> p e k"), AX,
                                    ALU.add).then_inc(sel_in, 1)

            tiles(ve, cross_step, 2, 2)

            t = Steps(ve, c_dve, 0, 200)
            t.n = N_CON

            def table_counts():
                t.then(v.tensor_copy(offi, off[0:1, :]))
                ve.sem_inc(tb_off, 1)
                t.then(v.tensor_tensor(nblk, off[:], eo[:], ALU.subtract))
                t.then(v.tensor_scalar(nblk, nblk, float(P - 1), None, ALU.add))
                t.then(v.tensor_copy(nblki[:], nblk))
                t.then(v.tensor_scalar(nblki[:], nblki[:], P.bit_length() - 1, None, ALU.arith_shift_right))
                t.then(v.tensor_copy(nblk, nblki[:]))
                t.then(v.tensor_scalar(nblk, nblk, 1.0, None, ALU.max))
                t.then(v.tensor_copy(pre[0], nblk))

            def table_prefix():
                cur, d = 0, 1
                while d < NE:
                    t.then(v.tensor_copy(pre[1 - cur][:, 0:d], pre[cur][:, 0:d]))
                    t.then(v.tensor_tensor(pre[1 - cur][:, d:NE], pre[cur][:, d:NE], pre[cur][:, 0:NE - d], ALU.add))
                    cur, d = 1 - cur, 2 * d
                return cur

            def table_ends(end):
                t.then(v.tensor_copy(endi, end[0:1, :]))
                t.then(v.tensor_scalar(lastf[:], end[0:1, NE - 1:NE], float(XS - 1), None, ALU.add))
                t.then(v.tensor_copy(lastg[:], lastf[:]))
                t.then(v.tensor_scalar(lastg[:], lastg[:], XS.bit_length() - 1, None, ALU.arith_shift_right))
                t.then(v.tensor_scalar(lastg[:], lastg[:], -1.0, None, ALU.add))
                t.then(v.tensor_tensor(start, end, nblk, ALU.subtract))
                t.then(v.scalar_tensor_tensor(rowof, start, float(-P), eo[:], ALU.mult, ALU.add))

            def table_column(end, c):
                bcol = bi[:, c:c + 1]
                t.then(v.tensor_scalar(ge_end, end, bcol, None, ALU.is_le))
                t.then(v.tensor_scalar(ge_start, start, bcol, None, ALU.is_le))
                t.then(v.tensor_tensor(inb, ge_start, ge_end, ALU.subtract))
                t.then(v.tensor_reduce(cols[:, c:c + 1], ge_end, AX, ALU.add))
                t.then(v.tensor_scalar(cols[:, c:c + 1], cols[:, c:c + 1], float(NE - 1), None, ALU.min))
                t.then(v.tensor_copy(wsi[:, c:c + 1], cols[:, c:c + 1]))
                t.then(v.tensor_scalar(wsi[:, c:c + 1], wsi[:, c:c + 1], WS - 1, None, ALU.bitwise_and))
                t.then(v.tensor_copy(cols[:, 4 + c:5 + c], wsi[:, c:c + 1]))
                t.then(v.tensor_scalar(cols[:, 6 + c:7 + c], cols[:, c:c + 1], 1.0, None, ALU.add))
                t.then(v.tensor_reduce(ns[:, c:c + 1], inb, AX, ALU.add))
                t.then(v.tensor_tensor(inb, inb, rowof, ALU.mult))
                t.then(v.tensor_reduce(cols[:, 2 + c:3 + c], inb, AX, ALU.add))
                t.then(v.tensor_scalar(w6[:, c:c + 1], bcol, float(P), float(-PAD_ROW), ALU.mult, ALU.add))
                t.then(v.scalar_tensor_tensor(cols[:, 2 + c:3 + c], w6[:, c:c + 1], ns[:, c:c + 1],
                                              cols[:, 2 + c:3 + c], ALU.mult, ALU.add))
                t.then(v.tensor_scalar(cols[:, 2 + c:3 + c], cols[:, 2 + c:3 + c], float(PAD_ROW), None, ALU.add))

            def table_out():
                ve.sem_inc(tb_cols, 1)
                ve.wait_ge(tb_t, 1)
                v.tensor_copy(tcol, ps[0:8, 4, 0:P]).then_inc(tb_row, 1)
                v.tensor_copy(tcoli, ps[0:8, 4, 0:P]).then_inc(tb_row, 1)


            ve.wait_ge(x2r_out, NT)

            def shared_product(n, f):
                m, r = SFC[f][1], n % 2
                wait(ve, sd_mm, (n - 1) * GROUP)
                ve.wait_ge(sg_act, n * 3 + (f + 1))
                v.tensor_tensor(shid[0:m, r, f, :], sgate[0:m, f, :], ps[0:m, SBANK[f] + 1, :], ALU.mult).then_inc(sh_in, 1)

            def shared_rows(n, j):
                ve.wait_ge(sd_mm, n * GROUP + (j + 1))
                v.tensor_tensor(share[:, bass.ds(n * GROUP + j, 1), :].rearrange("p i d -> p (i d)"),
                                ps[:, 4 + j % 2, 0:D],
                                x_sb[:, bass.ds(n * GROUP + j, 1), 0:D].rearrange("p i d -> p (i d)"),
                                ALU.add).then_inc(sd_ev, 1)

            def shared_step(n, more=True):
                if more:
                    shared_product(n + 1, 0)
                for j in range(GROUP):
                    shared_rows(n, j)
                if more:
                    for f in range(1, 3):
                        shared_product(n + 1, f)

            table_counts()
            shared_product(0, 0)
            end = pre[table_prefix()]
            shared_product(0, 1)
            table_ends(end)
            shared_product(0, 2)
            table_column(end, 0)
            shared_step(0)
            table_column(end, 1)
            shared_step(1)
            table_out()
            shared_step(2)
            shared_step(3, more=False)

            ve.wait_ge(tb_in, 32)

            def copy_rows(b, r):
                ready = ve.value_load(tab[0:1, bass.ds(b + 6 * P, 1)], min_val=1, max_val=NE)
                ve.wait_ge(w_ready, ready)
                ve.wait_ge(b_t1, b + 1)
                v.tensor_copy(xgT[:, r, :], ps[:, r, 0:D]).then_inc(b_xgT, 1)

            def multiply(b, r):
                ve.wait_ge(b_silu, b + 1)
                if not isinstance(b, int) or b >= 2:
                    ve.wait_ge(b_t2, b - 1)
                v.tensor_tensor(act[:, r, :], gate[:, r, :], ps[:, 2 + r, F:2 * F], ALU.mult).then_inc(b_act, 1)

            def block_step(b, r, q, n, ahead2=True, ahead1=True):
                if ahead2:
                    copy_rows(b + 2, r)
                ve.wait_ge(xg_in[q], n * 16 + 16)
                wait(ve, added[q], n * 16)
                v.tensor_scalar(toks[:, q:q + 1], xg[:, q, C_TOK:C_TOK + 1].bitcast(I32), float(q * (T + P)), None,
                                ALU.add).then_inc(b_meta, 1)
                v.scalar_tensor_tensor(w6[:], xg[:, q, C_E:C_E + TOPK], ebc[:, bass.ds(b, 1)],
                                       xg[:, q, C_W:C_W + TOPK], ALU.is_equal, ALU.mult).then_inc(b_meta, 1)
                ve.wait_ge(b_meta, b * 3 + 2)
                v.tensor_reduce(wcol[:, r:r + 1], w6[:], AX, ALU.add).then_inc(b_meta, 1)
                if ahead1:
                    multiply(b + 1, 1 - r)
                ve.wait_ge(b_meta, b * 3 + 3)
                ve.wait_ge(b_dn, b + 2)
                v.tensor_scalar(y_sb[:, q, :], ps[:, 6 + r, 0:D], wcol[:, r:r + 1], None, ALU.mult).then_inc(b_y, 1)

            copy_rows(0, 0)
            copy_rows(1, 1)
            multiply(0, 0)

            def group(n, last=False):
                for q in range(XS):
                    block_step(n * XS + q, q % 2, q, n, ahead2=not last or q + 2 < XS, ahead1=not last or q + 1 < XS)

            group(0)
            last = last_group(ve)
            groups(ve, last, group)
            group(last, last=True)

            def add_pair(i, q):
                ve.wait_ge(ac_in[q], (i - q) * (16 // XS) + 16)
                v.tensor_tensor(accl[:, q, 1, :], accl[:, q, 0, :], accl[:, q, 1, :], ALU.add).then_inc(f_pair, 1)

            def finish(g, q, bank, more=True):
                i = g * XS + q
                if more:
                    add_pair(i + 2, (q + 2) % XS)
                ve.wait_ge(f_sum, i + 1)
                ve.sem_inc(waited, 1)
                v.bn_stats(lstats[:], ps[:, bank + q, 0:D]).then_inc(f_steps, 1)
                ve.wait_ge(f_steps, i + 1)
                ve.sem_inc(waited, 1)
                v.bn_aggr(fmv[:, q, :], lstats[:]).then_inc(f_aggr, 1)
                ve.wait_ge(f_aggr, i + 1)

            def finish_group(g, h, last=False):
                for q in range(XS):
                    finish(g, q, h * XS, more=not last or q + 2 < XS)
                st = Steps(ve, f_newton, g, 3 + 3 * NEWTON)
                mean, var = fmv[:, :, 0:1], fmv[:, :, 1:2]
                st.then(v.tensor_scalar(fvar[:].unsqueeze(2), var, LN_EPS, None, ALU.add))
                st.then(v.tensor_scalar(ftmpi[:], fvar[:].bitcast(I32), 1, None, ALU.arith_shift_right))
                st.then(v.tensor_scalar(frsl[:].bitcast(I32), ftmpi[:], -1.0, float(0x5F3759DF), ALU.mult, ALU.add))
                for _ in range(NEWTON):
                    st.then(v.tensor_tensor(ftmp[:], frsl[:], frsl[:], ALU.mult))
                    st.then(v.scalar_tensor_tensor(ftmp[:], ftmp[:], -0.5, fvar[:], ALU.mult, ALU.mult))
                    st.then(v.scalar_tensor_tensor(frsl[:], ftmp[:], 1.5, frsl[:], ALU.add, ALU.mult))
                v.tensor_copy(frs[:, bass.ds(g * XS, XS)], frsl[:]).then_inc(f_stat, 1)
                v.scalar_tensor_tensor(fnm[:, bass.ds(g * XS, XS)].unsqueeze(2), mean, -1.0, frsl[:].unsqueeze(2),
                                       ALU.mult, ALU.mult).then_inc(f_stat, 1)
                ve.wait_ge(f_stat, g * 2 + 2)

            for i in range(2):
                add_pair(i, i)
            with ve.Fori(0, NT // XS // 2 - 1) as g2:
                for h in range(2):
                    finish_group(g2 * 2 + h, h)
            for h in range(2):
                finish_group(NT // XS - 2 + h, h, last=h == 1)


_INS = ["x", "xT", "ctxT", "ctx", "wqT", "wkT", "wvT", "woT", "bq", "bk", "bv", "bo", "slopes", "gwT", "wgu", "wdn",
        "wsgu", "wsda", "wsdb"]


def kernel(x, ctx_512, L0_attn_Wq, L0_attn_bq, L0_attn_Wk, L0_attn_bk, L0_attn_Wv, L0_attn_bv, L0_attn_Wo, L0_attn_bo,
           L0_attn_alibi_slopes, L0_ffn_gate_w, L0_ffn_w_gate_up, L0_ffn_w_down, L0_ffn_ws_gate_up, L0_ffn_ws_down):
    import numpy as np
    from concourse import bacc
    from concourse.bass_utils import run_bass_kernel_spmd

    tok = np.asarray(x).reshape(T, D)
    c = np.asarray(ctx_512)
    chunks = lambda w: np.asarray(w).T.reshape(KC, P, -1).transpose(1, 0, 2)
    sdown = np.asarray(L0_ffn_ws_down).T
    laid = {
        "x": tok.reshape(NT, P, D).transpose(1, 0, 2),
        "xT": chunks(tok),
        "ctxT": c.reshape(T, -1).T,
        "ctx": c.transpose(1, 0, 2).reshape(S, -1),
        "wqT": chunks(L0_attn_Wq), "wkT": chunks(L0_attn_Wk), "wvT": chunks(L0_attn_Wv),
        "woT": np.asarray(L0_attn_Wo).T.reshape(H // 2, 2, HD, D).transpose(0, 2, 1, 3).reshape(P, 2, D),
        "bq": np.asarray(L0_attn_bq).reshape(KC, P).T, "bk": np.asarray(L0_attn_bk).reshape(KC, P).T,
        "bv": np.asarray(L0_attn_bv).reshape(1, D), "bo": np.asarray(L0_attn_bo).reshape(1, D),
        "slopes": np.asarray(L0_attn_alibi_slopes).reshape(1, H),
        "gwT": chunks(L0_ffn_gate_w),
        "wgu": np.asarray(L0_ffn_w_gate_up).transpose(0, 2, 1).reshape(NE, KC, P, 2 * F).transpose(0, 2, 1, 3).reshape(NE, P, WGU),
        "wdn": np.asarray(L0_ffn_w_down).transpose(0, 2, 1).reshape(NE, 2, FH, D).transpose(0, 2, 1, 3).reshape(NE, FH, WDN),
        "wsgu": chunks(L0_ffn_ws_gate_up),
        "wsda": sdown[0:2 * P].reshape(2, P, D).transpose(1, 0, 2),
        "wsdb": sdown[2 * P:],
    }
    nc = bacc.Bacc("TRN2", target_bir_lowering=False, num_devices=1)
    arrays, args = {}, []
    for name in _INS:
        a = np.ascontiguousarray(laid[name])
        arrays[f"in_{name}"] = a
        args.append(nc.dram_tensor(f"in_{name}", a.shape, mybir.dt.from_np(a.dtype), kind="ExternalInput").ap())
    args.append(nc.dram_tensor("out_dram", (P, NT, D), F32, kind="ExternalOutput").ap())
    decoder(nc, *args)
    r = run_bass_kernel_spmd(nc, [arrays], core_ids=[0])
    return np.ascontiguousarray(r.results[0]["out_dram"].transpose(1, 0, 2)).reshape(B, S, D)
```
